# Optimizing a Trainium2 kernel written in Bass

```python
import numpy as np
import jax
import jax.numpy as jnp

def _softmax(x, axis=-1):
    return jax.nn.softmax(x, axis=axis)

def _gelu(x):
    return jax.nn.gelu(x, approximate=True)

def _silu(x):
    return jax.nn.silu(x)

def _sigmoid(x):
    return jax.nn.sigmoid(x)

def _layernorm(x, axis=-1, eps=1e-05):
    m = jnp.mean(x, axis=axis, keepdims=True)
    v = jnp.var(x, axis=axis, keepdims=True)
    return (x - m) / jnp.sqrt(v + eps)

def _scatter_add(tgt, idx, src, axis=0):
    return tgt.at[idx].add(src)

def _segment_sum(src, seg, n):
    return jax.ops.segment_sum(src, seg, n)
kernel_name = 'mk_gnn_resnorm_d4_gnn_r64_ffcfda'

def setup_inputs(seed: int=0):
    np.random.seed(seed)
    _w = jnp.asarray

    def _rec_inputs():
        import jax
        import jax.numpy as jnp
        _gk = jax.random.key(seed)
        x = -0.0003713 + 1 * jax.random.normal(jax.random.fold_in(_gk, 1), (100000, 128), jnp.float32)
        src = jax.random.randint(jax.random.fold_in(_gk, 2), (50000,), 0, 100000, jnp.int32)
        dst = jax.random.randint(jax.random.fold_in(_gk, 3), (50000,), 0, 100000, jnp.int32)
        _o = jnp.argsort(dst, stable=True)
        src = src[_o]
        dst = dst[_o]
        edge_weight = jax.random.uniform(jax.random.fold_in(_gk, 13), (50000,), jnp.float32, 0.0, 0.999996)
        return (x, src, dst, edge_weight)
    x, src, dst, edge_weight = _rec_inputs()

    def _L0_gnn_setup():
        import jax, jax.numpy as jnp
        import numpy as np
        N_NODES = 100000
        N_EDGES = 25000
        D_IN = 128
        D_OUT = 128

        def _gcn_aggregate(feats, src, dst, n_nodes):
            ones = jnp.ones(src.shape[0], dtype=feats.dtype)
            deg_out = jax.ops.segment_sum(ones, src, num_segments=n_nodes)
            deg_in = jax.ops.segment_sum(ones, dst, num_segments=n_nodes)
            norm_out = jax.lax.rsqrt(jnp.maximum(deg_out, 1.0))
            norm_in = jax.lax.rsqrt(jnp.maximum(deg_in, 1.0))
            msg = (feats * norm_out[:, None])[src]
            agg = jax.ops.segment_sum(msg, dst, num_segments=n_nodes)
            return agg * norm_in[:, None]
        key = jax.random.key(seed)
        k1, k2, k3, k4 = jax.random.split(key, 4)
        feats = jax.random.normal(k1, (N_NODES, D_IN), dtype=jnp.float32)
        limit = float(np.sqrt(6.0 / (D_IN + D_OUT)))
        weight = jax.random.uniform(k2, (D_IN, D_OUT), dtype=jnp.float32, minval=-limit, maxval=limit)
        bias = jnp.zeros((D_OUT,), dtype=jnp.float32)
        src = jax.random.randint(k3, (N_EDGES,), 0, N_NODES, dtype=jnp.int64 if jax.config.read('jax_enable_x64') else jnp.int32)
        dst = jax.random.randint(k4, (N_EDGES,), 0, N_NODES, dtype=jnp.int64 if jax.config.read('jax_enable_x64') else jnp.int32)
        return {'feats': feats, 'weight': weight, 'bias': bias, 'src': src, 'dst': dst}
    _L0_gnn_all = _L0_gnn_setup()
    _L0_gnn_in = {k: v for k, v in _L0_gnn_all.items() if k in ('weight', 'bias')}
    del _L0_gnn_all

    def _L1_gnn_setup():
        import jax, jax.numpy as jnp
        import numpy as np
        N_NODES = 50000
        N_EDGES = 6250
        F_IN = 128
        UNITS = 128
        N_REL = 8
        key = jax.random.key(seed)
        k_x, k_r, k_c, k_v, k_w = jax.random.split(key, 5)
        x = jax.random.normal(k_x, (N_NODES, F_IN), dtype=jnp.float32)
        edge_row = jax.random.randint(k_r, (N_EDGES,), 0, N_NODES)
        edge_col = jax.random.randint(k_c, (N_EDGES,), 0, N_NODES)
        edge_vals = jax.random.uniform(k_v, (N_EDGES,), dtype=jnp.float32)
        W = jax.random.normal(k_w, (N_REL, F_IN, UNITS), dtype=jnp.float32) * 0.05
        b = jnp.zeros((N_REL, UNITS), dtype=jnp.float32)
        return {'x': x, 'edge_row': edge_row, 'edge_col': edge_col, 'edge_vals': edge_vals, 'W': W, 'b': b}
    _L1_gnn_all = _L1_gnn_setup()
    _L1_gnn_in = {k: v for k, v in _L1_gnn_all.items() if k in ('W', 'b')}
    del _L1_gnn_all

    def _L2_gnn_setup():
        import jax, jax.numpy as jnp
        import numpy as np
        EPS = 1e-09
        LN_EPS = 1e-05

        def _proj_normalize(v):
            return v / (jnp.linalg.norm(v, axis=-1, keepdims=True) + EPS)
        N, E, Fin, Fout = (50000, 9375, 128, 128)
        key = jax.random.key(seed)
        ks = jax.random.split(key, 8)
        x = jax.random.normal(ks[0], (N, Fin), jnp.float32)
        edge_index = jax.random.randint(ks[1], (2, E), 0, N, dtype=jnp.int64)
        edge_weight = jax.random.normal(ks[2], (E,), jnp.float32)
        W_self = jax.random.normal(ks[3], (Fin, Fout), jnp.float32) / np.sqrt(Fin)
        b_self = jnp.zeros((Fout,), jnp.float32)
        W_nb = jax.random.normal(ks[4], (Fin, Fout), jnp.float32) / np.sqrt(Fin)
        b_nb = jnp.zeros((Fout,), jnp.float32)
        gamma = jnp.ones((Fout,), jnp.float32)
        beta = jnp.zeros((Fout,), jnp.float32)
        return dict(x=x, edge_index=edge_index, edge_weight=edge_weight, W_self=W_self, b_self=b_self, W_nb=W_nb, b_nb=b_nb, gamma=gamma, beta=beta)
    _L2_gnn_all = _L2_gnn_setup()
    _L2_gnn_in = {k: v for k, v in _L2_gnn_all.items() if k in ('W_self', 'b_self', 'W_nb', 'b_nb', 'gamma', 'beta')}
    del _L2_gnn_all

    def _L3_gnn_setup():
        import jax, jax.numpy as jnp
        import numpy as np
        N_NODES = 100000
        N_EDGES = 10000
        D_IN = 128
        D_OUT = 128
        key = jax.random.key(seed)
        k1, k2, k3, k4, k5 = jax.random.split(key, 5)
        feat = jax.random.normal(k1, (N_NODES, D_IN), dtype=jnp.float32)
        src = jax.random.randint(k2, (N_EDGES,), 0, N_NODES, dtype=jnp.int32)
        dst = jax.random.randint(k3, (N_EDGES,), 0, N_NODES, dtype=jnp.int32)
        scale = 1.0 / np.sqrt(D_IN)
        W_self = jax.random.normal(k4, (D_IN, D_OUT), dtype=jnp.float32) * scale
        W_neigh = jax.random.normal(k5, (D_IN, D_OUT), dtype=jnp.float32) * scale
        b_self = jnp.zeros((D_OUT,), dtype=jnp.float32)
        b_neigh = jnp.zeros((D_OUT,), dtype=jnp.float32)
        return {'feat': feat, 'src': src, 'dst': dst, 'W_self': W_self, 'b_self': b_self, 'W_neigh': W_neigh, 'b_neigh': b_neigh}
    _L3_gnn_all = _L3_gnn_setup()
    _L3_gnn_in = {k: v for k, v in _L3_gnn_all.items() if k in ('W_self', 'b_self', 'W_neigh', 'b_neigh')}
    del _L3_gnn_all
    return {'x': x, 'src': src, 'dst': dst, 'edge_weight': edge_weight, 'L0_gnn_weight': _L0_gnn_in['weight'], 'L0_gnn_bias': _L0_gnn_in['bias'], 'L1_gnn_W': _L1_gnn_in['W'], 'L1_gnn_b': _L1_gnn_in['b'], 'L2_gnn_W_self': _L2_gnn_in['W_self'], 'L2_gnn_b_self': _L2_gnn_in['b_self'], 'L2_gnn_W_nb': _L2_gnn_in['W_nb'], 'L2_gnn_b_nb': _L2_gnn_in['b_nb'], 'L2_gnn_gamma': _L2_gnn_in['gamma'], 'L2_gnn_beta': _L2_gnn_in['beta'], 'L3_gnn_W_self': _L3_gnn_in['W_self'], 'L3_gnn_b_self': _L3_gnn_in['b_self'], 'L3_gnn_W_neigh': _L3_gnn_in['W_neigh'], 'L3_gnn_b_neigh': _L3_gnn_in['b_neigh']}

def reference(x, src, dst, edge_weight, L0_gnn_weight, L0_gnn_bias, L1_gnn_W, L1_gnn_b, L2_gnn_W_self, L2_gnn_b_self, L2_gnn_W_nb, L2_gnn_b_nb, L2_gnn_gamma, L2_gnn_beta, L3_gnn_W_self, L3_gnn_b_self, L3_gnn_W_neigh, L3_gnn_b_neigh):
    import jax
    import jax.numpy as jnp

    def _L0_gnn_ref(feats, weight, bias, src, dst):
        import jax, jax.numpy as jnp
        import numpy as np
        N_NODES = 100000
        N_EDGES = 25000
        D_IN = 128
        D_OUT = 128

        def _gcn_aggregate(feats, src, dst, n_nodes):
            ones = jnp.ones(src.shape[0], dtype=feats.dtype)
            deg_out = jax.ops.segment_sum(ones, src, num_segments=n_nodes)
            deg_in = jax.ops.segment_sum(ones, dst, num_segments=n_nodes)
            norm_out = jax.lax.rsqrt(jnp.maximum(deg_out, 1.0))
            norm_in = jax.lax.rsqrt(jnp.maximum(deg_in, 1.0))
            msg = (feats * norm_out[:, None])[src]
            agg = jax.ops.segment_sum(msg, dst, num_segments=n_nodes)
            return agg * norm_in[:, None]
        rst = _gcn_aggregate(feats, src, dst, feats.shape[0])
        rst = jnp.matmul(rst, weight) + bias
        return jax.nn.relu(rst)

    def _L1_gnn_ref(x, edge_row, edge_col, edge_vals, W, b):
        import jax, jax.numpy as jnp
        import numpy as np
        N_NODES = 50000
        N_EDGES = 6250
        F_IN = 128
        UNITS = 128
        N_REL = 8
        n = x.shape[0]
        out = jnp.zeros((n, W.shape[2]), dtype=x.dtype)
        for r in range(W.shape[0]):
            h = x @ W[r] + b[r]
            msg = edge_vals[:, None] * h[edge_col]
            out = out + jax.ops.segment_sum(msg, edge_row, num_segments=n)
        return jax.nn.relu(out)

    def _L2_gnn_ref(x, edge_index, edge_weight, W_self, b_self, W_nb, b_nb, gamma, beta):
        import jax, jax.numpy as jnp
        import numpy as np
        EPS = 1e-09
        LN_EPS = 1e-05

        def _proj_normalize(v):
            return v / (jnp.linalg.norm(v, axis=-1, keepdims=True) + EPS)
        N = x.shape[0]
        src, tgt = (edge_index[0], edge_index[1])
        seg_max = jax.ops.segment_max(edge_weight, tgt, num_segments=N)
        ew = jnp.exp(edge_weight - seg_max[tgt])
        denom = jax.ops.segment_sum(ew, tgt, num_segments=N)
        alpha = ew / denom[tgt]
        agg = jax.ops.segment_sum(alpha[:, None] * x[src], tgt, num_segments=N)
        agg = _proj_normalize(agg)
        self_feat = x @ W_self + b_self
        nb_feat = agg @ W_nb + b_nb
        comb = _proj_normalize(0.5 * (self_feat + nb_feat))
        mu = jnp.mean(comb, axis=-1, keepdims=True)
        var = jnp.var(comb, axis=-1, keepdims=True)
        out = (comb - mu) / jnp.sqrt(var + LN_EPS) * gamma + beta
        return out

    def _L3_gnn_ref(feat, src, dst, W_self, b_self, W_neigh, b_neigh):
        import jax, jax.numpy as jnp
        import numpy as np
        N_NODES = 100000
        N_EDGES = 10000
        D_IN = 128
        D_OUT = 128
        n = feat.shape[0]
        msg = feat[src]
        neigh_sum = jax.ops.segment_sum(msg, dst, num_segments=n)
        deg = jax.ops.segment_sum(jnp.ones_like(dst, dtype=feat.dtype), dst, num_segments=n)
        h_neigh = neigh_sum / jnp.maximum(deg, 1.0)[:, None]
        rst = feat @ W_self + b_self + h_neigh @ W_neigh + b_neigh
        return rst
    edge_index = jnp.stack([src, dst])
    x = _layernorm(x + _L0_gnn_ref(x, L0_gnn_weight, L0_gnn_bias, src, dst), axis=-1)
    x = _layernorm(x + _L1_gnn_ref(x, src, dst, edge_weight, L1_gnn_W, L1_gnn_b), axis=-1)
    x = _layernorm(x + _L2_gnn_ref(x, edge_index, edge_weight, L2_gnn_W_self, L2_gnn_b_self, L2_gnn_W_nb, L2_gnn_b_nb, L2_gnn_gamma, L2_gnn_beta), axis=-1)
    x = _layernorm(x + _L3_gnn_ref(x, src, dst, L3_gnn_W_self, L3_gnn_b_self, L3_gnn_W_neigh, L3_gnn_b_neigh), axis=-1)
    return x

_drawn_inputs = setup_inputs


def setup_inputs(seed=0):
    import zlib

    import numpy as np

    out = dict(_drawn_inputs(seed))
    spreads = {'L0_gnn_bias': (0.0, 0.1),
     'L1_gnn_b': (0.0, 0.1),
     'L2_gnn_b_self': (0.0, 0.1),
     'L2_gnn_b_nb': (0.0, 0.1),
     'L2_gnn_gamma': (1.0, 0.2),
     'L2_gnn_beta': (0.0, 0.1),
     'L3_gnn_b_self': (0.0, 0.1),
     'L3_gnn_b_neigh': (0.0, 0.1)}
    factors = {}
    for name, (base, spread) in spreads.items():
        noise = np.random.default_rng([zlib.crc32(name.encode()), seed]).standard_normal(out[name].shape)
        drawn = base * np.exp(spread * noise) if base else spread * noise
        out[name] = jnp.asarray(drawn.astype(out[name].dtype))
    for name, factor in factors.items():
        out[name] = (out[name] * factor).astype(out[name].dtype)
    return out
```

```python
from contextlib import ExitStack, contextmanager

import concourse.bass as bass
from concourse import mybir

F32 = mybir.dt.float32
I32 = mybir.dt.int32
BF16 = mybir.dt.bfloat16
F16 = mybir.dt.float16
ALU = mybir.AluOpType
ACT = mybir.ActivationFunctionType
AX = mybir.AxisListType

P = 128
D = 128
GROUP = 256
BLOCK = 512
PER = BLOCK // P
RING = 8
SLOTS = 4
BIG = 1.0e30
HALF_SCALE = 2048.0
LN_EPS = 1e-5
NORM_EPS = 1e-9
N_REL = 8


class Dims:

    def __init__(self, n_nodes, n_edges):
        self.N, self.E = n_nodes, n_edges
        self.NB = -(-(n_nodes + GROUP) // (BLOCK * SLOTS)) * SLOTS
        self.NP = self.NB * BLOCK
        self.NG = self.NP // GROUP
        self.NC = -(-n_edges // (P * RING)) * RING
        self.EP = self.NC * P
        self.KEY_PAD = self.NP - GROUP
        self.RB = self.NC // 4
        self.SP = 125
        self.SW = n_edges // self.SP
        self.TILES = self.NP // P
        self.KH = -(-self.TILES // P)
        self.TH = self.TILES // self.KH
        assert self.KEY_PAD >= n_nodes and self.SP * self.SW == n_edges and self.TH * self.KH == self.TILES
        assert self.NC <= 512 and self.NG <= 512 and self.RB <= P and n_nodes % PER == 0


class Memory:

    def __init__(self, nc, ctx, d):
        def sb(name, shape, dt):
            return ctx.enter_context(nc.sbuf_tensor(name, shape, dt))

        self.bank = [ctx.enter_context(nc.psum_tensor(f"bank{i}", [P, 512], F32)) for i in range(8)]
        self.iota_free = sb("iota_free", [P, 512], F32)
        self.iota_half = sb("iota_half", [P, 1024], F16)
        self.iota_part = sb("iota_part", [P, 1], F32)
        self.group_base = sb("group_base", [P, d.NG], F32)
        self.ident = sb("ident", [P, P], F32)
        self.before = sb("before", [P, P], F16)
        self.ones_half = sb("ones_half", [P, P], F16)
        self.ones = sb("ones", [P, P], BF16)
        self.zeros = sb("zeros", [1, BLOCK], BF16)
        self.ones_col = sb("ones_col", [P, 1], F32)
        self.eps_col = sb("eps_col", [P, 1], F32)
        self.key_src = sb("key_src", [P, d.NC], F32)
        self.key_dst = sb("key_dst", [P, d.NC], F32)
        self.ev = sb("ev", [P, d.NC], F32)
        self.row_src = sb("row_src", [P, d.NC], I32)
        self.row_dst = sb("row_dst", [P, d.NC], I32)
        self.w_in = sb("w_in", [P, d.NC], F32)
        self.w_alpha = sb("w_alpha", [P, d.NC], F32)
        self.w_mean = sb("w_mean", [P, d.NC], F32)
        self.w_gcn = sb("w_gcn", [P, d.NC], F32)
        self.records = sb("records", [P, d.NC, 4], F32)
        self.s_key = sb("s_key", [P, d.NC], F32)
        self.s_row = sb("s_row", [P, d.NC], I32)
        self.s_ev = sb("s_ev", [P, d.NC], F32)
        self.s_ev_parts = sb("s_ev_parts", [P, d.NC, 3], BF16)
        self.end_dst = sb("end_dst", [1, d.NG], I32)
        self.end_src = sb("end_src", [1, d.NG], I32)
        self.w0 = sb("w0", [P, D], F32)
        self.w1 = sb("w1", [P, D], F32)
        self.w2s = sb("w2s", [P, D], F32)
        self.w2n = sb("w2n", [P, D], F32)
        self.w3s = sb("w3s", [P, D], F32)
        self.w3n = sb("w3n", [P, D], F32)
        self.b0 = sb("b0", [3, PER * D], BF16)
        self.b1 = sb("b1", [3, D], F32)
        self.b2 = sb("b2", [3, PER * D], BF16)
        self.b3 = sb("b3", [3, PER * D], BF16)
        self.gamma = sb("gamma", [P, PER, D], F32)
        self.beta = sb("beta", [P, PER, D], F32)


@contextmanager
def semaphores(nc):
    taken = []

    def take(name):
        taken.append(nc.alloc_semaphore(name))
        return taken[-1]

    yield take
    nc.clear_and_free_semaphores(taken)
    nc.all_engine_barrier()


def chain(engine, semaphore):
    count = [0]

    def link(instruction):
        count[0] += 1
        instruction.then_inc(semaphore, 1)
        engine.wait_ge(semaphore, count[0])

    return link


def rows_pieces(d):
    full, rest = divmod(d.E, P)
    out = []
    for k in range(4):
        n = min(max(full - k * d.RB, 0), d.RB)
        if n:
            out.append((k, 0, n, k * d.RB * P, P))
    if rest:
        out.append((full // d.RB, full % d.RB, 1, full * P, rest))
    return out


def phase_constants(nc, d, m):
    with ExitStack() as ctx:
        take = ctx.enter_context(semaphores(nc))

        iota_i = ctx.enter_context(nc.sbuf_tensor("iota_i", [P, 1024], I32))
        part_i = ctx.enter_context(nc.sbuf_tensor("part_i", [P, 1], I32))
        iotas = take("iotas")
        done = take("constants_done")
        block = ctx.enter_context(nc.Block())

        @block.gpsimd
        def _(pool):
            nc.gpsimd.iota(iota_i[:], pattern=[[1, 1024]], base=0, channel_multiplier=0).then_inc(iotas, 1)
            nc.gpsimd.iota(part_i[:], pattern=[[0, 1]], base=0, channel_multiplier=1).then_inc(iotas, 1)

        @block.vector
        def _(dve):
            link = chain(dve, done)
            dve.wait_ge(iotas, 2)
            nc.vector.tensor_copy(m.iota_half[:], iota_i[:])
            nc.vector.tensor_copy(m.iota_part[:], part_i[:])
            nc.vector.memset(m.ones[:], 1.0)
            nc.vector.memset(m.ones_col[:], 1.0)
            nc.vector.memset(m.ones_half[:], 1.0)
            nc.vector.memset(m.zeros[:], 0.0)
            nc.vector.memset(m.eps_col[:], LN_EPS)
            link(nc.vector.tensor_copy(m.iota_free[:], iota_i[:, 0:512]))
            nc.vector.tensor_scalar(m.group_base[:], m.iota_free[:, 0:d.NG], float(GROUP), None, ALU.mult)
            nc.vector.tensor_scalar(m.ident[:], m.iota_free[:, 0:P], m.iota_part[:], None, ALU.is_equal)
            nc.vector.tensor_scalar(m.before[:], m.iota_free[:, 0:P], m.iota_part[:], None, ALU.is_gt)


def phase_weights(nc, d, m, a):
    with ExitStack() as ctx:
        take = ctx.enter_context(semaphores(nc))

        def sb(name, shape, dt):
            return ctx.enter_context(nc.sbuf_tensor(name, shape, dt))

        rel = sb("rel", [P, N_REL, D], F32)
        rel_b = sb("rel_b", [3, N_REL, D], F32)
        bias = sb("bias", [3, 5, D], F32)
        hi = sb("hi", [3, D], BF16)
        mid = sb("mid", [3, D], BF16)
        lo = sb("lo", [3, D], BF16)
        rest = sb("rest", [3, D], F32)
        pick = sb("pick", [3, 3], F32)
        one = sb("one", [3, D], F32)
        loaded = take("weights_loaded")
        step = take("weights_step")
        block = ctx.enter_context(nc.Block())
        singles = [(m.w0, a["L0_gnn_weight"]), (m.w2s, a["L2_gnn_W_self"]), (m.w2n, a["L2_gnn_W_nb"]),
                   (m.w3s, a["L3_gnn_W_self"]), (m.w3n, a["L3_gnn_W_neigh"])]
        biases = ["L0_gnn_bias", "L2_gnn_b_self", "L2_gnn_b_nb", "L3_gnn_b_self", "L3_gnn_b_neigh"]

        n_loads = len(singles) + 1 + 3 + 3 * len(biases) + 2

        @block.sync
        def _(sp):
            for tile, source in singles:
                sp.dma_start(tile[:], source).then_inc(loaded, 16)
            sp.dma_start(rel[:], a["L1_gnn_W"].rearrange("r i o -> i r o")).then_inc(loaded, 16)
            for k in range(3):
                sp.dma_start(rel_b[k:k + 1, :, :], a["L1_gnn_b"].unsqueeze(0)).then_inc(loaded, 16)
                for i, name in enumerate(biases):
                    sp.dma_start(bias[k:k + 1, i, :], a[name].unsqueeze(0)).then_inc(loaded, 16)
            sp.dma_start(m.gamma[:, 0, :], a["L2_gnn_gamma"].partition_broadcast(P)).then_inc(loaded, 16)
            sp.dma_start(m.beta[:, 0, :], a["L2_gnn_beta"].partition_broadcast(P)).then_inc(loaded, 16)

        @block.vector
        def _(dve):
            link = chain(dve, step)
            dve.wait_ge(loaded, 16 * n_loads)
            for j in range(1, PER):
                nc.vector.tensor_copy(m.gamma[:, j, :], m.gamma[:, 0, :])
                nc.vector.tensor_copy(m.beta[:, j, :], m.beta[:, 0, :])
            for width in (4, 2, 1):
                nc.vector.tensor_tensor(rel[:, 0:width, :], rel[:, 0:width, :], rel[:, width:2 * width, :], ALU.add)
                link(nc.vector.tensor_tensor(rel_b[:, 0:width, :], rel_b[:, 0:width, :],
                                             rel_b[:, width:2 * width, :], ALU.add))
            nc.vector.tensor_copy(m.w1[:], rel[:, 0, :])
            nc.vector.tensor_copy(m.b1[:], rel_b[:, 0, :])
            nc.vector.tensor_tensor(bias[:, 1, :], bias[:, 1, :], bias[:, 2, :], ALU.add)
            nc.vector.tensor_tensor(bias[:, 3, :], bias[:, 3, :], bias[:, 4, :], ALU.add)
            for k in range(3):
                last = nc.vector.tensor_scalar(pick[:, k:k + 1], m.iota_part[0:3, :], float(k), None, ALU.is_equal)
            link(last)
            for out, i in ((m.b0, 0), (m.b2, 1), (m.b3, 3)):
                link(nc.vector.tensor_copy(hi[:], bias[:, i, :]))
                link(nc.vector.tensor_tensor(rest[:], bias[:, i, :], hi[:], ALU.subtract))
                link(nc.vector.tensor_copy(mid[:], rest[:]))
                link(nc.vector.tensor_tensor(lo[:], rest[:], mid[:], ALU.subtract))
                link(nc.vector.tensor_scalar(one[:], hi[:], pick[:, 0:1], None, ALU.mult))
                link(nc.vector.scalar_tensor_tensor(one[:], mid[:], pick[:, 1:2], one[:], ALU.mult, ALU.add))
                link(nc.vector.scalar_tensor_tensor(one[:], lo[:], pick[:, 2:3], one[:], ALU.mult, ALU.add))
                for j in range(PER):
                    last = nc.vector.tensor_copy(out[:, j * D:(j + 1) * D], one[:])
                link(last)


def phase_edges(nc, d, m, a):
    with ExitStack() as ctx:
        take = ctx.enter_context(semaphores(nc))

        names = ["src", "dst", "edge_weight"]
        rows = [ctx.enter_context(nc.sbuf_tensor(f"rows_{n}", [P, 4, P], F32 if n == "edge_weight" else I32))
                for n in names]
        rows_f = [ctx.enter_context(nc.sbuf_tensor(f"rowsf_{n}", [P, 4, P], F32)) for n in names[:2]]
        row_f = [ctx.enter_context(nc.sbuf_tensor(f"rowf_{n}", [P, d.NC], F32)) for n in names[:2]]
        filled = take("rows_filled")
        loaded = take("rows_loaded")
        as_float = take("rows_as_float")
        turned = take("rows_turned")
        copied = take("rows_copied")
        masked = take("rows_masked")
        block = ctx.enter_context(nc.Block())
        pieces = rows_pieces(d)

        @block.sync
        def _(sp):
            sp.wait_ge(filled, 1)
            for n, tile in zip(names, rows):
                for k, p0, np_, e0, w in pieces:
                    sp.dma_start(tile[p0:p0 + np_, k, 0:w],
                                 a[n][e0:e0 + (np_ - 1) * P + w].rearrange("(p w) -> p w", w=w)).then_inc(loaded, 16)

        @block.vector
        def _(dve):
            nc.vector.memset(rows[0][:], d.KEY_PAD)
            nc.vector.memset(rows[1][:], d.KEY_PAD)
            nc.vector.memset(rows[2][:], 0.0).then_inc(filled, 1)
            dve.wait_ge(loaded, 16 * 3 * len(pieces))
            nc.vector.tensor_copy(rows_f[0][:], rows[0][:])
            nc.vector.tensor_copy(rows_f[1][:], rows[1][:]).then_inc(as_float, 1)
            dve.wait_ge(turned, 1)
            nc.vector.tensor_copy(m.key_src[:], m.bank[0][:, 0:d.NC])
            nc.vector.tensor_copy(m.key_dst[:], m.bank[1][:, 0:d.NC])
            nc.vector.tensor_copy(m.ev[:], m.bank[2][:, 0:d.NC]).then_inc(copied, 1)
            dve.wait_ge(copied, 1)
            for key, out in ((m.key_src, row_f[0]), (m.key_dst, row_f[1])):
                last = nc.vector.scalar_tensor_tensor(out[:], key[:], float(d.N), key[:], ALU.is_lt, ALU.mult)
            last.then_inc(masked, 1)
            dve.wait_ge(masked, 1)
            nc.vector.tensor_copy(m.row_src[:], row_f[0][:])
            nc.vector.tensor_copy(m.row_dst[:], row_f[1][:])

        @block.tensor
        def _(pe):
            pe.wait_ge(as_float, 1)
            for i, tile in enumerate((rows_f[0], rows_f[1], rows[2])):
                for k in range(4):
                    last = nc.tensor.transpose(m.bank[i][:, k * d.RB:(k + 1) * d.RB], tile[0:d.RB, k, :],
                                               m.ident[0:d.RB, 0:d.RB])
            last.then_inc(turned, 1)


def phase_segments(nc, d, m, a, weights_dram):
    SP, SW = d.SP, d.SW
    with ExitStack() as ctx:
        take = ctx.enter_context(semaphores(nc))

        def sb(name, shape, dt=F32):
            return ctx.enter_context(nc.sbuf_tensor(name, shape, dt))

        def sem(name):
            return take(name)

        dst_i, prev_i, next_i = (sb(n, [SP, SW], I32) for n in ("sg_dst", "sg_prev", "sg_next"))
        ev = sb("sg_ev", [SP, SW])
        same_prev, same_next, ends = sb("same_prev", [SP, SW]), sb("same_next", [SP, SW]), sb("seg_ends", [SP, SW])
        reset = sb("sg_reset", [SP, SW])
        ones = sb("sg_ones", [SP, SW])
        top, ex, work, work2 = sb("sg_top", [SP, SW]), sb("sg_ex", [SP, SW]), sb("sg_work", [SP, SW]), sb("sg_work2", [SP, SW])
        alpha, mean, rsq = sb("sg_alpha", [SP, SW]), sb("sg_mean", [SP, SW]), sb("sg_rsq", [SP, SW])
        cols = sb("sg_cols", [SP, 8])
        carry = sb("sg_carry", [SP, 8])
        whole = sb("sg_whole", [1, 3, SP])
        over = sb("sg_over", [1, 6, SP + 1])
        wrows = sb("wrows", [P, 3, 4, P])
        filled, loaded, step = sem("sg_filled"), sem("sg_loaded"), sem("sg_step")
        col_ready, row_done, row_ready, col_done = sem("sg_col_ready"), sem("sg_row_done"), sem("sg_row_ready"), sem("sg_col_done")
        shifted, expd, rooted, stored = sem("sg_shifted"), sem("sg_exp"), sem("sg_rooted"), sem("sg_stored")
        w_ready, reloaded, turned = sem("sg_w_ready"), sem("sg_reloaded"), sem("sg_turned")
        deg_ready = sem("sg_deg_ready")
        block = ctx.enter_context(nc.Block())
        pieces = rows_pieces(d)
        row_ps = m.bank[0]
        col_ps = m.bank[1]

        @block.sync
        def _(sp):
            dst, E = a["dst"], d.E
            sp.dma_start(dst_i[:], dst.rearrange("(p w) -> p w", w=SW)).then_inc(loaded, 16)
            sp.dma_start(ev[:], a["edge_weight"].rearrange("(p w) -> p w", w=SW)).then_inc(loaded, 16)
            sp.wait_ge(filled, 1)
            sp.dma_start(prev_i[0:1, 1:SW], dst[0:SW - 1].unsqueeze(0)).then_inc(loaded, 16)
            sp.dma_start(prev_i[1:SP, :], dst[SW - 1:E - 1].rearrange("(p w) -> p w", w=SW)).then_inc(loaded, 16)
            sp.dma_start(next_i[0:SP - 1, :], dst[1:E - SW + 1].rearrange("(p w) -> p w", w=SW)).then_inc(loaded, 16)
            sp.dma_start(next_i[SP - 1:SP, 0:SW - 1], dst[E - SW + 1:E].unsqueeze(0)).then_inc(loaded, 16)
            sp.wait_ge(w_ready, 1)
            for i, tile in enumerate((rsq, alpha, mean)):
                sp.dma_start(weights_dram[i, :].rearrange("(p w) -> p w", w=SW), tile[:]).then_inc(stored, 16)
            sp.wait_ge(stored, 48)
            for i in range(3):
                for k, p0, np_, e0, w in pieces:
                    sp.dma_start(wrows[p0:p0 + np_, i, k, 0:w],
                                 weights_dram[i, e0:e0 + (np_ - 1) * P + w].rearrange("(p w) -> p w", w=w)).then_inc(reloaded, 16)

        @block.vector
        def _(dve):
            link = chain(dve, step)
            nc.vector.memset(prev_i[:], -1)
            nc.vector.memset(next_i[:], -1).then_inc(filled, 1)
            nc.vector.memset(wrows[:], 0.0)
            nc.vector.memset(ones[:], 1.0)
            nc.vector.memset(over[:], 0.0)
            dve.wait_ge(loaded, 96)
            nc.vector.tensor_tensor(same_prev[:], dst_i[:], prev_i[:], ALU.is_equal)
            link(nc.vector.tensor_tensor(same_next[:], dst_i[:], next_i[:], ALU.is_equal))
            nc.vector.tensor_scalar(ends[:], same_next[:], -1.0, 1.0, ALU.mult, ALU.add)
            nc.vector.tensor_scalar(reset[:], same_prev[:], -1.0, BIG, ALU.add, ALU.mult)
            nc.vector.tensor_reduce(cols[:, 0:1], same_prev[:], AX.X, ALU.min)
            nc.vector.tensor_reduce(cols[:, 1:2], same_next[:], AX.X, ALU.min).then_inc(col_ready, 2)
            dve.wait_ge(row_done, 2)
            link(nc.vector.tensor_copy(whole[0:1, 0:2, :], row_ps[0:1, 0:2 * SP].rearrange("o (k p) -> o k p", k=2)))
            nc.vector.memset(over[0:1, 0, 0:1], -BIG)
            link(nc.vector.tensor_scalar(whole[0:1, 2, :], whole[0:1, 0, :], -1.0, BIG, ALU.add, ALU.mult))

            def scan(k, out, data0, data1, op0, op1, row0, start, backwards):
                turn = (lambda x: x[:, ::-1]) if backwards else (lambda x: x)
                link(nc.vector.tensor_tensor_scan(turn(out[:]), turn(data0[:]), turn(data1[:]), start, op0, op1))
                last = 0 if backwards else SW - 1
                nc.vector.tensor_copy(cols[:, 2 + k:3 + k], out[:, last:last + 1]).then_inc(col_ready, 1)
                dve.wait_ge(row_done, 3 + k)
                first = 0 if backwards else 1
                nc.vector.tensor_tensor_scan(turn(over[0:1, k, first:first + SP]), turn(row0),
                                             turn(row_ps[0:1, 0:SP]), start, op0, op1).then_inc(row_ready, 1)
                dve.wait_ge(col_done, 1 + k)
                link(nc.vector.tensor_copy(carry[:, k:k + 1], col_ps[0:SP, 0:1]))
                link(nc.vector.tensor_tensor_scan(turn(out[:]), turn(data0[:]), turn(data1[:]),
                                                  carry[:, k:k + 1], op0, op1))

            def total(k, out, inclusive):
                link(nc.vector.tensor_tensor(inclusive[:], inclusive[:], ends[:], ALU.mult))
                scan(k, out, same_next, inclusive, ALU.mult, ALU.add, whole[0:1, 1, :], 0.0, True)

            scan(0, work, reset, ev, ALU.add, ALU.max, whole[0:1, 2, :], -BIG, False)
            total(1, top, work)
            nc.vector.tensor_tensor(ex[:], ev[:], top[:], ALU.subtract).then_inc(shifted, 1)
            scan(2, work, same_prev, ones, ALU.mult, ALU.add, whole[0:1, 0, :], 0.0, False)
            total(3, mean, work)
            link(nc.vector.tensor_copy(work2[:], mean[:]))
            nc.vector.engine_nop().then_inc(deg_ready, 1)
            link(nc.vector.reciprocal(mean[:], work2[:]))
            dve.wait_ge(expd, 1)
            scan(4, work, same_prev, alpha, ALU.mult, ALU.add, whole[0:1, 0, :], 0.0, False)
            total(5, top, work)
            link(nc.vector.reciprocal(top[:], top[:]))
            link(nc.vector.tensor_tensor(alpha[:], alpha[:], top[:], ALU.mult))
            dve.wait_ge(rooted, 1)
            link(nc.vector.reciprocal(rsq[:], rsq[:]))
            nc.vector.engine_nop().then_inc(w_ready, 1)
            dve.wait_ge(turned, 1)
            nc.vector.tensor_copy(m.w_in[:], m.bank[2][:, 0:d.NC])
            nc.vector.tensor_scalar(m.w_alpha[:], m.bank[3][:, 0:d.NC], HALF_SCALE, None, ALU.mult)
            nc.vector.tensor_scalar(m.w_mean[:], m.bank[4][:, 0:d.NC], HALF_SCALE, None, ALU.mult)

        @block.scalar
        def _(act):
            act.wait_ge(shifted, 1)
            nc.scalar.activation(alpha[:], ex[:], ACT.Exp).then_inc(expd, 1)
            act.wait_ge(deg_ready, 1)
            nc.scalar.activation(rsq[:], work2[:], ACT.Sqrt).then_inc(rooted, 1)

        @block.tensor
        def _(pe):
            pe.wait_ge(col_ready, 2)
            nc.tensor.transpose(row_ps[0:1, 0:SP], cols[:, 0:1], m.ident[0:SP, 0:SP])
            nc.tensor.transpose(row_ps[0:1, SP:2 * SP], cols[:, 1:2], m.ident[0:SP, 0:SP]).then_inc(row_done, 2)
            for k in range(6):
                backwards = k % 2
                pe.wait_ge(col_ready, 3 + k)
                nc.tensor.transpose(row_ps[0:1, 0:SP], cols[:, 2 + k:3 + k], m.ident[0:SP, 0:SP]).then_inc(row_done, 1)
                pe.wait_ge(row_ready, 1 + k)
                nc.tensor.transpose(col_ps[0:SP, 0:1], over[0:1, k, backwards:backwards + SP],
                                    m.ident[0:1, 0:1]).then_inc(col_done, 1)
            pe.wait_ge(reloaded, 16 * 3 * len(pieces))
            for i in range(3):
                for k in range(4):
                    last = nc.tensor.transpose(m.bank[2 + i][:, k * d.RB:(k + 1) * d.RB], wrows[0:d.RB, i, k, :],
                                               m.ident[0:d.RB, 0:d.RB])
            last.then_inc(turned, 1)


def phase_histogram(nc, d, m, norm_dram, sorts):
    with ExitStack() as ctx:
        take = ctx.enter_context(semaphores(nc))

        def sb(name, shape, dt):
            return ctx.enter_context(nc.sbuf_tensor(name, shape, dt))

        def sem(name):
            return take(name)

        U = RING
        oh_tile = sb("oh_tile", [P, 2, d.TILES], BF16)
        oh_node = sb("oh_node", [P, 2, P], BF16)
        oh_src = sb("oh_src", [P, 2, d.NG], BF16)
        oh_dst = sb("oh_dst", [P, 2, d.NG], BF16)
        deg = sb("deg", [d.TH, d.KH, P], F32)
        deg_r = sb("deg_r", [d.TH, d.KH, P], F32)
        incl = sb("incl", [P, 2, d.NG], F32)
        incl_i = sb("incl_i", [P, 2, d.NG], I32)
        start_f = sb("start_f", [P, d.NG], F32)
        start_i = sb("start_i", [P, 2, d.NG], I32)
        zeros = sb("h_zeros", [P, d.NG], F32)
        built, used, step = sem("hist_built"), sem("hist_used"), sem("hist_step")
        at_least_one, rooted, table_ready, stored = sem("hist_max"), sem("hist_root"), sem("hist_table"), sem("hist_stored")
        hist = m.bank[0:-(-d.KH // 4)]
        block = ctx.enter_context(nc.Block())

        def hist_ap(k):
            return hist[k // 4][0:d.TH, (k % 4) * P:(k % 4 + 1) * P]

        @block.vector
        def _(dve):
            link = chain(dve, step)
            with dve.Fori(0, d.NC // U) as i:
                for u in range(U):
                    c, s = i * U + u, u % 2
                    col = bass.ds(c, 1)
                    dve.wait_ge(used, c + 1)
                    nc.vector.tensor_scalar(oh_tile[:, s, :], m.iota_half[:, 0:d.TILES], sorts.src_tile[:, col], None, ALU.is_equal)
                    nc.vector.tensor_scalar(oh_node[:, s, :], m.iota_half[:, 0:P], sorts.src_node[:, col], None, ALU.is_equal)
                    nc.vector.tensor_scalar(oh_src[:, s, :], m.iota_half[:, 0:d.NG], sorts.src_group[:, col], None, ALU.is_equal)
                    nc.vector.tensor_scalar(oh_dst[:, s, :], m.iota_half[:, 0:d.NG], sorts.dst_group[:, col], None, ALU.is_equal).then_inc(built, 1)
            dve.wait_ge(used, d.NC + 2)
            for k in range(d.KH):
                last = nc.vector.tensor_scalar(deg[:, k, :], hist_ap(k), 1.0, None, ALU.max)
            last.then_inc(at_least_one, 1)
            link(nc.vector.memset(zeros[:], 0.0))
            for k in range(2):
                last = nc.vector.tensor_tensor_scan(incl[:, k, :], m.bank[2 + k][:, 0:d.NG], zeros[:], 0.0, ALU.add, ALU.add)
            link(last)
            nc.vector.tensor_copy(incl_i[:], incl[:])
            link(nc.vector.tensor_tensor(start_f[:], incl[:, 0, :], m.bank[2][:, 0:d.NG], ALU.subtract))
            link(nc.vector.tensor_copy(start_i[:, 0, :], start_f[:]))
            link(nc.vector.tensor_copy(start_i[:, 1, :], start_f[:]))
            nc.vector.tensor_scalar(incl_i[:], incl_i[:], 7, None, ALU.arith_shift_right)
            nc.vector.tensor_scalar(start_i[:, 0, :], start_i[:, 0, :], 7, None, ALU.arith_shift_right)
            link(nc.vector.tensor_scalar(start_i[:, 1, :], start_i[:, 1, :], 127, None, ALU.bitwise_and))
            link(nc.vector.tensor_scalar(start_f[:], start_i[:, 1, :], m.iota_part[:], None, ALU.is_gt))
            nc.vector.tensor_tensor(sorts.earlier[:, 0, :], start_f[:], start_i[:, 0, :], ALU.add)
            nc.vector.tensor_scalar(m.end_src[:], incl_i[0:1, 0, :], float(d.NC - 1), None, ALU.min)
            nc.vector.tensor_scalar(m.end_dst[:], incl_i[0:1, 1, :], float(d.NC - 1), None, ALU.min)
            dve.wait_ge(rooted, 1)
            nc.vector.reciprocal(deg_r[:], deg_r[:]).then_inc(table_ready, 1)

        @block.scalar
        def _(act):
            act.wait_ge(at_least_one, 1)
            nc.scalar.activation(deg_r[:], deg[:], ACT.Sqrt).then_inc(rooted, 1)

        @block.tensor
        def _(pe):
            pe.sem_inc(used, 2)

            for bank in hist:
                nc.tensor.matmul(bank[:], m.zeros[:, 0:P], m.zeros[:], start=True, stop=False)

            def chunk(c, s, first, last_one):
                pe.wait_ge(built, c + 1)
                for k in range(d.KH):
                    ends_bank = k % 4 == 3 or k == d.KH - 1
                    nc.tensor.matmul(hist_ap(k), oh_tile[:, s, k * d.TH:(k + 1) * d.TH], oh_node[:, s, :], start=False,
                                     stop=last_one and ends_bank)
                nc.tensor.matmul(m.bank[2][:, 0:d.NG], m.ones[:], oh_src[:, s, :], start=first, stop=last_one)
                nc.tensor.matmul(m.bank[3][:, 0:d.NG], m.ones[:], oh_dst[:, s, :], start=first, stop=last_one).then_inc(used, 1)

            chunk(0, 0, True, False)
            chunk(1, 1, False, False)
            with pe.Fori(1, d.NC // 2 - 1) as i:
                for u in range(2):
                    chunk(i * 2 + u, u, False, False)
            chunk(d.NC - 2, 0, False, False)
            chunk(d.NC - 1, 1, False, True)

        @block.sync
        def _(sp):
            sp.wait_ge(table_ready, 1)
            sp.dma_start(norm_dram.rearrange("(k r l) o -> r k (l o)", k=d.KH, l=P), deg_r[:]).then_inc(stored, 16)
            sp.wait_ge(stored, 16)


class Sorts:

    def __init__(self, nc, ctx, d):
        def sb(name, shape, dt=F32):
            return ctx.enter_context(nc.sbuf_tensor(name, shape, dt))

        self.src_tile, self.src_node = sb("src_tile", [P, d.NC]), sb("src_node", [P, d.NC])
        self.src_group, self.dst_group = sb("src_group", [P, d.NC]), sb("dst_group", [P, d.NC])
        self.earlier = sb("earlier", [P, 4, d.NG], F16)
        self.place = sb("place", [P, d.NC])
        self.place_i = sb("place_i", [P, 2, d.NC], I32)
        self.target = sb("target", [P, d.NC], I32)
        self.cut = sb("cut_i", [P, 5, d.NC], I32)


def phase_digits(nc, d, m, s):
    with ExitStack() as ctx:
        take = ctx.enter_context(semaphores(nc))

        step = take("digits_step")
        block = ctx.enter_context(nc.Block())

        @block.vector
        def _(dve):
            link = chain(dve, step)
            for k, key in enumerate((m.key_src, m.key_src, m.key_src, m.key_dst)):
                last = nc.vector.tensor_copy(s.cut[:, k, :], key[:])
            link(last)
            nc.vector.tensor_scalar(s.cut[:, 0, :], s.cut[:, 0, :], 7, None, ALU.arith_shift_right)
            nc.vector.tensor_scalar(s.cut[:, 1, :], s.cut[:, 1, :], 127, None, ALU.bitwise_and)
            nc.vector.tensor_scalar(s.cut[:, 2, :], s.cut[:, 2, :], 8, None, ALU.arith_shift_right)
            link(nc.vector.tensor_scalar(s.cut[:, 3, :], s.cut[:, 3, :], 8, None, ALU.arith_shift_right))
            for k, out in enumerate((s.src_tile, s.src_node, s.src_group, s.dst_group)):
                nc.vector.tensor_copy(out[:], s.cut[:, k, :])
            nc.vector.tensor_copy(m.records[:, :, 0], m.row_dst[:])
            nc.vector.tensor_copy(m.records[:, :, 1], m.key_src[:])
            nc.vector.tensor_copy(m.records[:, :, 2], m.ev[:])
            nc.vector.tensor_copy(m.records[:, :, 3], m.ev[:])


def phase_rank(nc, d, m, s, norm_dram):
    with ExitStack() as ctx:
        take = ctx.enter_context(semaphores(nc))

        def sb(name, shape, dt):
            return ctx.enter_context(nc.sbuf_tensor(name, shape, dt))

        def sem(name):
            return take(name)

        one_hot = sb("rank_hot", [P, 4, d.NG], F16)
        unused = sb("rank_unused", [P, 4, d.NG], BF16)
        index = sb("norm_index", [P, RING], I32)
        norms = sb("norm_rows", [P, RING], F32)
        norm_out = sb("norm_out", [P, d.NC], F32)
        hot_built, ranked, read = sem("rank_built"), sem("rank_ready"), sem("rank_read")
        index_staged = sem("norm_index_staged")
        past_wait = sem("norm_past_wait")
        gathered = [sem(f"norm_gathered{u}") for u in range(RING)]
        counted, copied, step = sem("rank_counted"), sem("norm_copied"), sem("rank_step")
        block = ctx.enter_context(nc.Block())

        @block.vector
        def _(dve):
            link = chain(dve, step)

            def build(c, slot):
                wait_from(dve, read, c - 3)
                nc.vector.tensor_scalar(one_hot[:, slot, :], m.iota_half[:, 0:d.NG], s.src_group[:, bass.ds(c, 1)], None,
                                        ALU.is_equal).then_inc(hot_built, 1)

            def count(c, slot):
                dve.wait_ge(hot_built, c + 1)
                wait_from(dve, counted, c)
                wait_from(dve, ranked, c - 2)
                nc.vector.tensor_tensor(s.earlier[:, (slot + 1) % 4, :], s.earlier[:, slot, :], one_hot[:, slot, :],
                                        ALU.add).then_inc(counted, 1)

            def extract(c, slot):
                dve.wait_ge(ranked, c + 1)
                wait_from(dve, read, c - 3)
                nc.vector.scalar_tensor_tensor(unused[:, slot, :], m.bank[slot][:, 0:d.NG], 1.0, one_hot[:, slot, :], ALU.mult, ALU.mult,
                                               accum_out=s.place[:, bass.ds(c, 1)]).then_inc(read, 1)

            build(0, 0)
            build(1, 1)
            count(0, 0)
            build(2, 2)
            count(1, 1)
            extract(0, 0)
            for c in (1, 2, 3):
                build(c + 2, (c + 2) % 4)
                count(c + 1, (c + 1) % 4)
                extract(c, c % 4)
            with dve.Fori(1, d.NC // 4 - 1) as i:
                for u in range(4):
                    build(i * 4 + u + 2, (u + 2) % 4)
                    count(i * 4 + u + 1, (u + 1) % 4)
                    extract(i * 4 + u, u)
            for u in range(4):
                c = d.NC - 4 + u
                if u < 2:
                    build(c + 2, u + 2)
                if u < 2:
                    count(c + 1, u + 1)
                extract(c, u)
            dve.wait_ge(read, d.NC)
            nc.vector.tensor_copy(s.place_i[:, 0, :], s.place[:])
            link(nc.vector.tensor_copy(s.place_i[:, 1, :], s.place[:]))
            nc.vector.tensor_scalar(s.place_i[:, 0, :], s.place_i[:, 0, :], 7, None, ALU.arith_shift_right)
            link(nc.vector.tensor_scalar(s.place_i[:, 1, :], s.place_i[:, 1, :], 127, None, ALU.bitwise_and))
            link(nc.vector.scalar_tensor_tensor(s.target[:], s.place_i[:, 1, :], float(d.NC), s.place_i[:, 0, :], ALU.mult, ALU.add))
            dve.wait_ge(copied, d.NC // RING)
            nc.vector.tensor_tensor(m.w_gcn[:], norm_out[:], m.w_in[:], ALU.mult)

        @block.tensor
        def _(pe):
            def chunk(c, slot):
                pe.wait_ge(hot_built, c + 1)
                wait_from(pe, counted, c)
                wait_from(pe, read, c - 3)
                nc.tensor.matmul(m.bank[slot][:, 0:d.NG], m.before[:], one_hot[:, slot, :], start=True, stop=False)
                nc.tensor.matmul(m.bank[slot][:, 0:d.NG], m.ones_half[:], s.earlier[:, slot, :], start=False,
                                 stop=True).then_inc(ranked, 1)

            for c in range(4):
                chunk(c, c)
            with pe.Fori(1, d.NC // 4) as i:
                for u in range(4):
                    chunk(i * 4 + u, u)

        @block.gpsimd
        def _(pool):
            with pool.Fori(0, d.NC // RING) as i:
                nc.gpsimd.tensor_copy(index[:], m.row_src[:, bass.ds(i * RING, RING)]).then_inc(index_staged, 1)
                pool.wait_ge(index_staged, i + 1)
                pool.sem_inc(past_wait, 1)
                for u in range(RING):
                    nc.gpsimd.indirect_dma_start(
                        out=norms[:, u:u + 1], out_offset=None, in_=norm_dram,
                        in_offset=bass.IndirectOffsetOnAxis(ap=index[:, u:u + 1], axis=0)).then_inc(gathered[u], 16)
                for u in range(RING):
                    pool.wait_ge(gathered[u], (i + 1) * 16)
                nc.gpsimd.tensor_copy(norm_out[:, bass.ds(i * RING, RING)], norms[:]).then_inc(copied, 1)
                pool.wait_ge(copied, i + 1)
                pool.sem_inc(past_wait, 1)


def phase_scatter(nc, d, m, s, sorted_dram):
    with ExitStack() as ctx:
        take = ctx.enter_context(semaphores(nc))

        def sb(name, shape, dt):
            return ctx.enter_context(nc.sbuf_tensor(name, shape, dt))

        def sem(name):
            return take(name)

        index = sb("place_index", [P, 2, RING], I32)
        sent = sb("records_sent", [P, 2, RING, 4], F32)
        back = sb("records_back", [P, d.NC, 4], F32)
        rest = sb("ev_rest", [P, d.NC], F32)
        staged, past_wait = sem("record_staged"), sem("record_past_wait")
        scattered = [[sem(f"scattered{h}_{u}") for u in range(RING)] for h in range(2)]
        all_done, loaded, step = sem("scatter_done"), sem("sorted_loaded"), sem("sorted_step")
        block = ctx.enter_context(nc.Block())
        rounds = d.NC // RING

        @block.gpsimd
        def _(pool):
            def send(i, h, k):
                nc.gpsimd.tensor_copy(index[:, h, :], s.target[:, bass.ds(i * RING, RING)])
                nc.gpsimd.tensor_copy(sent[:, h, :, :], m.records[:, bass.ds(i * RING, RING), :]).then_inc(staged, 1)
                pool.wait_ge(staged, i + 1)
                pool.sem_inc(past_wait, 1)
                for u in range(RING):
                    nc.gpsimd.indirect_dma_start(
                        out=sorted_dram, out_offset=bass.IndirectOffsetOnAxis(ap=index[:, h, u:u + 1], axis=0),
                        in_=sent[:, h, u, :], in_offset=None).then_inc(scattered[h][u], 16)

            def landed(h, k):
                for u in range(RING):
                    pool.wait_ge(scattered[h][u], 16 * k)
                pool.sem_inc(past_wait, 1)

            send(0, 0, 1)
            send(1, 1, 1)
            with pool.Fori(1, rounds // 2) as k:
                for h in range(2):
                    landed(h, k)
                    send(k * 2 + h, h, k + 1)
            if rounds % 2:
                landed(0, rounds // 2)
                send(rounds - 1, 0, rounds // 2 + 1)
            landed(0, (rounds + 1) // 2)
            landed(1, rounds // 2)
            pool.sem_inc(all_done, 1)

        @block.sync
        def _(sp):
            sp.wait_ge(all_done, 1)
            sp.dma_start(back[:], sorted_dram.rearrange("(p c) f -> p c f", c=d.NC)).then_inc(loaded, 16)

        @block.vector
        def _(dve):
            link = chain(dve, step)
            dve.wait_ge(loaded, 16)
            nc.vector.tensor_copy(m.s_row[:], back[:, :, 0])
            nc.vector.tensor_copy(m.s_key[:], back[:, :, 1])
            link(nc.vector.tensor_copy(m.s_ev[:], back[:, :, 2]))
            link(nc.vector.tensor_copy(m.s_ev_parts[:, :, 0], m.s_ev[:]))
            link(nc.vector.tensor_tensor(rest[:], m.s_ev[:], m.s_ev_parts[:, :, 0], ALU.subtract))
            link(nc.vector.tensor_copy(m.s_ev_parts[:, :, 1], rest[:]))
            link(nc.vector.tensor_tensor(m.s_ev_parts[:, :, 2], rest[:], m.s_ev_parts[:, :, 1], ALU.subtract))


GCN, REL, ATT, SAGE = "gcn", "rel", "att", "sage"


class At:

    def __init__(self, k, u, lag=0):
        self.k = k + (u - lag) // SLOTS
        self.u = (u - lag) % SLOTS
        self.b = self.k * SLOTS + self.u
        self.pair = self.u % 2


def over_blocks(engine, d, lags, body):
    def known(step):
        def at(lag):
            here = At(step // SLOTS, step % SLOTS, lag)
            return here if 0 <= here.b < d.NB else None
        body(at)

    for step in range(2 * SLOTS):
        known(step)
    with engine.Fori(2, d.NB // SLOTS - 1) as k:
        for u in range(SLOTS):
            body(lambda lag: At(k, u, lag))
    for step in range(d.NB - SLOTS, d.NB + lags):
        known(step)


def wait_from(engine, semaphore, value):
    if not isinstance(value, int) or value > 0:
        engine.wait_ge(semaphore, value)


def phase_layer(nc, d, m, kind, x_in, x_out, rows_out, row, key, weight, ends):
    att, transposed = kind == ATT, kind in (ATT, SAGE)
    n_sums = 2 if kind in (ATT, SAGE) else 3
    part_type = F16 if n_sums == 2 else BF16
    unscale = 1.0 / HALF_SCALE if n_sums == 2 else 1.0
    n_parts = 4 if kind == REL else n_sums
    node_lag = 3 if att else 2
    stats_lag = 4 if att else 2
    root_lag = stats_lag + 1
    scale_lag = root_lag + 1
    norm_lag = scale_lag + 1
    out_lag = norm_lag + 1
    with ExitStack() as ctx:
        take = ctx.enter_context(semaphores(nc))

        def sb(name, shape, dt=F32):
            return ctx.enter_context(nc.sbuf_tensor(f"{kind}_{name}", shape, dt))

        def sem(name):
            return take(f"{kind}_{name}")

        index = sb("index", [P, RING], I32)
        raw = sb("raw", [P, RING, D])
        parts = sb("parts", [P, RING * n_parts, D], part_type)
        resid = sb("resid", [P, RING, D]) if n_sums == 3 else None
        hot = sb("hot", [P, RING, GROUP], part_type)
        x = sb("x", [P, SLOTS, PER, D])
        agg = sb("agg", [P, 2, BLOCK])
        xt = sb("xt", [P, 2, BLOCK])
        y = sb("y", [P, SLOTS, PER, D])
        out = sb("out", [P, SLOTS, PER, D])
        stats = sb("stats", [P, SLOTS, PER, 6])
        moments = sb("moments", [P, SLOTS, PER, 2])
        root = sb("root", [P, SLOTS, PER])
        scale = sb("scale", [P, SLOTS, PER])
        shift = sb("shift", [P, SLOTS, PER])
        ev_sum = sb("ev_sum", [3, 2, BLOCK]) if kind == REL else None
        if att:
            square = sb("square", [P, 2, BLOCK])
            own = sb("own", [P, SLOTS, PER, D])
            u_ = sb("u", [P, SLOTS, PER, D])
            t_ = sb("t", [P, SLOTS, PER, D])
            xb = sb("xb", [P, SLOTS, PER, D])
            agg_norm = sb("agg_norm", [P, SLOTS, PER])
            inv = sb("inv", [P, SLOTS, PER])
            moments_u = sb("moments_u", [P, SLOTS, PER, 2])
            mean_sq = sb("mean_sq", [P, SLOTS, PER])
            u_norm = sb("u_norm", [P, SLOTS, PER])
            s_ = sb("s", [P, SLOTS, PER])
            s_sq = sb("s_sq", [P, SLOTS, PER])
            s_var = sb("s_var", [P, SLOTS, PER])
            root_var = sb("root_var", [P, SLOTS, PER])
            k_ = sb("k", [P, SLOTS, PER])
            shift_u = sb("shift_u", [P, SLOTS, PER])
            stats_u = sb("stats_u", [P, SLOTS, PER, 6])

        past_wait, past_dve_wait = sem("past_wait"), sem("past_dve_wait")
        index_staged = sem("index_staged")
        gathered = [sem(f"gathered{u}") for u in range(RING)]
        raw_ready, raw_free = sem("raw_ready"), sem("raw_free")
        hi_done, mid_done = sem("hi_done"), sem("mid_done")
        low_done = sem("low_done") if n_sums == 3 else None
        hot_built, pairs_done = sem("hot_built"), sem("pairs_done")
        x_loaded = [sem(f"x_loaded{u}") for u in range(SLOTS)]
        stored = [sem(f"stored{u}") for u in range(SLOTS)]
        agg_summed, agg_copied = sem("agg_summed"), sem("agg_copied")
        x_turned, xt_copied = sem("x_turned"), sem("xt_copied")
        y_ready, summed = sem("y_ready"), sem("summed")
        x_used = sem("x_used") if att else summed
        stats_done, moments_done, rooted, inverted, scaled, normed = (sem(n) for n in (
            "stats_done", "moments_done", "rooted", "inverted", "scaled", "normed"))
        zeroed, step = sem("zeroed"), sem("step")
        if att:
            own_copied, agg_rooted, mean_ready, u_rooted = sem("own_copied"), sem("agg_rooted"), sem("mean_ready"), sem("u_rooted")
            k_step, var_ready, var_rooted, k_ready, t_ready, t_scaled = (sem(n) for n in (
                "k_step", "var_ready", "var_rooted", "k_ready", "t_ready", "t_scaled"))
        agg_ps = m.bank[0:2]
        y_ps = m.bank[2:4]
        xt_ps = m.bank[4]
        own_ps = m.bank[5:7]
        ev_ps = m.bank[6:8]
        norm_ps = m.bank[7]
        block = ctx.enter_context(nc.Block())

        def slot(c):
            return bass.ds(c % RING, 1)

        def part(c, k):
            return parts[:, bass.ds(c % RING * n_parts + k, 1), :].rearrange("p s f -> p (s f)")

        def flat(ap):
            return ap.rearrange("p j f -> p (j f)")

        @block.gpsimd
        def _(pool):
            pool.sem_inc(raw_free, RING)
            half = RING // 2

            def gather(i, h):
                nc.gpsimd.tensor_copy(index[:, h * half:(h + 1) * half],
                                      row[:, bass.ds(i * RING + h * half, half)]).then_inc(index_staged, 1)
                pool.wait_ge(index_staged, i * 2 + h + 1)
                for u in range(h * half, (h + 1) * half):
                    pool.wait_ge(raw_free, i * RING + u + 1)
                    pool.sem_inc(past_wait, 1)
                    nc.gpsimd.indirect_dma_start(
                        out=raw[:, u, :], out_offset=None, in_=x_in,
                        in_offset=bass.IndirectOffsetOnAxis(ap=index[:, u:u + 1], axis=0)).then_inc(gathered[u], 16)

            def pass_on(i, h):
                for u in range(h * half, (h + 1) * half):
                    pool.wait_ge(gathered[u], (i + 1) * 16)
                    pool.sem_inc(raw_ready, 1)

            gather(0, 0)
            gather(0, 1)
            pass_on(0, 0)
            with pool.Fori(1, d.NC // RING) as i:
                gather(i, 0)
                pass_on(i - 1, 1)
                gather(i, 1)
                pass_on(i, 0)
            pass_on(d.NC // RING - 1, 1)

        @block.sync
        def _(sp):
            def body(at):
                here = at(0)
                if here:
                    wait_from(sp, x_used, here.b - SLOTS + 1)
                    rows = x_in.shape[0]
                    if isinstance(here.b, int) and (here.b + 1) * BLOCK > rows:
                        p = (rows - here.b * BLOCK) // PER
                        sp.dma_start(flat(x[0:p, here.u, :, :]), x_in[here.b * BLOCK:rows, :].rearrange(
                            "(p j) f -> p (j f)", j=PER)).then_inc(x_loaded[here.u], 16)
                    else:
                        sp.dma_start(flat(x[:, here.u, :, :]), x_in[bass.ds(here.b * BLOCK, BLOCK), :].rearrange(
                            "(p j) f -> p (j f)", j=PER)).then_inc(x_loaded[here.u], 16)
                here = at(out_lag)
                if here:
                    sp.wait_ge(normed, here.b + 1)
                    if isinstance(here.b, int) and (here.b + 1) * BLOCK > rows_out:
                        p = (rows_out - here.b * BLOCK) // PER
                        sp.dma_start(x_out[here.b * BLOCK:rows_out, :].rearrange("(p j) f -> p (j f)", j=PER),
                                     flat(out[0:p, here.u, :, :])).then_inc(stored[here.u], 16)
                    else:
                        sp.dma_start(x_out[bass.ds(here.b * BLOCK, BLOCK), :].rearrange("(p j) f -> p (j f)", j=PER),
                                     flat(out[:, here.u, :, :])).then_inc(stored[here.u], 16)

            over_blocks(sp, d, out_lag, body)
            for u in range(SLOTS):
                sp.wait_ge(stored[u], 16 * (d.NB // SLOTS))

        @block.scalar
        def _(act):
            chunk = act.alloc_register(f"{kind}_act_chunk")
            end = [act.alloc_register(f"{kind}_act_end{i}") for i in range(2 * SLOTS)]
            act.reg_mov(chunk, 0)

            def high(c, g):
                act.wait_ge(raw_ready, c + 1)
                act.wait_ge(pairs_done, c + g + 1)
                nc.scalar.activation(part(c, 0), raw[:, slot(c), :].rearrange("p s f -> p (s f)"), ACT.Copy,
                                     scale=weight[:, bass.ds(c, 1)]).then_inc(hi_done, 1)

            high(0, 0)

            def body(at):
                here = at(0)
                if here:
                    if here.u == 0:
                        act.reg_load(end, ends[0:1, bass.ds(here.b * 2, 2 * SLOTS)])
                    for h in range(2):
                        with act.While(lambda: act.snap(chunk) < act.snap(end[here.u * 2 + h])):
                            act.reg_add(chunk, chunk, 1)
                            high(act.snap(chunk), here.b * 2 + h)
                here = at(1)
                if here:
                    q = here.pair
                    if transposed:
                        act.wait_ge(x_turned, here.b + 1)
                        wait_from(act, y_ready, here.b - 1)
                        nc.scalar.copy(xt[:, q, :], xt_ps[:]).then_inc(xt_copied, 1)
                    act.wait_ge(agg_summed, here.b + 1)
                    wait_from(act, y_ready, here.b - 1)
                    if kind == REL:
                        nc.scalar.copy(ev_sum[:, q, :], ev_ps[q][0:3, :])
                    if att:
                        nc.scalar.activation(square[:, q, :], agg_ps[q][:], ACT.Square, scale=unscale)
                    nc.scalar.activation(agg[:, q, :], agg_ps[q][:], ACT.Copy, scale=unscale).then_inc(agg_copied, 1)
                here = at(2)
                if here and att:
                    act.wait_ge(y_ready, here.b + 1)
                    wait_from(act, summed, here.b - SLOTS + 1)
                    nc.scalar.activation(agg_norm[:, here.u, :], norm_ps[:, 0:PER], ACT.Sqrt).then_inc(agg_rooted, 1)
                    nc.scalar.copy(flat(own[:, here.u, :, :]), own_ps[here.pair][:]).then_inc(own_copied, 1)
                here = at(4)
                if here and att:
                    act.wait_ge(var_ready, here.b + 1)
                    nc.scalar.activation(root_var[:, here.u, :], s_var[:, here.u, :], ACT.Sqrt, bias=m.eps_col[:]).then_inc(var_rooted, 1)
                    act.wait_ge(k_ready, here.b + 1)
                    for j in range(PER):
                        last = nc.scalar.activation(t_[:, here.u, j, :], u_[:, here.u, j, :], ACT.Identity,
                                                    bias=shift_u[:, here.u, j:j + 1], scale=k_[:, here.u, j:j + 1])
                    last.then_inc(t_ready, 1)
                here = at(3)
                if here and att:
                    act.wait_ge(mean_ready, here.b + 1)
                    nc.scalar.activation(u_norm[:, here.u, :], mean_sq[:, here.u, :], ACT.Sqrt, scale=float(D)).then_inc(u_rooted, 1)
                here = at(root_lag)
                if here:
                    act.wait_ge(moments_done, here.b + 1)
                    nc.scalar.activation(root[:, here.u, :], moments[:, here.u, :, 1], ACT.Sqrt, bias=m.eps_col[:]).then_inc(rooted, 1)
                here = at(norm_lag)
                if here:
                    act.wait_ge(scaled, here.b + 1)
                    wait_from(act, stored[here.u], here.k * 16)
                    for j in range(PER):
                        last = nc.scalar.activation(out[:, here.u, j, :], y[:, here.u, j, :], ACT.Identity,
                                                    bias=shift[:, here.u, j:j + 1], scale=scale[:, here.u, j:j + 1])
                    last.then_inc(normed, 1)

            over_blocks(act, d, norm_lag, body)

        @block.vector
        def _(dve):
            chunk = dve.alloc_register(f"{kind}_dve_chunk")
            end = [dve.alloc_register(f"{kind}_dve_end{i}") for i in range(2 * SLOTS)]
            dve.reg_mov(chunk, 0)
            if kind == REL:
                nc.vector.memset(parts[:, 3:RING * n_parts:n_parts, :], 0.0).then_inc(zeroed, 1)
                dve.wait_ge(zeroed, 1)

            def low(c, between=lambda half: None):
                rows = raw[:, slot(c), :].rearrange("p s f -> p (s f)")
                dve.wait_ge(hi_done, c + 1)
                if n_sums == 2:
                    nc.vector.scalar_tensor_tensor(part(c, 1), rows, weight[:, bass.ds(c, 1)], part(c, 0), ALU.mult,
                                                   ALU.subtract).then_inc(raw_free, 1)
                    between(0)
                    between(1)
                    return
                left = resid[:, slot(c), :].rearrange("p s f -> p (s f)")
                nc.vector.scalar_tensor_tensor(left, rows, weight[:, bass.ds(c, 1)], part(c, 0), ALU.mult,
                                               ALU.subtract).then_inc(raw_free, 1)
                if kind == REL:
                    nc.vector.tensor_copy(part(c, 3)[:, 0:3], m.s_ev_parts[:, bass.ds(c, 1), :].rearrange("p c k -> p (c k)"))
                between(0)
                dve.wait_ge(raw_free, c + 1 + RING)
                nc.vector.tensor_copy(part(c, 1), left).then_inc(mid_done, 1)
                between(1)
                dve.wait_ge(mid_done, c + 1)
                nc.vector.tensor_tensor(part(c, 2), left, part(c, 1), ALU.subtract).then_inc(low_done, 1)

            def one_hot(c, g, half):
                to = slice(half * (GROUP // 2), (half + 1) * (GROUP // 2))
                dve.wait_ge(pairs_done, c + g + 1)
                return nc.vector.tensor_scalar(hot[:, slot(c + g), to].rearrange("p s n -> p (s n)"), m.iota_half[:, to],
                                               m.group_base[:, bass.ds(g, 1)], key[:, bass.ds(c, 1)], ALU.add, ALU.is_equal)

            low(0)

            def one_hots(c, g):
                one_hot(c, g, 0)
                one_hot(c, g, 1).then_inc(hot_built, 1)

            def body(at):
                here = at(node_lag)
                if here:
                    dve.wait_ge(y_ready, here.b + 1)
                    dve.wait_ge(x_loaded[here.u], (here.k + 1) * 16)
                    if kind == ATT:
                        dve.wait_ge(agg_rooted, here.b + 1)
                        dve.wait_ge(own_copied, here.b + 1)
                        nc.vector.tensor_scalar(inv[:, here.u, :], agg_norm[:, here.u, :], NORM_EPS, None, ALU.add).then_inc(step, 1)
                        nc.vector.tensor_tensor(flat(xb[:, here.u, :, :]), flat(x[:, here.u, :, :]), flat(m.beta[:]), ALU.add).then_inc(x_used, 1)
                        dve.wait_ge(step, here.b * 5 + 1)
                        nc.vector.reciprocal(inv[:, here.u, :], inv[:, here.u, :]).then_inc(step, 1)
                        dve.wait_ge(step, here.b * 5 + 2)
                        for j in range(PER):
                            last = nc.vector.scalar_tensor_tensor(u_[:, here.u, j, :], y_ps[here.pair][:, j * D:(j + 1) * D],
                                                                  inv[:, here.u, j:j + 1], own[:, here.u, j, :], ALU.mult, ALU.add)
                        last.then_inc(summed, 1)
                        dve.wait_ge(summed, here.b + 1)
                        for j in range(PER):
                            last = nc.vector.bn_stats(stats_u[:, here.u, j, :], u_[:, here.u, j, :])
                        last.then_inc(step, 1)
                        dve.wait_ge(step, here.b * 5 + 3)
                        dve.sem_inc(past_dve_wait, 1)
                        for j in range(PER):
                            last = nc.vector.bn_aggr(moments_u[:, here.u, j, :], stats_u[:, here.u, j, :])
                        last.then_inc(step, 1)
                        dve.wait_ge(step, here.b * 5 + 4)
                        mean, var = moments_u[:, here.u, :, 0], moments_u[:, here.u, :, 1]
                        nc.vector.tensor_tensor(mean_sq[:, here.u, :], mean, mean, ALU.mult).then_inc(step, 1)
                        dve.wait_ge(step, here.b * 5 + 5)
                        nc.vector.tensor_tensor(mean_sq[:, here.u, :], mean_sq[:, here.u, :], var, ALU.add).then_inc(mean_ready, 1)
                    else:
                        wait_from(dve, normed, here.b - SLOTS + 1)
                    if kind == SAGE:
                        nc.vector.tensor_tensor(flat(y[:, here.u, :, :]), y_ps[here.pair][:], flat(x[:, here.u, :, :]),
                                                ALU.add).then_inc(summed, 1)
                    elif not att:
                        nc.vector.scalar_tensor_tensor(flat(y[:, here.u, :, :]), y_ps[here.pair][:], 0.0,
                                                       flat(x[:, here.u, :, :]), ALU.max, ALU.add).then_inc(summed, 1)
                here = at(4)
                if here and att:
                    mean, var = moments_u[:, here.u, :, 0], moments_u[:, here.u, :, 1]
                    dve.wait_ge(u_rooted, here.b + 1)
                    nc.vector.tensor_scalar(s_[:, here.u, :], u_norm[:, here.u, :], 2.0 * NORM_EPS, None, ALU.add).then_inc(k_step, 1)
                    dve.wait_ge(k_step, here.b * 5 + 1)
                    nc.vector.reciprocal(s_[:, here.u, :], s_[:, here.u, :]).then_inc(k_step, 1)
                    dve.wait_ge(k_step, here.b * 5 + 2)
                    nc.vector.tensor_tensor(s_sq[:, here.u, :], s_[:, here.u, :], s_[:, here.u, :], ALU.mult).then_inc(k_step, 1)
                    dve.wait_ge(k_step, here.b * 5 + 3)
                    nc.vector.tensor_tensor(s_var[:, here.u, :], s_sq[:, here.u, :], var, ALU.mult).then_inc(var_ready, 1)
                first = at(0)
                if first:
                    if first.u == 0:
                        dve.reg_load(end, ends[0:1, bass.ds(first.b * 2, 2 * SLOTS)])
                    for h in range(2):
                        g = first.b * 2 + h
                        one_hots(dve.snap(chunk), g)
                        with dve.While(lambda: dve.snap(chunk) < dve.snap(end[first.u * 2 + h])):
                            dve.reg_add(chunk, chunk, 1)
                            c = dve.snap(chunk)

                            def between(half):
                                made = one_hot(c, g, half)
                                if half:
                                    made.then_inc(hot_built, 1)

                            low(c, between)
                if here and att:
                    dve.wait_ge(var_rooted, here.b + 1)
                    nc.vector.reciprocal(k_[:, here.u, :], root_var[:, here.u, :]).then_inc(k_step, 1)
                    dve.wait_ge(k_step, here.b * 5 + 4)
                    nc.vector.tensor_tensor(k_[:, here.u, :], k_[:, here.u, :], s_[:, here.u, :], ALU.mult).then_inc(k_step, 1)
                    dve.wait_ge(k_step, here.b * 5 + 5)
                    nc.vector.scalar_tensor_tensor(shift_u[:, here.u, :], mean, -1.0, k_[:, here.u, :], ALU.mult, ALU.mult).then_inc(k_ready, 1)
                    dve.wait_ge(t_ready, here.b + 1)
                    nc.vector.tensor_tensor(flat(t_[:, here.u, :, :]), flat(t_[:, here.u, :, :]), flat(m.gamma[:]), ALU.mult).then_inc(t_scaled, 1)
                    dve.wait_ge(t_scaled, here.b * 2 + 1)
                    wait_from(dve, normed, here.b - SLOTS + 1)
                    nc.vector.tensor_tensor(flat(y[:, here.u, :, :]), flat(t_[:, here.u, :, :]), flat(xb[:, here.u, :, :]), ALU.add).then_inc(t_scaled, 1)
                here, last_one = at(stats_lag), at(scale_lag)
                if last_one:
                    dve.wait_ge(rooted, last_one.b + 1)
                    nc.vector.reciprocal(scale[:, last_one.u, :], root[:, last_one.u, :]).then_inc(inverted, 1)
                if here:
                    if att:
                        dve.wait_ge(t_scaled, here.b * 2 + 2)
                    else:
                        dve.wait_ge(summed, here.b + 1)
                    for j in range(PER):
                        last = nc.vector.bn_stats(stats[:, here.u, j, :], y[:, here.u, j, :])
                    last.then_inc(stats_done, 1)
                if last_one:
                    dve.wait_ge(inverted, last_one.b + 1)
                    nc.vector.scalar_tensor_tensor(shift[:, last_one.u, :], moments[:, last_one.u, :, 0], -1.0,
                                                   scale[:, last_one.u, :], ALU.mult, ALU.mult).then_inc(scaled, 1)
                if here:
                    dve.wait_ge(stats_done, here.b + 1)
                    dve.sem_inc(past_dve_wait, 1)
                    for j in range(PER):
                        last = nc.vector.bn_aggr(moments[:, here.u, j, :], stats[:, here.u, j, :])
                    last.then_inc(moments_done, 1)

            over_blocks(dve, d, scale_lag, body)

        @block.tensor
        def _(pe):
            chunk = pe.alloc_register(f"{kind}_pe_chunk")
            end = [pe.alloc_register(f"{kind}_pe_end{i}") for i in range(2 * SLOTS)]
            pe.reg_mov(chunk, 0)
            pe.sem_inc(pairs_done, RING)

            def pair(c, g, h, here, stop):
                window = slice(h * GROUP, (h + 1) * GROUP)
                one_hot = hot[:, slot(c + g), :].rearrange("p s n -> p (s n)")
                pe.wait_ge(hot_built, c + g + 1)
                if n_sums == 3:
                    pe.wait_ge(low_done, c + 1)
                else:
                    pe.wait_ge(raw_free, c + 1 + RING)
                if kind == REL:
                    nc.tensor.matmul(ev_ps[here.pair][:, window], part(c, 3), one_hot, start=False, stop=stop)
                for k in range(n_sums):
                    last = nc.tensor.matmul(agg_ps[here.pair][:, window], part(c, k), one_hot, start=False,
                                            stop=stop and k == n_sums - 1)
                last.then_inc(pairs_done, 1)

            def body(at):
                here = at(0)
                if here:
                    if here.u == 0:
                        pe.reg_load(end, ends[0:1, bass.ds(here.b * 2, 2 * SLOTS)])
                    wait_from(pe, agg_copied, here.b - 1)
                    for h in range(2):
                        g = here.b * 2 + h
                        for sums in (agg_ps, ev_ps)[:1 + (kind == REL)]:
                            nc.tensor.matmul(sums[here.pair][:, h * GROUP:(h + 1) * GROUP], m.zeros[:, 0:P], m.zeros[:, 0:GROUP],
                                             start=True, stop=False)
                        with pe.While(lambda: pe.snap(chunk) < pe.snap(end[here.u * 2 + h])):
                            pair(pe.snap(chunk), g, h, here, False)
                            pe.reg_add(chunk, chunk, 1)
                        pair(pe.snap(chunk), g, h, here, True)
                    pe.wait_ge(pairs_done, pe.snap(chunk) + (here.b * 2 + 2 + RING))
                    pe.sem_inc(agg_summed, 1)
                    if transposed:
                        pe.wait_ge(x_loaded[here.u], (here.k + 1) * 16)
                        wait_from(pe, xt_copied, here.b)
                        for j in range(PER):
                            last = nc.tensor.transpose(xt_ps[:, j * P:(j + 1) * P], x[:, here.u, j, :], m.ident[:])
                        last.then_inc(x_turned, 1)
                here = at(1)
                if here:
                    q = here.pair
                    sums = y_ps[q]
                    pe.wait_ge(agg_copied, here.b + 1)
                    wait_from(pe, summed, here.b - 1)
                    aggT = [agg[:, q, j:BLOCK:PER] for j in range(PER)]
                    xT = [xt[:, q, j * P:(j + 1) * P] for j in range(PER)]
                    if kind == GCN or kind == SAGE:
                        nc.tensor.matmul(sums[:], m.ones[0:3, :], (m.b0 if kind == GCN else m.b3)[:], start=True, stop=False)
                    if att:
                        nc.tensor.matmul(own_ps[q][:], m.ones[0:3, :], m.b2[:], start=True, stop=False)
                    for j in range(PER):
                        window = slice(j * D, (j + 1) * D)
                        if kind == GCN:
                            last = nc.tensor.matmul(sums[:, window], aggT[j], m.w0[:], start=False, stop=j == PER - 1)
                        elif kind == REL:
                            nc.tensor.matmul(sums[:, window], ev_sum[:, q, j:BLOCK:PER], m.b1[:], start=True, stop=False)
                            last = nc.tensor.matmul(sums[:, window], aggT[j], m.w1[:], start=False, stop=True)
                        elif kind == SAGE:
                            nc.tensor.matmul(sums[:, window], xT[j], m.w3s[:], start=False, stop=False)
                            last = nc.tensor.matmul(sums[:, window], aggT[j], m.w3n[:], start=False, stop=j == PER - 1)
                        else:
                            nc.tensor.matmul(own_ps[q][:, window], xT[j], m.w2s[:], start=False, stop=j == PER - 1)
                            last = nc.tensor.matmul(sums[:, window], aggT[j], m.w2n[:], start=True, stop=True)
                    if att:
                        wait_from(pe, agg_rooted, here.b)
                        for j in range(PER):
                            last = nc.tensor.matmul(norm_ps[:, j:j + 1], square[:, q, j:BLOCK:PER], m.ones_col[:], start=True, stop=True)
                    last.then_inc(y_ready, 1)

            over_blocks(pe, d, 1, body)


NAMES = ["x", "src", "dst", "edge_weight", "L0_gnn_weight", "L0_gnn_bias", "L1_gnn_W", "L1_gnn_b", "L2_gnn_W_self",
         "L2_gnn_b_self", "L2_gnn_W_nb", "L2_gnn_b_nb", "L2_gnn_gamma", "L2_gnn_beta", "L3_gnn_W_self",
         "L3_gnn_b_self", "L3_gnn_W_neigh", "L3_gnn_b_neigh"]


def program(nc, *args):
    a = dict(zip(NAMES, args))
    result = args[len(NAMES)]
    d = Dims(a["x"].shape[0], a["src"].shape[0])
    weights_dram = nc.dram_tensor("weights_scratch", [3, d.E], F32).ap()
    norm_dram = nc.dram_tensor("norm_scratch", [d.NP, 1], F32).ap()
    sorted_dram = nc.dram_tensor("sorted_scratch", [d.EP, 4], F32).ap()
    x1 = nc.dram_tensor("x1_scratch", [d.NP, D], F32).ap()
    x2 = nc.dram_tensor("x2_scratch", [d.NP, D], F32).ap()
    with ExitStack() as ctx:
        m = Memory(nc, ctx, d)
        with ExitStack() as prep:
            s = Sorts(nc, prep, d)
            phase_constants(nc, d, m)
            phase_weights(nc, d, m, a)
            phase_edges(nc, d, m, a)
            phase_segments(nc, d, m, a, weights_dram)
            phase_digits(nc, d, m, s)
            phase_histogram(nc, d, m, norm_dram, s)
            phase_rank(nc, d, m, s, norm_dram)
            phase_scatter(nc, d, m, s, sorted_dram)
        by_dst = (m.row_src, m.key_dst)
        phase_layer(nc, d, m, GCN, a["x"], x1, d.NP, *by_dst, m.w_gcn, m.end_dst)
        phase_layer(nc, d, m, REL, x1, x2, d.NP, m.s_row, m.s_key, m.s_ev, m.end_src)
        phase_layer(nc, d, m, ATT, x2, x1, d.NP, *by_dst, m.w_alpha, m.end_dst)
        phase_layer(nc, d, m, SAGE, x1, result, d.N, *by_dst, m.w_mean, m.end_dst)


def kernel(**inputs):
    import numpy as np
    import concourse.bacc as bacc
    from concourse.bass_utils import run_bass_kernel_spmd

    nc = bacc.Bacc("TRN2", target_bir_lowering=False, num_devices=1)
    arrays, args = {}, []
    for name in NAMES:
        value = np.ascontiguousarray(inputs[name])
        arrays[f"in_{name}"] = value
        args.append(nc.dram_tensor(f"in_{name}", value.shape, mybir.dt.from_np(value.dtype), kind="ExternalInput").ap())
    args.append(nc.dram_tensor("out_0", arrays["in_x"].shape, F32, kind="ExternalOutput").ap())
    program(nc, *args)
    results = run_bass_kernel_spmd(nc, [arrays], core_ids=[0])
    return results.results[0]["out_0"]
```

```python
from contextlib import ExitStack, contextmanager

import concourse.bass as bass
from concourse import mybir

F32 = mybir.dt.float32
I32 = mybir.dt.int32
BF16 = mybir.dt.bfloat16
F16 = mybir.dt.float16
ALU = mybir.AluOpType
ACT = mybir.ActivationFunctionType
AX = mybir.AxisListType

P = 128
D = 128
GROUP = 256
BLOCK = 512
PER = BLOCK // P
RING = 8
SLOTS = 4
BIG = 1.0e30
HALF_SCALE = 2048.0
LN_EPS = 1e-5
NORM_EPS = 1e-9
N_REL = 8
SPAN = 3


class Dims:

    def __init__(self, n_nodes, n_edges):
        self.N, self.E = n_nodes, n_edges
        self.NB = -(-(n_nodes + GROUP) // (BLOCK * SLOTS)) * SLOTS
        self.NP = self.NB * BLOCK
        self.NG = self.NP // GROUP
        self.NC = -(-n_edges // (P * RING)) * RING
        self.EP = self.NC * P
        self.KEY_PAD = self.NP - GROUP
        self.RB = self.NC // 4
        self.SP = 125
        self.SW = n_edges // self.SP
        self.TILES = self.NP // P
        self.KH = -(-self.TILES // P)
        self.TH = self.TILES // self.KH
        self.NQ = self.NB * SPAN
        self.WT = -(-self.NB // P)
        self.WP = self.NB // self.WT
        assert self.WP * self.WT == self.NB
        assert self.KEY_PAD >= n_nodes and self.SP * self.SW == n_edges and self.TH * self.KH == self.TILES
        assert self.NC <= 512 and self.NG <= 512 and self.RB <= P and n_nodes % PER == 0


class Memory:

    def __init__(self, nc, ctx, d):
        def sb(name, shape, dt):
            return ctx.enter_context(nc.sbuf_tensor(name, shape, dt))

        self.bank = [ctx.enter_context(nc.psum_tensor(f"bank{i}", [P, 512], F32)) for i in range(8)]
        self.iota_free = sb("iota_free", [P, 512], F32)
        self.iota_half = sb("iota_half", [P, 1024], F16)
        self.iota_part = sb("iota_part", [P, 1], F32)
        self.group_base = sb("group_base", [P, d.NG], F32)
        self.ident = sb("ident", [P, P], F32)
        self.before = sb("before", [P, P], F16)
        self.ones_half = sb("ones_half", [P, P], F16)
        self.ones = sb("ones", [P, P], BF16)
        self.zeros = sb("zeros", [1, BLOCK], BF16)
        self.ones_col = sb("ones_col", [P, 1], F32)
        self.eps_col = sb("eps_col", [P, 1], F32)
        self.key_src = sb("key_src", [P, d.NC], F32)
        self.key_dst = sb("key_dst", [P, d.NC], F32)
        self.ev = sb("ev", [P, d.NC], F32)
        self.row_src = sb("row_src", [P, d.NC], I32)
        self.row_dst = sb("row_dst", [P, d.NC], I32)
        self.w_in = sb("w_in", [P, d.NC], F32)
        self.w_alpha = sb("w_alpha", [P, d.NC], F32)
        self.w_mean = sb("w_mean", [P, d.NC], F32)
        self.w_gcn = sb("w_gcn", [P, d.NC], F32)
        self.records = sb("records", [P, d.NC, 4], F32)
        self.s_key = sb("s_key", [P, d.NC], F32)
        self.s_row = sb("s_row", [P, d.NC], I32)
        self.s_ev = sb("s_ev", [P, d.NC], F32)
        self.s_ev_parts = sb("s_ev_parts", [P, d.NC, 3], BF16)
        self.end_dst = sb("end_dst", [1, d.NG], I32)
        self.end_src = sb("end_src", [1, d.NG], I32)
        self.start = sb("start", [1, 2, d.NB], F32)
        self.regular = sb("regular", [1, 1], I32)
        self.b_key, self.b_row = sb("b_key", [P, d.NQ], F32), sb("b_row", [P, d.NQ], I32)
        self.b_gcn, self.b_alpha, self.b_mean = (sb(n, [P, d.NQ], F32) for n in ("b_gcn", "b_alpha", "b_mean"))
        self.bs_key, self.bs_row, self.bs_ev = sb("bs_key", [P, d.NQ], F32), sb("bs_row", [P, d.NQ], I32), sb("bs_ev", [P, d.NQ], F32)
        self.bs_ev_parts = sb("bs_ev_parts", [P, d.NQ, 3], BF16)
        self.w0 = sb("w0", [P, D], F32)
        self.w1 = sb("w1", [P, D], F32)
        self.w2s = sb("w2s", [P, D], F32)
        self.w2n = sb("w2n", [P, D], F32)
        self.w3s = sb("w3s", [P, D], F32)
        self.w3n = sb("w3n", [P, D], F32)
        self.b0 = sb("b0", [3, PER * D], BF16)
        self.b1 = sb("b1", [3, D], F32)
        self.b2 = sb("b2", [3, PER * D], BF16)
        self.b3 = sb("b3", [3, PER * D], BF16)
        self.gamma = sb("gamma", [P, PER, D], F32)
        self.beta = sb("beta", [P, PER, D], F32)


@contextmanager
def semaphores(nc):
    taken = []

    def take(name):
        taken.append(nc.alloc_semaphore(name))
        return taken[-1]

    yield take
    nc.clear_and_free_semaphores(taken)
    nc.all_engine_barrier()


def chain(engine, semaphore):
    count = [0]

    def link(instruction):
        count[0] += 1
        instruction.then_inc(semaphore, 1)
        engine.wait_ge(semaphore, count[0])

    return link


def rows_pieces(d):
    full, rest = divmod(d.E, P)
    out = []
    for k in range(4):
        n = min(max(full - k * d.RB, 0), d.RB)
        if n:
            out.append((k, 0, n, k * d.RB * P, P))
    if rest:
        out.append((full // d.RB, full % d.RB, 1, full * P, rest))
    return out


def phase_constants(nc, d, m):
    with ExitStack() as ctx:
        take = ctx.enter_context(semaphores(nc))

        iota_i = ctx.enter_context(nc.sbuf_tensor("iota_i", [P, 1024], I32))
        part_i = ctx.enter_context(nc.sbuf_tensor("part_i", [P, 1], I32))
        iotas = take("iotas")
        done = take("constants_done")
        block = ctx.enter_context(nc.Block())

        @block.gpsimd
        def _(pool):
            nc.gpsimd.iota(iota_i[:], pattern=[[1, 1024]], base=0, channel_multiplier=0).then_inc(iotas, 1)
            nc.gpsimd.iota(part_i[:], pattern=[[0, 1]], base=0, channel_multiplier=1).then_inc(iotas, 1)

        @block.vector
        def _(dve):
            link = chain(dve, done)
            dve.wait_ge(iotas, 2)
            nc.vector.tensor_copy(m.iota_half[:], iota_i[:])
            nc.vector.tensor_copy(m.iota_part[:], part_i[:])
            nc.vector.memset(m.ones[:], 1.0)
            nc.vector.memset(m.ones_col[:], 1.0)
            nc.vector.memset(m.ones_half[:], 1.0)
            nc.vector.memset(m.zeros[:], 0.0)
            nc.vector.memset(m.eps_col[:], LN_EPS)
            link(nc.vector.tensor_copy(m.iota_free[:], iota_i[:, 0:512]))
            nc.vector.tensor_scalar(m.group_base[:], m.iota_free[:, 0:d.NG], float(GROUP), None, ALU.mult)
            nc.vector.tensor_scalar(m.ident[:], m.iota_free[:, 0:P], m.iota_part[:], None, ALU.is_equal)
            nc.vector.tensor_scalar(m.before[:], m.iota_free[:, 0:P], m.iota_part[:], None, ALU.is_gt)


def phase_weights(nc, d, m, a):
    with ExitStack() as ctx:
        take = ctx.enter_context(semaphores(nc))

        def sb(name, shape, dt):
            return ctx.enter_context(nc.sbuf_tensor(name, shape, dt))

        rel = sb("rel", [P, N_REL, D], F32)
        rel_b = sb("rel_b", [3, N_REL, D], F32)
        bias = sb("bias", [3, 5, D], F32)
        hi = sb("hi", [3, D], BF16)
        mid = sb("mid", [3, D], BF16)
        lo = sb("lo", [3, D], BF16)
        rest = sb("rest", [3, D], F32)
        pick = sb("pick", [3, 3], F32)
        one = sb("one", [3, D], F32)
        loaded = take("weights_loaded")
        step = take("weights_step")
        block = ctx.enter_context(nc.Block())
        singles = [(m.w0, a["L0_gnn_weight"]), (m.w2s, a["L2_gnn_W_self"]), (m.w2n, a["L2_gnn_W_nb"]),
                   (m.w3s, a["L3_gnn_W_self"]), (m.w3n, a["L3_gnn_W_neigh"])]
        biases = ["L0_gnn_bias", "L2_gnn_b_self", "L2_gnn_b_nb", "L3_gnn_b_self", "L3_gnn_b_neigh"]

        n_loads = len(singles) + 1 + 3 + 3 * len(biases) + 2

        @block.sync
        def _(sp):
            for tile, source in singles:
                sp.dma_start(tile[:], source).then_inc(loaded, 16)
            sp.dma_start(rel[:], a["L1_gnn_W"].rearrange("r i o -> i r o")).then_inc(loaded, 16)
            for k in range(3):
                sp.dma_start(rel_b[k:k + 1, :, :], a["L1_gnn_b"].unsqueeze(0)).then_inc(loaded, 16)
                for i, name in enumerate(biases):
                    sp.dma_start(bias[k:k + 1, i, :], a[name].unsqueeze(0)).then_inc(loaded, 16)
            sp.dma_start(m.gamma[:, 0, :], a["L2_gnn_gamma"].partition_broadcast(P)).then_inc(loaded, 16)
            sp.dma_start(m.beta[:, 0, :], a["L2_gnn_beta"].partition_broadcast(P)).then_inc(loaded, 16)

        @block.vector
        def _(dve):
            link = chain(dve, step)
            dve.wait_ge(loaded, 16 * n_loads)
            for j in range(1, PER):
                nc.vector.tensor_copy(m.gamma[:, j, :], m.gamma[:, 0, :])
                nc.vector.tensor_copy(m.beta[:, j, :], m.beta[:, 0, :])
            for width in (4, 2, 1):
                nc.vector.tensor_tensor(rel[:, 0:width, :], rel[:, 0:width, :], rel[:, width:2 * width, :], ALU.add)
                link(nc.vector.tensor_tensor(rel_b[:, 0:width, :], rel_b[:, 0:width, :],
                                             rel_b[:, width:2 * width, :], ALU.add))
            nc.vector.tensor_copy(m.w1[:], rel[:, 0, :])
            nc.vector.tensor_copy(m.b1[:], rel_b[:, 0, :])
            nc.vector.tensor_tensor(bias[:, 1, :], bias[:, 1, :], bias[:, 2, :], ALU.add)
            nc.vector.tensor_tensor(bias[:, 3, :], bias[:, 3, :], bias[:, 4, :], ALU.add)
            for k in range(3):
                last = nc.vector.tensor_scalar(pick[:, k:k + 1], m.iota_part[0:3, :], float(k), None, ALU.is_equal)
            link(last)
            for out, i in ((m.b0, 0), (m.b2, 1), (m.b3, 3)):
                link(nc.vector.tensor_copy(hi[:], bias[:, i, :]))
                link(nc.vector.tensor_tensor(rest[:], bias[:, i, :], hi[:], ALU.subtract))
                link(nc.vector.tensor_copy(mid[:], rest[:]))
                link(nc.vector.tensor_tensor(lo[:], rest[:], mid[:], ALU.subtract))
                link(nc.vector.tensor_scalar(one[:], hi[:], pick[:, 0:1], None, ALU.mult))
                link(nc.vector.scalar_tensor_tensor(one[:], mid[:], pick[:, 1:2], one[:], ALU.mult, ALU.add))
                link(nc.vector.scalar_tensor_tensor(one[:], lo[:], pick[:, 2:3], one[:], ALU.mult, ALU.add))
                for j in range(PER):
                    last = nc.vector.tensor_copy(out[:, j * D:(j + 1) * D], one[:])
                link(last)


def phase_edges(nc, d, m, a):
    with ExitStack() as ctx:
        take = ctx.enter_context(semaphores(nc))

        names = ["src", "dst", "edge_weight"]
        rows = [ctx.enter_context(nc.sbuf_tensor(f"rows_{n}", [P, 4, P], F32 if n == "edge_weight" else I32))
                for n in names]
        rows_f = [ctx.enter_context(nc.sbuf_tensor(f"rowsf_{n}", [P, 4, P], F32)) for n in names[:2]]
        row_f = [ctx.enter_context(nc.sbuf_tensor(f"rowf_{n}", [P, d.NC], F32)) for n in names[:2]]
        filled = take("rows_filled")
        loaded = take("rows_loaded")
        as_float = take("rows_as_float")
        turned = take("rows_turned")
        copied = take("rows_copied")
        masked = take("rows_masked")
        block = ctx.enter_context(nc.Block())
        pieces = rows_pieces(d)

        @block.sync
        def _(sp):
            sp.wait_ge(filled, 1)
            for n, tile in zip(names, rows):
                for k, p0, np_, e0, w in pieces:
                    sp.dma_start(tile[p0:p0 + np_, k, 0:w],
                                 a[n][e0:e0 + (np_ - 1) * P + w].rearrange("(p w) -> p w", w=w)).then_inc(loaded, 16)

        @block.vector
        def _(dve):
            nc.vector.memset(rows[0][:], d.KEY_PAD)
            nc.vector.memset(rows[1][:], d.KEY_PAD)
            nc.vector.memset(rows[2][:], 0.0).then_inc(filled, 1)
            dve.wait_ge(loaded, 16 * 3 * len(pieces))
            nc.vector.tensor_copy(rows_f[0][:], rows[0][:])
            nc.vector.tensor_copy(rows_f[1][:], rows[1][:]).then_inc(as_float, 1)
            dve.wait_ge(turned, 1)
            nc.vector.tensor_copy(m.key_src[:], m.bank[0][:, 0:d.NC])
            nc.vector.tensor_copy(m.key_dst[:], m.bank[1][:, 0:d.NC])
            nc.vector.tensor_copy(m.ev[:], m.bank[2][:, 0:d.NC]).then_inc(copied, 1)
            dve.wait_ge(copied, 1)
            for key, out in ((m.key_src, row_f[0]), (m.key_dst, row_f[1])):
                last = nc.vector.scalar_tensor_tensor(out[:], key[:], float(d.N), key[:], ALU.is_lt, ALU.mult)
            last.then_inc(masked, 1)
            dve.wait_ge(masked, 1)
            nc.vector.tensor_copy(m.row_src[:], row_f[0][:])
            nc.vector.tensor_copy(m.row_dst[:], row_f[1][:])

        @block.tensor
        def _(pe):
            pe.wait_ge(as_float, 1)
            for i, tile in enumerate((rows_f[0], rows_f[1], rows[2])):
                for k in range(4):
                    last = nc.tensor.transpose(m.bank[i][:, k * d.RB:(k + 1) * d.RB], tile[0:d.RB, k, :],
                                               m.ident[0:d.RB, 0:d.RB])
            last.then_inc(turned, 1)


def phase_segments(nc, d, m, a, weights_dram):
    SP, SW = d.SP, d.SW
    with ExitStack() as ctx:
        take = ctx.enter_context(semaphores(nc))

        def sb(name, shape, dt=F32):
            return ctx.enter_context(nc.sbuf_tensor(name, shape, dt))

        def sem(name):
            return take(name)

        dst_i, prev_i, next_i = (sb(n, [SP, SW], I32) for n in ("sg_dst", "sg_prev", "sg_next"))
        ev = sb("sg_ev", [SP, SW])
        same_prev, same_next, ends = sb("same_prev", [SP, SW]), sb("same_next", [SP, SW]), sb("seg_ends", [SP, SW])
        reset = sb("sg_reset", [SP, SW])
        ones = sb("sg_ones", [SP, SW])
        top, ex, work, work2 = sb("sg_top", [SP, SW]), sb("sg_ex", [SP, SW]), sb("sg_work", [SP, SW]), sb("sg_work2", [SP, SW])
        alpha, mean, rsq = sb("sg_alpha", [SP, SW]), sb("sg_mean", [SP, SW]), sb("sg_rsq", [SP, SW])
        cols = sb("sg_cols", [SP, 8])
        carry = sb("sg_carry", [SP, 8])
        whole = sb("sg_whole", [1, 3, SP])
        over = sb("sg_over", [1, 6, SP + 1])
        wrows = sb("wrows", [P, 3, 4, P])
        filled, loaded, step = sem("sg_filled"), sem("sg_loaded"), sem("sg_step")
        col_ready, row_done, row_ready, col_done = sem("sg_col_ready"), sem("sg_row_done"), sem("sg_row_ready"), sem("sg_col_done")
        shifted, expd, rooted, stored = sem("sg_shifted"), sem("sg_exp"), sem("sg_rooted"), sem("sg_stored")
        w_ready, reloaded, turned = sem("sg_w_ready"), sem("sg_reloaded"), sem("sg_turned")
        deg_ready = sem("sg_deg_ready")
        block = ctx.enter_context(nc.Block())
        pieces = rows_pieces(d)
        row_ps = m.bank[0]
        col_ps = m.bank[1]

        @block.sync
        def _(sp):
            dst, E = a["dst"], d.E
            sp.dma_start(dst_i[:], dst.rearrange("(p w) -> p w", w=SW)).then_inc(loaded, 16)
            sp.dma_start(ev[:], a["edge_weight"].rearrange("(p w) -> p w", w=SW)).then_inc(loaded, 16)
            sp.wait_ge(filled, 1)
            sp.dma_start(prev_i[0:1, 1:SW], dst[0:SW - 1].unsqueeze(0)).then_inc(loaded, 16)
            sp.dma_start(prev_i[1:SP, :], dst[SW - 1:E - 1].rearrange("(p w) -> p w", w=SW)).then_inc(loaded, 16)
            sp.dma_start(next_i[0:SP - 1, :], dst[1:E - SW + 1].rearrange("(p w) -> p w", w=SW)).then_inc(loaded, 16)
            sp.dma_start(next_i[SP - 1:SP, 0:SW - 1], dst[E - SW + 1:E].unsqueeze(0)).then_inc(loaded, 16)
            sp.wait_ge(w_ready, 1)
            for i, tile in enumerate((rsq, alpha, mean)):
                sp.dma_start(weights_dram[i, :].rearrange("(p w) -> p w", w=SW), tile[:]).then_inc(stored, 16)
            sp.wait_ge(stored, 48)
            for i in range(3):
                for k, p0, np_, e0, w in pieces:
                    sp.dma_start(wrows[p0:p0 + np_, i, k, 0:w],
                                 weights_dram[i, e0:e0 + (np_ - 1) * P + w].rearrange("(p w) -> p w", w=w)).then_inc(reloaded, 16)

        @block.vector
        def _(dve):
            link = chain(dve, step)
            nc.vector.memset(prev_i[:], -1)
            nc.vector.memset(next_i[:], -1).then_inc(filled, 1)
            nc.vector.memset(wrows[:], 0.0)
            nc.vector.memset(ones[:], 1.0)
            nc.vector.memset(over[:], 0.0)
            dve.wait_ge(loaded, 96)
            nc.vector.tensor_tensor(same_prev[:], dst_i[:], prev_i[:], ALU.is_equal)
            link(nc.vector.tensor_tensor(same_next[:], dst_i[:], next_i[:], ALU.is_equal))
            nc.vector.tensor_scalar(ends[:], same_next[:], -1.0, 1.0, ALU.mult, ALU.add)
            nc.vector.tensor_scalar(reset[:], same_prev[:], -1.0, BIG, ALU.add, ALU.mult)
            nc.vector.tensor_reduce(cols[:, 0:1], same_prev[:], AX.X, ALU.min)
            nc.vector.tensor_reduce(cols[:, 1:2], same_next[:], AX.X, ALU.min).then_inc(col_ready, 2)
            dve.wait_ge(row_done, 2)
            link(nc.vector.tensor_copy(whole[0:1, 0:2, :], row_ps[0:1, 0:2 * SP].rearrange("o (k p) -> o k p", k=2)))
            nc.vector.memset(over[0:1, 0, 0:1], -BIG)
            link(nc.vector.tensor_scalar(whole[0:1, 2, :], whole[0:1, 0, :], -1.0, BIG, ALU.add, ALU.mult))

            def scan(k, out, data0, data1, op0, op1, row0, start, backwards):
                turn = (lambda x: x[:, ::-1]) if backwards else (lambda x: x)
                link(nc.vector.tensor_tensor_scan(turn(out[:]), turn(data0[:]), turn(data1[:]), start, op0, op1))
                last = 0 if backwards else SW - 1
                nc.vector.tensor_copy(cols[:, 2 + k:3 + k], out[:, last:last + 1]).then_inc(col_ready, 1)
                dve.wait_ge(row_done, 3 + k)
                first = 0 if backwards else 1
                nc.vector.tensor_tensor_scan(turn(over[0:1, k, first:first + SP]), turn(row0),
                                             turn(row_ps[0:1, 0:SP]), start, op0, op1).then_inc(row_ready, 1)
                dve.wait_ge(col_done, 1 + k)
                link(nc.vector.tensor_copy(carry[:, k:k + 1], col_ps[0:SP, 0:1]))
                link(nc.vector.tensor_tensor_scan(turn(out[:]), turn(data0[:]), turn(data1[:]),
                                                  carry[:, k:k + 1], op0, op1))

            def total(k, out, inclusive):
                link(nc.vector.tensor_tensor(inclusive[:], inclusive[:], ends[:], ALU.mult))
                scan(k, out, same_next, inclusive, ALU.mult, ALU.add, whole[0:1, 1, :], 0.0, True)

            scan(0, work, reset, ev, ALU.add, ALU.max, whole[0:1, 2, :], -BIG, False)
            total(1, top, work)
            nc.vector.tensor_tensor(ex[:], ev[:], top[:], ALU.subtract).then_inc(shifted, 1)
            scan(2, work, same_prev, ones, ALU.mult, ALU.add, whole[0:1, 0, :], 0.0, False)
            total(3, mean, work)
            link(nc.vector.tensor_copy(work2[:], mean[:]))
            nc.vector.engine_nop().then_inc(deg_ready, 1)
            link(nc.vector.reciprocal(mean[:], work2[:]))
            dve.wait_ge(expd, 1)
            scan(4, work, same_prev, alpha, ALU.mult, ALU.add, whole[0:1, 0, :], 0.0, False)
            total(5, top, work)
            link(nc.vector.reciprocal(top[:], top[:]))
            link(nc.vector.tensor_tensor(alpha[:], alpha[:], top[:], ALU.mult))
            dve.wait_ge(rooted, 1)
            link(nc.vector.reciprocal(rsq[:], rsq[:]))
            nc.vector.engine_nop().then_inc(w_ready, 1)
            dve.wait_ge(turned, 1)
            nc.vector.tensor_copy(m.w_in[:], m.bank[2][:, 0:d.NC])
            nc.vector.tensor_scalar(m.w_alpha[:], m.bank[3][:, 0:d.NC], HALF_SCALE, None, ALU.mult)
            nc.vector.tensor_scalar(m.w_mean[:], m.bank[4][:, 0:d.NC], HALF_SCALE, None, ALU.mult)

        @block.scalar
        def _(act):
            act.wait_ge(shifted, 1)
            nc.scalar.activation(alpha[:], ex[:], ACT.Exp).then_inc(expd, 1)
            act.wait_ge(deg_ready, 1)
            nc.scalar.activation(rsq[:], work2[:], ACT.Sqrt).then_inc(rooted, 1)

        @block.tensor
        def _(pe):
            pe.wait_ge(col_ready, 2)
            nc.tensor.transpose(row_ps[0:1, 0:SP], cols[:, 0:1], m.ident[0:SP, 0:SP])
            nc.tensor.transpose(row_ps[0:1, SP:2 * SP], cols[:, 1:2], m.ident[0:SP, 0:SP]).then_inc(row_done, 2)
            for k in range(6):
                backwards = k % 2
                pe.wait_ge(col_ready, 3 + k)
                nc.tensor.transpose(row_ps[0:1, 0:SP], cols[:, 2 + k:3 + k], m.ident[0:SP, 0:SP]).then_inc(row_done, 1)
                pe.wait_ge(row_ready, 1 + k)
                nc.tensor.transpose(col_ps[0:SP, 0:1], over[0:1, k, backwards:backwards + SP],
                                    m.ident[0:1, 0:1]).then_inc(col_done, 1)
            pe.wait_ge(reloaded, 16 * 3 * len(pieces))
            for i in range(3):
                for k in range(4):
                    last = nc.tensor.transpose(m.bank[2 + i][:, k * d.RB:(k + 1) * d.RB], wrows[0:d.RB, i, k, :],
                                               m.ident[0:d.RB, 0:d.RB])
            last.then_inc(turned, 1)


def phase_histogram(nc, d, m, norm_dram, sorts):
    with ExitStack() as ctx:
        take = ctx.enter_context(semaphores(nc))

        def sb(name, shape, dt):
            return ctx.enter_context(nc.sbuf_tensor(name, shape, dt))

        def sem(name):
            return take(name)

        U = RING
        oh_tile = sb("oh_tile", [P, 2, d.TILES], BF16)
        oh_node = sb("oh_node", [P, 2, P], BF16)
        oh_src = sb("oh_src", [P, 2, d.NG], BF16)
        oh_dst = sb("oh_dst", [P, 2, d.NG], BF16)
        deg = sb("deg", [d.TH, d.KH, P], F32)
        deg_r = sb("deg_r", [d.TH, d.KH, P], F32)
        incl = sb("incl", [P, 2, d.NG], F32)
        incl_i = sb("incl_i", [P, 2, d.NG], I32)
        start_f = sb("start_f", [P, d.NG], F32)
        start_i = sb("start_i", [P, 2, d.NG], I32)
        zeros = sb("h_zeros", [P, d.NG], F32)
        in_block = sb("in_block", [1, 2, d.NB], F32)
        most = sb("most", [1, 1], F32)
        built, used, step = sem("hist_built"), sem("hist_used"), sem("hist_step")
        at_least_one, rooted, table_ready, stored = sem("hist_max"), sem("hist_root"), sem("hist_table"), sem("hist_stored")
        hist = m.bank[0:-(-d.KH // 4)]
        block = ctx.enter_context(nc.Block())

        def hist_ap(k):
            return hist[k // 4][0:d.TH, (k % 4) * P:(k % 4 + 1) * P]

        @block.vector
        def _(dve):
            link = chain(dve, step)
            with dve.Fori(0, d.NC // U) as i:
                for u in range(U):
                    c, s = i * U + u, u % 2
                    col = bass.ds(c, 1)
                    dve.wait_ge(used, c + 1)
                    nc.vector.tensor_scalar(oh_tile[:, s, :], m.iota_half[:, 0:d.TILES], sorts.src_tile[:, col], None, ALU.is_equal)
                    nc.vector.tensor_scalar(oh_node[:, s, :], m.iota_half[:, 0:P], sorts.src_node[:, col], None, ALU.is_equal)
                    nc.vector.tensor_scalar(oh_src[:, s, :], m.iota_half[:, 0:d.NG], sorts.src_group[:, col], None, ALU.is_equal)
                    nc.vector.tensor_scalar(oh_dst[:, s, :], m.iota_half[:, 0:d.NG], sorts.dst_group[:, col], None, ALU.is_equal).then_inc(built, 1)
            dve.wait_ge(used, d.NC + 2)
            for k in range(d.KH):
                last = nc.vector.tensor_scalar(deg[:, k, :], hist_ap(k), 1.0, None, ALU.max)
            last.then_inc(at_least_one, 1)
            link(nc.vector.memset(zeros[:], 0.0))
            for k in range(2):
                last = nc.vector.tensor_tensor_scan(incl[:, k, :], m.bank[2 + k][:, 0:d.NG], zeros[:], 0.0, ALU.add, ALU.add)
            link(last)
            nc.vector.tensor_copy(incl_i[:], incl[:])
            for k in range(2):
                last = nc.vector.tensor_tensor(m.start[0:1, k, :], incl[0:1, k, 0:d.NG:2], m.bank[2 + k][0:1, 0:d.NG:2], ALU.subtract)
            link(last)
            link(nc.vector.tensor_tensor(in_block[:], incl[0:1, :, 1:d.NG:2], m.start[:], ALU.subtract))
            link(nc.vector.tensor_reduce(most[:], in_block[:], AX.XY, ALU.max))
            nc.vector.tensor_scalar(m.regular[:], most[:], float(SPAN * P), None, ALU.is_le)
            link(nc.vector.tensor_tensor(start_f[:], incl[:, 0, :], m.bank[2][:, 0:d.NG], ALU.subtract))
            link(nc.vector.tensor_copy(start_i[:, 0, :], start_f[:]))
            link(nc.vector.tensor_copy(start_i[:, 1, :], start_f[:]))
            nc.vector.tensor_scalar(incl_i[:], incl_i[:], 7, None, ALU.arith_shift_right)
            nc.vector.tensor_scalar(start_i[:, 0, :], start_i[:, 0, :], 7, None, ALU.arith_shift_right)
            link(nc.vector.tensor_scalar(start_i[:, 1, :], start_i[:, 1, :], 127, None, ALU.bitwise_and))
            link(nc.vector.tensor_scalar(start_f[:], start_i[:, 1, :], m.iota_part[:], None, ALU.is_gt))
            nc.vector.tensor_tensor(sorts.earlier[:, 0, :], start_f[:], start_i[:, 0, :], ALU.add)
            nc.vector.tensor_scalar(m.end_src[:], incl_i[0:1, 0, :], float(d.NC - 1), None, ALU.min)
            nc.vector.tensor_scalar(m.end_dst[:], incl_i[0:1, 1, :], float(d.NC - 1), None, ALU.min)
            dve.wait_ge(rooted, 1)
            nc.vector.reciprocal(deg_r[:], deg_r[:]).then_inc(table_ready, 1)

        @block.scalar
        def _(act):
            act.wait_ge(at_least_one, 1)
            nc.scalar.activation(deg_r[:], deg[:], ACT.Sqrt).then_inc(rooted, 1)

        @block.tensor
        def _(pe):
            pe.sem_inc(used, 2)

            for bank in hist:
                nc.tensor.matmul(bank[:], m.zeros[:, 0:P], m.zeros[:], start=True, stop=False)

            def chunk(c, s, first, last_one):
                pe.wait_ge(built, c + 1)
                for k in range(d.KH):
                    ends_bank = k % 4 == 3 or k == d.KH - 1
                    nc.tensor.matmul(hist_ap(k), oh_tile[:, s, k * d.TH:(k + 1) * d.TH], oh_node[:, s, :], start=False,
                                     stop=last_one and ends_bank)
                nc.tensor.matmul(m.bank[2][:, 0:d.NG], m.ones[:], oh_src[:, s, :], start=first, stop=last_one)
                nc.tensor.matmul(m.bank[3][:, 0:d.NG], m.ones[:], oh_dst[:, s, :], start=first, stop=last_one).then_inc(used, 1)

            chunk(0, 0, True, False)
            chunk(1, 1, False, False)
            with pe.Fori(1, d.NC // 2 - 1) as i:
                for u in range(2):
                    chunk(i * 2 + u, u, False, False)
            chunk(d.NC - 2, 0, False, False)
            chunk(d.NC - 1, 1, False, True)

        @block.sync
        def _(sp):
            sp.wait_ge(table_ready, 1)
            sp.dma_start(norm_dram.rearrange("(k r l) o -> r k (l o)", k=d.KH, l=P), deg_r[:]).then_inc(stored, 16)
            sp.wait_ge(stored, 16)


class Sorts:

    def __init__(self, nc, ctx, d):
        def sb(name, shape, dt=F32):
            return ctx.enter_context(nc.sbuf_tensor(name, shape, dt))

        self.src_tile, self.src_node = sb("src_tile", [P, d.NC]), sb("src_node", [P, d.NC])
        self.src_group, self.dst_group = sb("src_group", [P, d.NC]), sb("dst_group", [P, d.NC])
        self.earlier = sb("earlier", [P, 4, d.NG], F16)
        self.place = sb("place", [P, d.NC])
        self.place_i = sb("place_i", [P, 2, d.NC], I32)
        self.target = sb("target", [P, d.NC], I32)
        self.cut = sb("cut_i", [P, 5, d.NC], I32)


def phase_digits(nc, d, m, s):
    with ExitStack() as ctx:
        take = ctx.enter_context(semaphores(nc))

        step = take("digits_step")
        block = ctx.enter_context(nc.Block())

        @block.vector
        def _(dve):
            link = chain(dve, step)
            for k, key in enumerate((m.key_src, m.key_src, m.key_src, m.key_dst)):
                last = nc.vector.tensor_copy(s.cut[:, k, :], key[:])
            link(last)
            nc.vector.tensor_scalar(s.cut[:, 0, :], s.cut[:, 0, :], 7, None, ALU.arith_shift_right)
            nc.vector.tensor_scalar(s.cut[:, 1, :], s.cut[:, 1, :], 127, None, ALU.bitwise_and)
            nc.vector.tensor_scalar(s.cut[:, 2, :], s.cut[:, 2, :], 8, None, ALU.arith_shift_right)
            link(nc.vector.tensor_scalar(s.cut[:, 3, :], s.cut[:, 3, :], 8, None, ALU.arith_shift_right))
            for k, out in enumerate((s.src_tile, s.src_node, s.src_group, s.dst_group)):
                nc.vector.tensor_copy(out[:], s.cut[:, k, :])
            nc.vector.tensor_copy(m.records[:, :, 0], m.row_dst[:])
            nc.vector.tensor_copy(m.records[:, :, 1], m.key_src[:])
            nc.vector.tensor_copy(m.records[:, :, 2], m.ev[:])
            nc.vector.tensor_copy(m.records[:, :, 3], m.ev[:])


def phase_rank(nc, d, m, s, norm_dram):
    with ExitStack() as ctx:
        take = ctx.enter_context(semaphores(nc))

        def sb(name, shape, dt):
            return ctx.enter_context(nc.sbuf_tensor(name, shape, dt))

        def sem(name):
            return take(name)

        one_hot = sb("rank_hot", [P, 4, d.NG], F16)
        unused = sb("rank_unused", [P, 4, d.NG], BF16)
        index = sb("norm_index", [P, RING], I32)
        norms = sb("norm_rows", [P, RING], F32)
        norm_out = sb("norm_out", [P, d.NC], F32)
        hot_built, ranked, read = sem("rank_built"), sem("rank_ready"), sem("rank_read")
        index_staged = sem("norm_index_staged")
        past_wait = sem("norm_past_wait")
        gathered = [sem(f"norm_gathered{u}") for u in range(RING)]
        counted, copied, step = sem("rank_counted"), sem("norm_copied"), sem("rank_step")
        block = ctx.enter_context(nc.Block())

        @block.vector
        def _(dve):
            link = chain(dve, step)

            def build(c, slot):
                wait_from(dve, read, c - 3)
                nc.vector.tensor_scalar(one_hot[:, slot, :], m.iota_half[:, 0:d.NG], s.src_group[:, bass.ds(c, 1)], None,
                                        ALU.is_equal).then_inc(hot_built, 1)

            def count(c, slot):
                dve.wait_ge(hot_built, c + 1)
                wait_from(dve, counted, c)
                wait_from(dve, ranked, c - 2)
                nc.vector.tensor_tensor(s.earlier[:, (slot + 1) % 4, :], s.earlier[:, slot, :], one_hot[:, slot, :],
                                        ALU.add).then_inc(counted, 1)

            def extract(c, slot):
                dve.wait_ge(ranked, c + 1)
                wait_from(dve, read, c - 3)
                nc.vector.scalar_tensor_tensor(unused[:, slot, :], m.bank[slot][:, 0:d.NG], 1.0, one_hot[:, slot, :], ALU.mult, ALU.mult,
                                               accum_out=s.place[:, bass.ds(c, 1)]).then_inc(read, 1)

            build(0, 0)
            build(1, 1)
            count(0, 0)
            build(2, 2)
            count(1, 1)
            extract(0, 0)
            for c in (1, 2, 3):
                build(c + 2, (c + 2) % 4)
                count(c + 1, (c + 1) % 4)
                extract(c, c % 4)
            with dve.Fori(1, d.NC // 4 - 1) as i:
                for u in range(4):
                    build(i * 4 + u + 2, (u + 2) % 4)
                    count(i * 4 + u + 1, (u + 1) % 4)
                    extract(i * 4 + u, u)
            for u in range(4):
                c = d.NC - 4 + u
                if u < 2:
                    build(c + 2, u + 2)
                if u < 2:
                    count(c + 1, u + 1)
                extract(c, u)
            dve.wait_ge(read, d.NC)
            nc.vector.tensor_copy(s.place_i[:, 0, :], s.place[:])
            link(nc.vector.tensor_copy(s.place_i[:, 1, :], s.place[:]))
            nc.vector.tensor_scalar(s.place_i[:, 0, :], s.place_i[:, 0, :], 7, None, ALU.arith_shift_right)
            link(nc.vector.tensor_scalar(s.place_i[:, 1, :], s.place_i[:, 1, :], 127, None, ALU.bitwise_and))
            link(nc.vector.scalar_tensor_tensor(s.target[:], s.place_i[:, 1, :], float(d.NC), s.place_i[:, 0, :], ALU.mult, ALU.add))
            dve.wait_ge(copied, d.NC // RING)
            nc.vector.tensor_tensor(m.w_gcn[:], norm_out[:], m.w_in[:], ALU.mult)

        @block.tensor
        def _(pe):
            def chunk(c, slot):
                pe.wait_ge(hot_built, c + 1)
                wait_from(pe, counted, c)
                wait_from(pe, read, c - 3)
                nc.tensor.matmul(m.bank[slot][:, 0:d.NG], m.before[:], one_hot[:, slot, :], start=True, stop=False)
                nc.tensor.matmul(m.bank[slot][:, 0:d.NG], m.ones_half[:], s.earlier[:, slot, :], start=False,
                                 stop=True).then_inc(ranked, 1)

            for c in range(4):
                chunk(c, c)
            with pe.Fori(1, d.NC // 4) as i:
                for u in range(4):
                    chunk(i * 4 + u, u)

        @block.gpsimd
        def _(pool):
            with pool.Fori(0, d.NC // RING) as i:
                nc.gpsimd.tensor_copy(index[:], m.row_src[:, bass.ds(i * RING, RING)]).then_inc(index_staged, 1)
                pool.wait_ge(index_staged, i + 1)
                pool.sem_inc(past_wait, 1)
                for u in range(RING):
                    nc.gpsimd.indirect_dma_start(
                        out=norms[:, u:u + 1], out_offset=None, in_=norm_dram,
                        in_offset=bass.IndirectOffsetOnAxis(ap=index[:, u:u + 1], axis=0)).then_inc(gathered[u], 16)
                for u in range(RING):
                    pool.wait_ge(gathered[u], (i + 1) * 16)
                nc.gpsimd.tensor_copy(norm_out[:, bass.ds(i * RING, RING)], norms[:]).then_inc(copied, 1)
                pool.wait_ge(copied, i + 1)
                pool.sem_inc(past_wait, 1)


def phase_scatter(nc, d, m, s, sorted_dram):
    with ExitStack() as ctx:
        take = ctx.enter_context(semaphores(nc))

        def sb(name, shape, dt):
            return ctx.enter_context(nc.sbuf_tensor(name, shape, dt))

        def sem(name):
            return take(name)

        index = sb("place_index", [P, 2, RING], I32)
        sent = sb("records_sent", [P, 2, RING, 4], F32)
        back = sb("records_back", [P, d.NC, 4], F32)
        rest = sb("ev_rest", [P, d.NC], F32)
        staged, past_wait = sem("record_staged"), sem("record_past_wait")
        scattered = [[sem(f"scattered{h}_{u}") for u in range(RING)] for h in range(2)]
        all_done, loaded, step = sem("scatter_done"), sem("sorted_loaded"), sem("sorted_step")
        block = ctx.enter_context(nc.Block())
        rounds = d.NC // RING

        @block.gpsimd
        def _(pool):
            def send(i, h, k):
                nc.gpsimd.tensor_copy(index[:, h, :], s.target[:, bass.ds(i * RING, RING)])
                nc.gpsimd.tensor_copy(sent[:, h, :, :], m.records[:, bass.ds(i * RING, RING), :]).then_inc(staged, 1)
                pool.wait_ge(staged, i + 1)
                pool.sem_inc(past_wait, 1)
                for u in range(RING):
                    nc.gpsimd.indirect_dma_start(
                        out=sorted_dram, out_offset=bass.IndirectOffsetOnAxis(ap=index[:, h, u:u + 1], axis=0),
                        in_=sent[:, h, u, :], in_offset=None).then_inc(scattered[h][u], 16)

            def landed(h, k):
                for u in range(RING):
                    pool.wait_ge(scattered[h][u], 16 * k)
                pool.sem_inc(past_wait, 1)

            send(0, 0, 1)
            send(1, 1, 1)
            with pool.Fori(1, rounds // 2) as k:
                for h in range(2):
                    landed(h, k)
                    send(k * 2 + h, h, k + 1)
            if rounds % 2:
                landed(0, rounds // 2)
                send(rounds - 1, 0, rounds // 2 + 1)
            landed(0, (rounds + 1) // 2)
            landed(1, rounds // 2)
            pool.sem_inc(all_done, 1)

        @block.sync
        def _(sp):
            sp.wait_ge(all_done, 1)
            sp.dma_start(back[:], sorted_dram.rearrange("(p c) f -> p c f", c=d.NC)).then_inc(loaded, 16)

        @block.vector
        def _(dve):
            link = chain(dve, step)
            dve.wait_ge(loaded, 16)
            nc.vector.tensor_copy(m.s_row[:], back[:, :, 0])
            nc.vector.tensor_copy(m.s_key[:], back[:, :, 1])
            link(nc.vector.tensor_copy(m.s_ev[:], back[:, :, 2]))
            link(nc.vector.tensor_copy(m.s_ev_parts[:, :, 0], m.s_ev[:]))
            link(nc.vector.tensor_tensor(rest[:], m.s_ev[:], m.s_ev_parts[:, :, 0], ALU.subtract))
            link(nc.vector.tensor_copy(m.s_ev_parts[:, :, 1], rest[:]))
            link(nc.vector.tensor_tensor(m.s_ev_parts[:, :, 2], rest[:], m.s_ev_parts[:, :, 1], ALU.subtract))


def phase_blocks(nc, d, m, starts_dram, flat_dst, flat_src):
    with ExitStack() as ctx:
        take = ctx.enter_context(semaphores(nc))

        def sb(name, shape, dt=F32):
            return ctx.enter_context(nc.sbuf_tensor(name, shape, dt))

        def sem(name):
            return take(name)

        rows_f = sb("rows_float", [P, 2, d.NC])
        rest = sb("bl_rest", [P, d.NQ])
        orders = [(1, flat_dst, [m.key_dst[:], rows_f[:, 0, :], m.w_gcn[:], m.w_alpha[:], m.w_mean[:]],
                   [m.b_key, m.b_row, m.b_gcn, m.b_alpha, m.b_mean]),
                  (0, flat_src, [m.s_key[:], rows_f[:, 1, :], m.s_ev[:]], [m.bs_key, m.bs_row, m.bs_ev])]
        width = SPAN * P
        recs = [sb(f"recs{o}", [d.RB, 4, P, len(f)]) for o, _, f, _ in orders]
        wins = [sb(f"wins{o}", [d.WP, d.WT, width, len(f)]) for o, _, f, _ in orders]
        tails = [sb(f"tails{o}", [1, width, len(f)]) for o, _, f, _ in orders]
        first_f = sb("first_f", [d.WP, 2, d.WT])
        at_f = sb("at_f", [d.WP, 2, d.WT])
        at_i = sb("at_i", [d.WP, 2, d.WT], I32)
        as_float, turned, copied, step = sem("bl_as_float"), sem("bl_turned"), sem("bl_copied"), sem("bl_step")
        starts_out, starts_in, tails_ready, flat_out = sem("bl_starts_out"), sem("bl_starts_in"), sem("bl_tails"), sem("bl_flat_out")
        at_ready, cut, cut_turned, placed = sem("bl_at_ready"), [sem(f"bl_cut{i}") for i in range(2)], sem("bl_cut_turned"), sem("bl_placed")
        block = ctx.enter_context(nc.Block())
        fields = [(o, i, k) for i, (o, _, f, _) in enumerate(orders) for k in range(len(f))]
        cuts = [(o, i, k, j) for o, i, k in fields for j in range(SPAN)]

        @block.sync
        def _(sp):
            sp.dma_start(starts_dram, m.start[0:1, :, :]).then_inc(starts_out, 16)
            sp.wait_ge(starts_out, 16)
            for o in range(2):
                for t in range(d.WT):
                    sp.dma_start(first_f[:, o, t:t + 1],
                                 starts_dram[0, o, t * d.WP:(t + 1) * d.WP].unsqueeze(1)).then_inc(starts_in, 16)
            sp.wait_ge(tails_ready, 1)
            for i, (o, flat, f, _) in enumerate(orders):
                n = len(f)
                sp.dma_start(flat[d.EP * n:(d.EP + width) * n].unsqueeze(0), tails[i][:].rearrange("o e f -> o (e f)")).then_inc(flat_out, 16)
            for i, (o, flat, f, _) in enumerate(orders):
                sp.wait_ge(copied, len(fields) if i else len(orders[0][2]))
                n = len(f)
                sp.dma_start(flat[0:d.EP * n].rearrange("(k r w) -> r k w", k=4, r=d.RB),
                             recs[i][:].rearrange("r k e f -> r k (e f)")).then_inc(flat_out, 16)

        @block.vector
        def _(dve):
            link = chain(dve, step)
            nc.vector.tensor_copy(rows_f[:, 0, :], m.row_src[:])
            nc.vector.tensor_copy(rows_f[:, 1, :], m.s_row[:]).then_inc(as_float, 1)
            for i, (o, _, f, _) in enumerate(orders):
                link(nc.vector.memset(tails[i][:], 0.0))
                link(nc.vector.memset(tails[i][:, :, 0], -1.0))
            nc.vector.engine_nop().then_inc(tails_ready, 1)
            dve.wait_ge(starts_in, 32 * d.WT)
            for i, (o, _, f, _) in enumerate(orders):
                last = nc.vector.tensor_scalar(at_f[:, o, :], first_f[:, o, :], float(len(f)), None, ALU.mult)
            link(last)
            nc.vector.tensor_copy(at_i[:], at_f[:]).then_inc(at_ready, 1)
            for x, (o, i, k) in enumerate(fields):
                dve.wait_ge(turned, x + 1)
                nc.vector.tensor_copy(recs[i][:, :, :, k], m.bank[x % 4][0:d.RB, :].rearrange("r (k e) -> r k e", k=4)).then_inc(copied, 1)
            for x, (o, i, k, j) in enumerate(cuts):
                out = orders[i][3][k][:, j:d.NQ:SPAN]
                dve.wait_ge(cut_turned, x + 1)
                if k == 0:
                    last = nc.vector.tensor_tensor(out, m.bank[4 + x % 4][:, 0:d.NB], m.group_base[:, 0:d.NG:2], ALU.subtract)
                else:
                    last = nc.vector.tensor_copy(out, m.bank[4 + x % 4][:, 0:d.NB])
                last.then_inc(placed, 1)
            dve.wait_ge(placed, len(cuts))
            link(nc.vector.tensor_copy(m.bs_ev_parts[:, :, 0], m.bs_ev[:]))
            link(nc.vector.tensor_tensor(rest[:], m.bs_ev[:], m.bs_ev_parts[:, :, 0], ALU.subtract))
            link(nc.vector.tensor_copy(m.bs_ev_parts[:, :, 1], rest[:]))
            link(nc.vector.tensor_tensor(m.bs_ev_parts[:, :, 2], rest[:], m.bs_ev_parts[:, :, 1], ALU.subtract))

        @block.tensor
        def _(pe):
            pe.wait_ge(as_float, 1)
            for x, (o, i, k) in enumerate(fields):
                wait_from(pe, copied, x - 3)
                for q in range(4):
                    last = nc.tensor.transpose(m.bank[x % 4][0:d.RB, q * P:(q + 1) * P],
                                               orders[i][2][k][:, q * d.RB:(q + 1) * d.RB], m.ident[:])
                last.then_inc(turned, 1)
            for x, (o, i, k, j) in enumerate(cuts):
                pe.wait_ge(cut[i], 16 * d.WT)
                wait_from(pe, placed, x - 3)
                for t in range(d.WT):
                    last = nc.tensor.transpose(m.bank[4 + x % 4][:, t * d.WP:(t + 1) * d.WP],
                                               wins[i][:, t, j * P:(j + 1) * P, k], m.ident[0:d.WP, 0:d.WP])
                last.then_inc(cut_turned, 1)

        @block.gpsimd
        def _(pool):
            pool.wait_ge(at_ready, 1)
            pool.wait_ge(flat_out, 64)
            for i, (o, flat, f, _) in enumerate(orders):
                for t in range(d.WT):
                    nc.gpsimd.indirect_dma_start(
                        out=wins[i][:, t, :, :].rearrange("p e f -> p (e f)"), out_offset=None, in_=flat.unsqueeze(1),
                        in_offset=bass.IndirectOffsetOnAxis(ap=at_i[:, o, t:t + 1], axis=0)).then_inc(cut[i], 16)


GCN, REL, ATT, SAGE = "gcn", "rel", "att", "sage"


class At:

    def __init__(self, k, u, lag=0):
        self.k = k + (u - lag) // SLOTS
        self.u = (u - lag) % SLOTS
        self.b = self.k * SLOTS + self.u
        self.pair = self.u % 2


def over_blocks(engine, d, lags, body):
    first = -(-lags // SLOTS) + 1
    def known(step):
        def at(lag):
            here = At(step // SLOTS, step % SLOTS, lag)
            return here if 0 <= here.b < d.NB else None
        body(at)

    for step in range(first * SLOTS):
        known(step)
    with engine.Fori(first, d.NB // SLOTS - 1) as k:
        for u in range(SLOTS):
            body(lambda lag: At(k, u, lag))
    for step in range(d.NB - SLOTS, d.NB + lags):
        known(step)


def wait_from(engine, semaphore, value):
    if not isinstance(value, int) or value > 0:
        engine.wait_ge(semaphore, value)


def phase_layer(nc, d, m, kind, x_in, x_out, rows_out, row, key, weight, ends, b_row, b_key, b_weight):
    att, transposed = kind == ATT, kind in (ATT, SAGE)
    n_sums = 2 if kind in (ATT, SAGE) else 3
    part_type = F16 if n_sums == 2 else BF16
    unscale = 1.0 / HALF_SCALE if n_sums == 2 else 1.0
    n_parts = 4 if kind == REL else n_sums
    node_lag = 3
    length_lag, variance_lag, factor_lag = 4, 5, 6
    stats_lag = 7 if att else 3
    root_lag = stats_lag + 1
    scale_lag = root_lag + 1
    norm_lag = scale_lag + 1
    out_lag = norm_lag + 1
    with ExitStack() as ctx:
        take = ctx.enter_context(semaphores(nc))

        def sb(name, shape, dt=F32):
            return ctx.enter_context(nc.sbuf_tensor(f"{kind}_{name}", shape, dt))

        def sem(name):
            return take(f"{kind}_{name}")

        index = sb("index", [P, RING], I32)
        raw = sb("raw", [P, RING, D])
        parts = sb("parts", [P, RING * n_parts, D], part_type)
        resid = sb("resid", [P, RING, D]) if n_sums == 3 else None
        hot = sb("hot", [P, RING, GROUP], part_type)
        b_index = sb("b_index", [P, SLOTS * SPAN], I32)
        b_raw = sb("b_raw", [P, SLOTS * SPAN, D])
        b_hot = sb("b_hot", [P, 2 * SPAN, BLOCK])
        b_ones = sb("b_ones", [P, 2 * SPAN, BLOCK], BF16) if kind == REL else None
        x = sb("x", [P, SLOTS, PER, D])
        agg = sb("agg", [P, 2, BLOCK])
        xt = sb("xt", [P, 2, BLOCK])
        y = sb("y", [P, SLOTS, PER, D])
        out = sb("out", [P, SLOTS, PER, D])
        stats = sb("stats", [P, SLOTS, PER, 6])
        moments = sb("moments", [P, SLOTS, PER, 2])
        root = sb("root", [P, SLOTS, PER])
        scale = sb("scale", [P, SLOTS, PER])
        shift = sb("shift", [P, SLOTS, PER])
        ev_sum = sb("ev_sum", [3, 2, BLOCK]) if kind == REL else None
        if att:
            square = sb("square", [P, 2, BLOCK])
            own = sb("own", [P, SLOTS, PER, D])
            u_ = sb("u", [P, SLOTS, PER, D])
            t_ = sb("t", [P, SLOTS, PER, D])
            xb = sb("xb", [P, SLOTS, PER, D])
            agg_norm = sb("agg_norm", [P, SLOTS, PER])
            inv = sb("inv", [P, SLOTS, PER])
            moments_u = sb("moments_u", [P, SLOTS, PER, 2])
            mean_sq = sb("mean_sq", [P, SLOTS, PER])
            u_norm = sb("u_norm", [P, SLOTS, PER])
            s_ = sb("s", [P, SLOTS, PER])
            s_sq = sb("s_sq", [P, SLOTS, PER])
            s_var = sb("s_var", [P, SLOTS, PER])
            root_var = sb("root_var", [P, SLOTS, PER])
            k_ = sb("k", [P, SLOTS, PER])
            shift_u = sb("shift_u", [P, SLOTS, PER])
            stats_u = sb("stats_u", [P, SLOTS, PER, 6])

        past_wait, past_dve_wait = sem("past_wait"), sem("past_dve_wait")
        index_staged = sem("index_staged")
        gathered = [sem(f"gathered{u}") for u in range(RING)]
        b_gathered = [sem(f"b_gathered{u}") for u in range(SLOTS * SPAN)]
        b_index_staged, b_hot_built = sem("b_index_staged"), sem("b_hot_built")
        raw_ready, raw_free = sem("raw_ready"), sem("raw_free")
        hi_done, mid_done = sem("hi_done"), sem("mid_done")
        low_done = sem("low_done") if n_sums == 3 else None
        hot_built, pairs_done = sem("hot_built"), sem("pairs_done")
        x_loaded = [sem(f"x_loaded{u}") for u in range(SLOTS)]
        stored = [sem(f"stored{u}") for u in range(SLOTS)]
        agg_summed, agg_copied = sem("agg_summed"), sem("agg_copied")
        x_turned, xt_copied = sem("x_turned"), sem("xt_copied")
        y_ready, summed = sem("y_ready"), sem("summed")
        x_used = sem("x_used") if att else summed
        stats_done, moments_done, rooted, inverted, scaled, normed = (sem(n) for n in (
            "stats_done", "moments_done", "rooted", "inverted", "scaled", "normed"))
        zeroed, step = sem("zeroed"), sem("step")
        if att:
            own_copied = sem("own_copied")
            agg_rooted, mean_ready, u_rooted, s_step = sem("agg_rooted"), sem("mean_ready"), sem("u_rooted"), sem("s_step")
            k_step, var_ready, var_rooted, k_ready, t_ready, t_scaled = (sem(n) for n in (
                "k_step", "var_ready", "var_rooted", "k_ready", "t_ready", "t_scaled"))
        agg_ps = m.bank[0:2]
        y_ps = m.bank[2:4]
        xt_ps = m.bank[4]
        own_ps = m.bank[5:7]
        ev_ps = m.bank[6:8]
        norm_ps = m.bank[7]
        block = ctx.enter_context(nc.Block())

        def slot(c):
            return bass.ds(c % RING, 1)

        def part(c, k):
            return parts[:, bass.ds(c % RING * n_parts + k, 1), :].rearrange("p s f -> p (s f)")

        def flat(ap):
            return ap.rearrange("p j f -> p (j f)")

        @block.gpsimd
        def _(pool):
            half_b = SLOTS // 2

            def gather_blocks(k, h):
                wait_from(pool, agg_summed, (k - 1) * SLOTS + (h + 1) * half_b)
                window = slice(h * half_b * SPAN, (h + 1) * half_b * SPAN)
                nc.gpsimd.tensor_copy(b_index[:, window], b_row[:, bass.ds((k * SLOTS + h * half_b) * SPAN, half_b * SPAN)]).then_inc(
                    b_index_staged, 1)
                pool.wait_ge(b_index_staged, k * 2 + h + 1)
                pool.sem_inc(past_wait, 1)
                for u in range(window.start, window.stop):
                    nc.gpsimd.indirect_dma_start(
                        out=b_raw[:, u, :], out_offset=None, in_=x_in,
                        in_offset=bass.IndirectOffsetOnAxis(ap=b_index[:, u:u + 1], axis=0)).then_inc(b_gathered[u], 16)

            regular = pool.alloc_register(f"{kind}_pool_regular")
            pool.reg_load(regular, m.regular[0:1, 0:1])
            with pool.If(pool.snap(regular) > 0):
                gather_blocks(0, 0)
                gather_blocks(0, 1)
                with pool.Fori(1, d.NB // SLOTS) as k:
                    gather_blocks(k, 0)
                    gather_blocks(k, 1)
            with pool.Else():
                pool.sem_inc(raw_free, RING)
                half = RING // 2

                def gather(i, h):
                    nc.gpsimd.tensor_copy(index[:, h * half:(h + 1) * half],
                                          row[:, bass.ds(i * RING + h * half, half)]).then_inc(index_staged, 1)
                    pool.wait_ge(index_staged, i * 2 + h + 1)
                    for u in range(h * half, (h + 1) * half):
                        pool.wait_ge(raw_free, i * RING + u + 1)
                        pool.sem_inc(past_wait, 1)
                        nc.gpsimd.indirect_dma_start(
                            out=raw[:, u, :], out_offset=None, in_=x_in,
                            in_offset=bass.IndirectOffsetOnAxis(ap=index[:, u:u + 1], axis=0)).then_inc(gathered[u], 16)

                def pass_on(i, h):
                    for u in range(h * half, (h + 1) * half):
                        pool.wait_ge(gathered[u], (i + 1) * 16)
                        pool.sem_inc(raw_ready, 1)

                gather(0, 0)
                gather(0, 1)
                pass_on(0, 0)
                with pool.Fori(1, d.NC // RING) as i:
                    gather(i, 0)
                    pass_on(i - 1, 1)
                    gather(i, 1)
                    pass_on(i, 0)
                pass_on(d.NC // RING - 1, 1)

        @block.sync
        def _(sp):
            def body(at):
                here = at(0)
                if here:
                    wait_from(sp, x_used, here.b - SLOTS + 1)
                    rows = x_in.shape[0]
                    if isinstance(here.b, int) and (here.b + 1) * BLOCK > rows:
                        p = (rows - here.b * BLOCK) // PER
                        sp.dma_start(flat(x[0:p, here.u, :, :]), x_in[here.b * BLOCK:rows, :].rearrange(
                            "(p j) f -> p (j f)", j=PER)).then_inc(x_loaded[here.u], 16)
                    else:
                        sp.dma_start(flat(x[:, here.u, :, :]), x_in[bass.ds(here.b * BLOCK, BLOCK), :].rearrange(
                            "(p j) f -> p (j f)", j=PER)).then_inc(x_loaded[here.u], 16)
                here = at(out_lag)
                if here:
                    sp.wait_ge(normed, here.b + 1)
                    if isinstance(here.b, int) and (here.b + 1) * BLOCK > rows_out:
                        p = (rows_out - here.b * BLOCK) // PER
                        sp.dma_start(x_out[here.b * BLOCK:rows_out, :].rearrange("(p j) f -> p (j f)", j=PER),
                                     flat(out[0:p, here.u, :, :])).then_inc(stored[here.u], 16)
                    else:
                        sp.dma_start(x_out[bass.ds(here.b * BLOCK, BLOCK), :].rearrange("(p j) f -> p (j f)", j=PER),
                                     flat(out[:, here.u, :, :])).then_inc(stored[here.u], 16)

            over_blocks(sp, d, out_lag, body)
            for u in range(SLOTS):
                sp.wait_ge(stored[u], 16 * (d.NB // SLOTS))

        @block.scalar
        def _(act):
            chunk = act.alloc_register(f"{kind}_act_chunk")
            end = [act.alloc_register(f"{kind}_act_end{i}") for i in range(2 * SLOTS)]
            act.reg_mov(chunk, 0)

            def high(c, g):
                act.wait_ge(raw_ready, c + 1)
                act.wait_ge(pairs_done, c + g + 1)
                nc.scalar.activation(part(c, 0), raw[:, slot(c), :].rearrange("p s f -> p (s f)"), ACT.Copy,
                                     scale=weight[:, bass.ds(c, 1)]).then_inc(hi_done, 1)

            def body(at, by_block):
                here = at(0)
                if here and not by_block:
                    if here.u == 0:
                        act.reg_load(end, ends[0:1, bass.ds(here.b * 2, 2 * SLOTS)])
                    for h in range(2):
                        with act.While(lambda: act.snap(chunk) < act.snap(end[here.u * 2 + h])):
                            act.reg_add(chunk, chunk, 1)
                            high(act.snap(chunk), here.b * 2 + h)
                here = at(1)
                if here:
                    q = here.pair
                    if transposed:
                        act.wait_ge(x_turned, here.b + 1)
                        wait_from(act, y_ready, here.b - 1)
                        nc.scalar.copy(xt[:, q, :], xt_ps[:]).then_inc(xt_copied, 1)
                    act.wait_ge(agg_summed, here.b + 1)
                    wait_from(act, y_ready, here.b - 1)
                    if kind == REL:
                        nc.scalar.copy(ev_sum[:, q, :], ev_ps[q][0:3, :])
                    if att:
                        nc.scalar.activation(square[:, q, :], agg_ps[q][:], ACT.Square, scale=unscale)
                    nc.scalar.activation(agg[:, q, :], agg_ps[q][:], ACT.Copy, scale=unscale).then_inc(agg_copied, 1)
                here = at(2)
                if here and att:
                    act.wait_ge(y_ready, here.b + 1)
                    wait_from(act, summed, here.b - SLOTS + 1)
                    nc.scalar.activation(agg_norm[:, here.u, :], norm_ps[:, 0:PER], ACT.Sqrt).then_inc(agg_rooted, 1)
                    nc.scalar.copy(flat(own[:, here.u, :, :]), own_ps[here.pair][:]).then_inc(own_copied, 1)
                here = at(length_lag)
                if here and att:
                    act.wait_ge(mean_ready, here.b + 1)
                    nc.scalar.activation(u_norm[:, here.u, :], mean_sq[:, here.u, :], ACT.Sqrt, scale=float(D)).then_inc(u_rooted, 1)
                here = at(variance_lag)
                if here and att:
                    act.wait_ge(var_ready, here.b + 1)
                    nc.scalar.activation(root_var[:, here.u, :], s_var[:, here.u, :], ACT.Sqrt, bias=m.eps_col[:]).then_inc(var_rooted, 1)
                here = at(factor_lag)
                if here and att:
                    act.wait_ge(k_ready, here.b + 1)
                    for j in range(PER):
                        last = nc.scalar.activation(t_[:, here.u, j, :], u_[:, here.u, j, :], ACT.Identity,
                                                    bias=shift_u[:, here.u, j:j + 1], scale=k_[:, here.u, j:j + 1])
                    last.then_inc(t_ready, 1)
                here = at(root_lag)
                if here:
                    act.wait_ge(moments_done, here.b + 1)
                    nc.scalar.activation(root[:, here.u, :], moments[:, here.u, :, 1], ACT.Sqrt, bias=m.eps_col[:]).then_inc(rooted, 1)
                here = at(norm_lag)
                if here:
                    act.wait_ge(scaled, here.b + 1)
                    wait_from(act, stored[here.u], here.k * 16)
                    for j in range(PER):
                        last = nc.scalar.activation(out[:, here.u, j, :], y[:, here.u, j, :], ACT.Identity,
                                                    bias=shift[:, here.u, j:j + 1], scale=scale[:, here.u, j:j + 1])
                    last.then_inc(normed, 1)

            regular = act.alloc_register(f"{kind}_act_regular")
            act.reg_load(regular, m.regular[0:1, 0:1])
            with act.If(act.snap(regular) > 0):
                over_blocks(act, d, norm_lag, lambda at: body(at, True))
            with act.Else():
                high(0, 0)
                over_blocks(act, d, norm_lag, lambda at: body(at, False))

        @block.vector
        def _(dve):
            chunk = dve.alloc_register(f"{kind}_dve_chunk")
            end = [dve.alloc_register(f"{kind}_dve_end{i}") for i in range(2 * SLOTS)]
            dve.reg_mov(chunk, 0)
            if kind == REL:
                nc.vector.memset(parts[:, 3:RING * n_parts:n_parts, :], 0.0).then_inc(zeroed, 1)
                dve.wait_ge(zeroed, 1)

            def low(c, between=lambda half: None):
                rows = raw[:, slot(c), :].rearrange("p s f -> p (s f)")
                dve.wait_ge(hi_done, c + 1)
                if n_sums == 2:
                    nc.vector.scalar_tensor_tensor(part(c, 1), rows, weight[:, bass.ds(c, 1)], part(c, 0), ALU.mult,
                                                   ALU.subtract).then_inc(raw_free, 1)
                    between(0)
                    between(1)
                    return
                left = resid[:, slot(c), :].rearrange("p s f -> p (s f)")
                nc.vector.scalar_tensor_tensor(left, rows, weight[:, bass.ds(c, 1)], part(c, 0), ALU.mult,
                                               ALU.subtract).then_inc(raw_free, 1)
                if kind == REL:
                    nc.vector.tensor_copy(part(c, 3)[:, 0:3], m.s_ev_parts[:, bass.ds(c, 1), :].rearrange("p c k -> p (c k)"))
                between(0)
                dve.wait_ge(raw_free, c + 1 + RING)
                nc.vector.tensor_copy(part(c, 1), left).then_inc(mid_done, 1)
                between(1)
                dve.wait_ge(mid_done, c + 1)
                nc.vector.tensor_tensor(part(c, 2), left, part(c, 1), ALU.subtract).then_inc(low_done, 1)

            def one_hot(c, g, half):
                to = slice(half * (GROUP // 2), (half + 1) * (GROUP // 2))
                dve.wait_ge(pairs_done, c + g + 1)
                return nc.vector.tensor_scalar(hot[:, slot(c + g), to].rearrange("p s n -> p (s n)"), m.iota_half[:, to],
                                               m.group_base[:, bass.ds(g, 1)], key[:, bass.ds(c, 1)], ALU.add, ALU.is_equal)

            def one_hots(c, g):
                one_hot(c, g, 0)
                one_hot(c, g, 1).then_inc(hot_built, 1)

            def body(at, by_block):
                here, kth, yth = (at(lag) if att else None for lag in (variance_lag, factor_lag, stats_lag))
                if kth:
                    dve.wait_ge(var_rooted, kth.b + 1)
                    nc.vector.reciprocal(k_[:, kth.u, :], root_var[:, kth.u, :]).then_inc(k_step, 1)
                if here:
                    dve.wait_ge(u_rooted, here.b + 1)
                    nc.vector.tensor_scalar(s_[:, here.u, :], u_norm[:, here.u, :], 2.0 * NORM_EPS, None, ALU.add).then_inc(s_step, 1)
                if kth:
                    dve.wait_ge(k_step, kth.b * 2 + 1)
                    nc.vector.tensor_tensor(k_[:, kth.u, :], k_[:, kth.u, :], s_[:, kth.u, :], ALU.mult).then_inc(k_step, 1)
                if here:
                    dve.wait_ge(s_step, here.b * 3 + 1)
                    nc.vector.reciprocal(s_[:, here.u, :], s_[:, here.u, :]).then_inc(s_step, 1)
                if kth:
                    dve.wait_ge(k_step, kth.b * 2 + 2)
                    nc.vector.scalar_tensor_tensor(shift_u[:, kth.u, :], moments_u[:, kth.u, :, 0], -1.0, k_[:, kth.u, :], ALU.mult,
                                                   ALU.mult).then_inc(k_ready, 1)
                if here:
                    dve.wait_ge(s_step, here.b * 3 + 2)
                    nc.vector.tensor_tensor(s_sq[:, here.u, :], s_[:, here.u, :], s_[:, here.u, :], ALU.mult).then_inc(s_step, 1)
                if yth:
                    dve.wait_ge(t_ready, yth.b + 1)
                    nc.vector.tensor_tensor(flat(t_[:, yth.u, :, :]), flat(t_[:, yth.u, :, :]), flat(m.gamma[:]), ALU.mult).then_inc(t_scaled, 1)
                if here:
                    dve.wait_ge(s_step, here.b * 3 + 3)
                    nc.vector.tensor_tensor(s_var[:, here.u, :], s_sq[:, here.u, :], moments_u[:, here.u, :, 1], ALU.mult).then_inc(var_ready, 1)
                if yth:
                    dve.wait_ge(t_scaled, yth.b * 2 + 1)
                    wait_from(dve, normed, yth.b - SLOTS + 1)
                    nc.vector.tensor_tensor(flat(y[:, yth.u, :, :]), flat(t_[:, yth.u, :, :]), flat(xb[:, yth.u, :, :]), ALU.add).then_inc(t_scaled, 1)
                here = at(node_lag)
                if here:
                    dve.wait_ge(y_ready, here.b + 1)
                    dve.wait_ge(x_loaded[here.u], (here.k + 1) * 16)
                if here and att:
                    dve.wait_ge(agg_rooted, here.b + 1)
                    dve.wait_ge(own_copied, here.b + 1)
                    wait_from(dve, t_ready, here.b - SLOTS + 1)
                    wait_from(dve, t_scaled, (here.b - SLOTS) * 2 + 2)
                    nc.vector.tensor_scalar(inv[:, here.u, :], agg_norm[:, here.u, :], NORM_EPS, None, ALU.add).then_inc(step, 1)
                    nc.vector.tensor_tensor(flat(xb[:, here.u, :, :]), flat(x[:, here.u, :, :]), flat(m.beta[:]), ALU.add).then_inc(x_used, 1)
                    dve.wait_ge(step, here.b * 5 + 1)
                    nc.vector.reciprocal(inv[:, here.u, :], inv[:, here.u, :]).then_inc(step, 1)
                    dve.wait_ge(step, here.b * 5 + 2)
                    for j in range(PER):
                        last = nc.vector.scalar_tensor_tensor(u_[:, here.u, j, :], y_ps[here.pair][:, j * D:(j + 1) * D],
                                                              inv[:, here.u, j:j + 1], own[:, here.u, j, :],
                                                              ALU.mult, ALU.add)
                    last.then_inc(summed, 1)
                    dve.wait_ge(summed, here.b + 1)
                    for j in range(PER):
                        last = nc.vector.bn_stats(stats_u[:, here.u, j, :], u_[:, here.u, j, :])
                    last.then_inc(step, 1)
                elif here:
                    wait_from(dve, normed, here.b - SLOTS + 1)
                    if kind == SAGE:
                        nc.vector.tensor_tensor(flat(y[:, here.u, :, :]), y_ps[here.pair][:], flat(x[:, here.u, :, :]),
                                                ALU.add).then_inc(summed, 1)
                    else:
                        nc.vector.scalar_tensor_tensor(flat(y[:, here.u, :, :]), y_ps[here.pair][:], 0.0,
                                                       flat(x[:, here.u, :, :]), ALU.max, ALU.add).then_inc(summed, 1)
                first = at(0)
                if first and by_block:
                    wait_from(dve, agg_summed, first.b - 1)
                    for j in range(SPAN):
                        q = bass.ds(first.b * SPAN + j, 1)
                        if kind == REL:
                            nc.vector.tensor_scalar(b_ones[:, first.pair * SPAN + j, :], m.iota_half[:, 0:BLOCK], b_key[:, q], None,
                                                    ALU.is_equal)
                        nc.vector.tensor_scalar(b_hot[:, first.pair * SPAN + j, :], m.iota_half[:, 0:BLOCK], b_key[:, q], b_weight[:, q],
                                                ALU.is_equal, ALU.mult).then_inc(b_hot_built, 1)
                elif first:
                    if first.u == 0:
                        dve.reg_load(end, ends[0:1, bass.ds(first.b * 2, 2 * SLOTS)])
                    for h in range(2):
                        g = first.b * 2 + h
                        one_hots(dve.snap(chunk), g)
                        with dve.While(lambda: dve.snap(chunk) < dve.snap(end[first.u * 2 + h])):
                            dve.reg_add(chunk, chunk, 1)
                            c = dve.snap(chunk)

                            def between(half):
                                made = one_hot(c, g, half)
                                if half:
                                    made.then_inc(hot_built, 1)

                            low(c, between)
                here = at(node_lag)
                if here and att:
                    dve.wait_ge(step, here.b * 5 + 3)
                    dve.sem_inc(past_dve_wait, 1)
                    for j in range(PER):
                        last = nc.vector.bn_aggr(moments_u[:, here.u, j, :], stats_u[:, here.u, j, :])
                    last.then_inc(step, 1)
                last_one = at(scale_lag)
                if last_one:
                    dve.wait_ge(rooted, last_one.b + 1)
                    nc.vector.reciprocal(scale[:, last_one.u, :], root[:, last_one.u, :]).then_inc(inverted, 1)
                if here and att:
                    dve.wait_ge(step, here.b * 5 + 4)
                    mean, var = moments_u[:, here.u, :, 0], moments_u[:, here.u, :, 1]
                    nc.vector.tensor_tensor(mean_sq[:, here.u, :], mean, mean, ALU.mult).then_inc(step, 1)
                if last_one:
                    dve.wait_ge(inverted, last_one.b + 1)
                    nc.vector.scalar_tensor_tensor(shift[:, last_one.u, :], moments[:, last_one.u, :, 0], -1.0,
                                                   scale[:, last_one.u, :], ALU.mult, ALU.mult).then_inc(scaled, 1)
                if here and att:
                    dve.wait_ge(step, here.b * 5 + 5)
                    nc.vector.tensor_tensor(mean_sq[:, here.u, :], mean_sq[:, here.u, :], var, ALU.add).then_inc(mean_ready, 1)
                here = at(stats_lag)
                if here:
                    if att:
                        dve.wait_ge(t_scaled, here.b * 2 + 2)
                    else:
                        dve.wait_ge(summed, here.b + 1)
                    for j in range(PER):
                        last = nc.vector.bn_stats(stats[:, here.u, j, :], y[:, here.u, j, :])
                    last.then_inc(stats_done, 1)
                    dve.wait_ge(stats_done, here.b + 1)
                    dve.sem_inc(past_dve_wait, 1)
                    for j in range(PER):
                        last = nc.vector.bn_aggr(moments[:, here.u, j, :], stats[:, here.u, j, :])
                    last.then_inc(moments_done, 1)

            regular = dve.alloc_register(f"{kind}_dve_regular")
            dve.reg_load(regular, m.regular[0:1, 0:1])
            with dve.If(dve.snap(regular) > 0):
                over_blocks(dve, d, scale_lag, lambda at: body(at, True))
            with dve.Else():
                low(0)
                over_blocks(dve, d, scale_lag, lambda at: body(at, False))

        @block.tensor
        def _(pe):
            chunk = pe.alloc_register(f"{kind}_pe_chunk")
            end = [pe.alloc_register(f"{kind}_pe_end{i}") for i in range(2 * SLOTS)]
            pe.reg_mov(chunk, 0)
            pe.sem_inc(pairs_done, RING)

            def pair(c, g, h, here, stop):
                window = slice(h * GROUP, (h + 1) * GROUP)
                one_hot = hot[:, slot(c + g), :].rearrange("p s n -> p (s n)")
                pe.wait_ge(hot_built, c + g + 1)
                if n_sums == 3:
                    pe.wait_ge(low_done, c + 1)
                else:
                    pe.wait_ge(raw_free, c + 1 + RING)
                if kind == REL:
                    nc.tensor.matmul(ev_ps[here.pair][:, window], part(c, 3), one_hot, start=False, stop=stop)
                for k in range(n_sums):
                    last = nc.tensor.matmul(agg_ps[here.pair][:, window], part(c, k), one_hot, start=False,
                                            stop=stop and k == n_sums - 1)
                last.then_inc(pairs_done, 1)

            def body(at, by_block):
                here = at(0)
                if here and by_block:
                    wait_from(pe, agg_copied, here.b - 1)
                    for j in range(SPAN):
                        u = here.u * SPAN + j
                        one_hot = b_hot[:, here.pair * SPAN + j, :]
                        pe.wait_ge(b_hot_built, here.b * SPAN + j + 1)
                        pe.wait_ge(b_gathered[u], (here.k + 1) * 16)
                        if kind == REL:
                            nc.tensor.matmul(ev_ps[here.pair][0:3, :], m.bs_ev_parts[:, bass.ds(here.b * SPAN + j, 1), :].rearrange("p q k -> p (q k)"),
                                             b_ones[:, here.pair * SPAN + j, :], start=j == 0, stop=j == SPAN - 1)
                        last = nc.tensor.matmul(agg_ps[here.pair][:], b_raw[:, u, :], one_hot, start=j == 0, stop=j == SPAN - 1)
                    last.then_inc(agg_summed, 1)
                elif here:
                    if here.u == 0:
                        pe.reg_load(end, ends[0:1, bass.ds(here.b * 2, 2 * SLOTS)])
                    wait_from(pe, agg_copied, here.b - 1)
                    for h in range(2):
                        g = here.b * 2 + h
                        for sums in (agg_ps, ev_ps)[:1 + (kind == REL)]:
                            nc.tensor.matmul(sums[here.pair][:, h * GROUP:(h + 1) * GROUP], m.zeros[:, 0:P], m.zeros[:, 0:GROUP],
                                             start=True, stop=False)
                        with pe.While(lambda: pe.snap(chunk) < pe.snap(end[here.u * 2 + h])):
                            pair(pe.snap(chunk), g, h, here, False)
                            pe.reg_add(chunk, chunk, 1)
                        pair(pe.snap(chunk), g, h, here, True)
                    pe.wait_ge(pairs_done, pe.snap(chunk) + (here.b * 2 + 2 + RING))
                    pe.sem_inc(agg_summed, 1)
                if here:
                    if transposed:
                        pe.wait_ge(x_loaded[here.u], (here.k + 1) * 16)
                        wait_from(pe, xt_copied, here.b)
                        for j in range(PER):
                            last = nc.tensor.transpose(xt_ps[:, j * P:(j + 1) * P], x[:, here.u, j, :], m.ident[:])
                        last.then_inc(x_turned, 1)
                here = at(1)
                if here:
                    q = here.pair
                    sums = y_ps[q]
                    pe.wait_ge(agg_copied, here.b + 1)
                    wait_from(pe, summed, here.b - 1)
                    aggT = [agg[:, q, j:BLOCK:PER] for j in range(PER)]
                    xT = [xt[:, q, j * P:(j + 1) * P] for j in range(PER)]
                    if kind == GCN or kind == SAGE:
                        nc.tensor.matmul(sums[:], m.ones[0:3, :], (m.b0 if kind == GCN else m.b3)[:], start=True, stop=False)
                    if att:
                        nc.tensor.matmul(own_ps[q][:], m.ones[0:3, :], m.b2[:], start=True, stop=False)
                    for j in range(PER):
                        window = slice(j * D, (j + 1) * D)
                        if kind == GCN:
                            last = nc.tensor.matmul(sums[:, window], aggT[j], m.w0[:], start=False, stop=j == PER - 1)
                        elif kind == REL:
                            nc.tensor.matmul(sums[:, window], ev_sum[:, q, j:BLOCK:PER], m.b1[:], start=True, stop=False)
                            last = nc.tensor.matmul(sums[:, window], aggT[j], m.w1[:], start=False, stop=True)
                        elif kind == SAGE:
                            nc.tensor.matmul(sums[:, window], xT[j], m.w3s[:], start=False, stop=False)
                            last = nc.tensor.matmul(sums[:, window], aggT[j], m.w3n[:], start=False, stop=j == PER - 1)
                        else:
                            nc.tensor.matmul(own_ps[q][:, window], xT[j], m.w2s[:], start=False, stop=j == PER - 1)
                            last = nc.tensor.matmul(sums[:, window], aggT[j], m.w2n[:], start=True, stop=True)
                    if att:
                        wait_from(pe, agg_rooted, here.b)
                        for j in range(PER):
                            last = nc.tensor.matmul(norm_ps[:, j:j + 1], square[:, q, j:BLOCK:PER], m.ones_col[:], start=True, stop=True)
                    last.then_inc(y_ready, 1)

            regular = pe.alloc_register(f"{kind}_pe_regular")
            pe.reg_load(regular, m.regular[0:1, 0:1])
            with pe.If(pe.snap(regular) > 0):
                over_blocks(pe, d, 1, lambda at: body(at, True))
            with pe.Else():
                over_blocks(pe, d, 1, lambda at: body(at, False))


NAMES = ["x", "src", "dst", "edge_weight", "L0_gnn_weight", "L0_gnn_bias", "L1_gnn_W", "L1_gnn_b", "L2_gnn_W_self",
         "L2_gnn_b_self", "L2_gnn_W_nb", "L2_gnn_b_nb", "L2_gnn_gamma", "L2_gnn_beta", "L3_gnn_W_self",
         "L3_gnn_b_self", "L3_gnn_W_neigh", "L3_gnn_b_neigh"]


def program(nc, *args):
    a = dict(zip(NAMES, args))
    result = args[len(NAMES)]
    d = Dims(a["x"].shape[0], a["src"].shape[0])
    weights_dram = nc.dram_tensor("weights_scratch", [3, d.E], F32).ap()
    norm_dram = nc.dram_tensor("norm_scratch", [d.NP, 1], F32).ap()
    sorted_dram = nc.dram_tensor("sorted_scratch", [d.EP, 4], F32).ap()
    starts_dram = nc.dram_tensor("starts_scratch", [1, 2, d.NB], F32).ap()
    flat_dst = nc.dram_tensor("flat_dst_scratch", [(d.EP + SPAN * P) * 5], F32).ap()
    flat_src = nc.dram_tensor("flat_src_scratch", [(d.EP + SPAN * P) * 3], F32).ap()
    x1 = nc.dram_tensor("x1_scratch", [d.NP, D], F32).ap()
    x2 = nc.dram_tensor("x2_scratch", [d.NP, D], F32).ap()
    with ExitStack() as ctx:
        m = Memory(nc, ctx, d)
        with ExitStack() as prep:
            s = Sorts(nc, prep, d)
            phase_constants(nc, d, m)
            phase_weights(nc, d, m, a)
            phase_edges(nc, d, m, a)
            phase_segments(nc, d, m, a, weights_dram)
            phase_digits(nc, d, m, s)
            phase_histogram(nc, d, m, norm_dram, s)
            phase_rank(nc, d, m, s, norm_dram)
            phase_scatter(nc, d, m, s, sorted_dram)
        phase_blocks(nc, d, m, starts_dram, flat_dst, flat_src)
        by_dst = (m.row_src, m.key_dst)
        phase_layer(nc, d, m, GCN, a["x"], x1, d.NP, *by_dst, m.w_gcn, m.end_dst, m.b_row, m.b_key, m.b_gcn)
        phase_layer(nc, d, m, REL, x1, x2, d.NP, m.s_row, m.s_key, m.s_ev, m.end_src, m.bs_row, m.bs_key, m.bs_ev)
        phase_layer(nc, d, m, ATT, x2, x1, d.NP, *by_dst, m.w_alpha, m.end_dst, m.b_row, m.b_key, m.b_alpha)
        phase_layer(nc, d, m, SAGE, x1, result, d.N, *by_dst, m.w_mean, m.end_dst, m.b_row, m.b_key, m.b_mean)


def kernel(**inputs):
    import numpy as np
    import concourse.bacc as bacc
    from concourse.bass_utils import run_bass_kernel_spmd

    nc = bacc.Bacc("TRN2", target_bir_lowering=False, num_devices=1)
    arrays, args = {}, []
    for name in NAMES:
        value = np.ascontiguousarray(inputs[name])
        arrays[f"in_{name}"] = value
        args.append(nc.dram_tensor(f"in_{name}", value.shape, mybir.dt.from_np(value.dtype), kind="ExternalInput").ap())
    args.append(nc.dram_tensor("out_0", arrays["in_x"].shape, F32, kind="ExternalOutput").ap())
    program(nc, *args)
    results = run_bass_kernel_spmd(nc, [arrays], core_ids=[0])
    return results.results[0]["out_0"]
```

```python
from contextlib import ExitStack, contextmanager

import concourse.bass as bass
from concourse import mybir

F32 = mybir.dt.float32
I32 = mybir.dt.int32
BF16 = mybir.dt.bfloat16
F16 = mybir.dt.float16
ALU = mybir.AluOpType
ACT = mybir.ActivationFunctionType
AX = mybir.AxisListType

P = 128
D = 128
GROUP = 256
BLOCK = 512
PER = BLOCK // P
RING = 8
SLOTS = 4
BIG = 1.0e30
HALF_SCALE = 2048.0
LN_EPS = 1e-5
NORM_EPS = 1e-9
N_REL = 8
SPAN = 3


class Dims:

    def __init__(self, n_nodes, n_edges):
        self.N, self.E = n_nodes, n_edges
        self.NB = -(-(n_nodes + GROUP) // (BLOCK * SLOTS)) * SLOTS
        self.NP = self.NB * BLOCK
        self.NG = self.NP // GROUP
        self.NC = -(-n_edges // (P * RING)) * RING
        self.EP = self.NC * P
        self.KEY_PAD = self.NP - GROUP
        self.RB = self.NC // 4
        self.SP = 125
        self.SW = n_edges // self.SP
        self.KH = -(-self.NG // P)
        self.TH = self.NG // self.KH
        self.LO = 16
        self.HI = -(-self.NG // self.LO)
        self.NQ = self.NB * SPAN
        self.WT = -(-self.NB // P)
        self.WP = self.NB // self.WT
        assert self.WP * self.WT == self.NB
        assert self.KEY_PAD >= n_nodes and self.SP * self.SW == n_edges and self.TH * self.KH == self.NG
        assert self.NC <= 512 and self.NG <= 512 and self.RB <= P and n_nodes % PER == 0


class Memory:

    def __init__(self, nc, ctx, d):
        def sb(name, shape, dt):
            return ctx.enter_context(nc.sbuf_tensor(name, shape, dt))

        self.bank = [ctx.enter_context(nc.psum_tensor(f"bank{i}", [P, 512], F32)) for i in range(8)]
        self.iota_free = sb("iota_free", [P, 512], F32)
        self.iota_half = sb("iota_half", [P, 1024], F16)
        self.iota_part = sb("iota_part", [P, 1], F32)
        self.group_base = sb("group_base", [P, d.NG], F32)
        self.ident = sb("ident", [P, P], F32)
        self.before = sb("before", [P, P], F16)
        self.ones_half = sb("ones_half", [P, P], F16)
        self.ones = sb("ones", [P, P], BF16)
        self.zeros = sb("zeros", [1, BLOCK], BF16)
        self.ones_col = sb("ones_col", [P, 1], F32)
        self.eps_col = sb("eps_col", [P, 1], F32)
        self.eps_length = sb("eps_length", [P, 1], F32)
        self.key_src = sb("key_src", [P, d.NC], F32)
        self.key_dst = sb("key_dst", [P, d.NC], F32)
        self.ev = sb("ev", [P, d.NC], F32)
        self.row_src = sb("row_src", [P, d.NC], I32)
        self.row_dst = sb("row_dst", [P, d.NC], I32)
        self.w_in = sb("w_in", [P, d.NC], F32)
        self.w_alpha = sb("w_alpha", [P, d.NC], F32)
        self.w_mean = sb("w_mean", [P, d.NC], F32)
        self.w_gcn = sb("w_gcn", [P, d.NC], F32)
        self.records = sb("records", [P, d.NC, 4], F32)
        self.s_key = sb("s_key", [P, d.NC], F32)
        self.s_row = sb("s_row", [P, d.NC], I32)
        self.s_ev = sb("s_ev", [P, d.NC], F32)
        self.s_ev_parts = sb("s_ev_parts", [P, d.NC, 3], BF16)
        self.end_dst = sb("end_dst", [1, d.NG], I32)
        self.end_src = sb("end_src", [1, d.NG], I32)
        self.start = sb("start", [1, 2, d.NB], F32)
        self.regular = sb("regular", [1, 1], I32)
        self.b_key, self.b_row = sb("b_key", [P, d.NQ], F32), sb("b_row", [P, d.NQ], I32)
        self.b_gcn, self.b_alpha, self.b_mean = (sb(n, [P, d.NQ], F32) for n in ("b_gcn", "b_alpha", "b_mean"))
        self.bs_key, self.bs_row, self.bs_ev = sb("bs_key", [P, d.NQ], F32), sb("bs_row", [P, d.NQ], I32), sb("bs_ev", [P, d.NQ], F32)
        self.bs_ev_parts = sb("bs_ev_parts", [P, d.NQ, 3], BF16)
        self.w0 = sb("w0", [P, D], F32)
        self.w1 = sb("w1", [P, D], F32)
        self.w2s = sb("w2s", [P, D], F32)
        self.w2n = sb("w2n", [P, D], F32)
        self.w3s = sb("w3s", [P, D], F32)
        self.w3n = sb("w3n", [P, D], F32)
        self.b0 = sb("b0", [3, PER * D], BF16)
        self.b1 = sb("b1", [3, D], F32)
        self.b2 = sb("b2", [3, PER * D], BF16)
        self.b3 = sb("b3", [3, PER * D], BF16)
        self.gamma = sb("gamma", [P, PER, D], F32)
        self.beta = sb("beta", [P, PER, D], F32)


@contextmanager
def semaphores(nc):
    taken = []

    def take(name):
        taken.append(nc.alloc_semaphore(name))
        return taken[-1]

    yield take
    nc.clear_and_free_semaphores(taken)
    nc.all_engine_barrier()


def chain(engine, semaphore):
    count = [0]

    def link(instruction):
        count[0] += 1
        instruction.then_inc(semaphore, 1)
        engine.wait_ge(semaphore, count[0])

    return link


def rows_pieces(d):
    full, rest = divmod(d.E, P)
    out = []
    for k in range(4):
        n = min(max(full - k * d.RB, 0), d.RB)
        if n:
            out.append((k, 0, n, k * d.RB * P, P))
    if rest:
        out.append((full // d.RB, full % d.RB, 1, full * P, rest))
    return out


def phase_constants(nc, d, m):
    with ExitStack() as ctx:
        take = ctx.enter_context(semaphores(nc))

        iota_i = ctx.enter_context(nc.sbuf_tensor("iota_i", [P, 1024], I32))
        part_i = ctx.enter_context(nc.sbuf_tensor("part_i", [P, 1], I32))
        iotas = take("iotas")
        done = take("constants_done")
        block = ctx.enter_context(nc.Block())

        @block.gpsimd
        def _(pool):
            nc.gpsimd.iota(iota_i[:], pattern=[[1, 1024]], base=0, channel_multiplier=0).then_inc(iotas, 1)
            nc.gpsimd.iota(part_i[:], pattern=[[0, 1]], base=0, channel_multiplier=1).then_inc(iotas, 1)

        @block.vector
        def _(dve):
            link = chain(dve, done)
            dve.wait_ge(iotas, 2)
            nc.vector.tensor_copy(m.iota_half[:], iota_i[:])
            nc.vector.tensor_copy(m.iota_part[:], part_i[:])
            nc.vector.memset(m.ones[:], 1.0)
            nc.vector.memset(m.ones_col[:], 1.0)
            nc.vector.memset(m.ones_half[:], 1.0)
            nc.vector.memset(m.zeros[:], 0.0)
            nc.vector.memset(m.eps_col[:], LN_EPS)
            nc.vector.memset(m.eps_length[:], LN_EPS ** 0.5 * 2.0 * NORM_EPS)
            link(nc.vector.tensor_copy(m.iota_free[:], iota_i[:, 0:512]))
            nc.vector.tensor_scalar(m.group_base[:], m.iota_free[:, 0:d.NG], float(GROUP), None, ALU.mult)
            nc.vector.tensor_scalar(m.ident[:], m.iota_free[:, 0:P], m.iota_part[:], None, ALU.is_equal)
            nc.vector.tensor_scalar(m.before[:], m.iota_free[:, 0:P], m.iota_part[:], None, ALU.is_gt)


def phase_weights(nc, d, m, a):
    with ExitStack() as ctx:
        take = ctx.enter_context(semaphores(nc))

        def sb(name, shape, dt):
            return ctx.enter_context(nc.sbuf_tensor(name, shape, dt))

        rel = sb("rel", [P, N_REL, D], F32)
        rel_b = sb("rel_b", [3, N_REL, D], F32)
        bias = sb("bias", [3, 5, D], F32)
        hi = sb("hi", [3, D], BF16)
        mid = sb("mid", [3, D], BF16)
        lo = sb("lo", [3, D], BF16)
        rest = sb("rest", [3, D], F32)
        pick = sb("pick", [3, 3], F32)
        one = sb("one", [3, D], F32)
        loaded = take("weights_loaded")
        step = take("weights_step")
        block = ctx.enter_context(nc.Block())
        singles = [(m.w0, a["L0_gnn_weight"]), (m.w2s, a["L2_gnn_W_self"]), (m.w2n, a["L2_gnn_W_nb"]),
                   (m.w3s, a["L3_gnn_W_self"]), (m.w3n, a["L3_gnn_W_neigh"])]
        biases = ["L0_gnn_bias", "L2_gnn_b_self", "L2_gnn_b_nb", "L3_gnn_b_self", "L3_gnn_b_neigh"]

        n_loads = len(singles) + 1 + 3 + 3 * len(biases) + 2

        @block.sync
        def _(sp):
            for tile, source in singles:
                sp.dma_start(tile[:], source).then_inc(loaded, 16)
            sp.dma_start(rel[:], a["L1_gnn_W"].rearrange("r i o -> i r o")).then_inc(loaded, 16)
            for k in range(3):
                sp.dma_start(rel_b[k:k + 1, :, :], a["L1_gnn_b"].unsqueeze(0)).then_inc(loaded, 16)
                for i, name in enumerate(biases):
                    sp.dma_start(bias[k:k + 1, i, :], a[name].unsqueeze(0)).then_inc(loaded, 16)
            sp.dma_start(m.gamma[:, 0, :], a["L2_gnn_gamma"].partition_broadcast(P)).then_inc(loaded, 16)
            sp.dma_start(m.beta[:, 0, :], a["L2_gnn_beta"].partition_broadcast(P)).then_inc(loaded, 16)

        @block.vector
        def _(dve):
            link = chain(dve, step)
            dve.wait_ge(loaded, 16 * n_loads)
            for j in range(1, PER):
                nc.vector.tensor_copy(m.gamma[:, j, :], m.gamma[:, 0, :])
                nc.vector.tensor_copy(m.beta[:, j, :], m.beta[:, 0, :])
            for width in (4, 2, 1):
                nc.vector.tensor_tensor(rel[:, 0:width, :], rel[:, 0:width, :], rel[:, width:2 * width, :], ALU.add)
                link(nc.vector.tensor_tensor(rel_b[:, 0:width, :], rel_b[:, 0:width, :],
                                             rel_b[:, width:2 * width, :], ALU.add))
            nc.vector.tensor_copy(m.w1[:], rel[:, 0, :])
            nc.vector.tensor_copy(m.b1[:], rel_b[:, 0, :])
            nc.vector.tensor_tensor(bias[:, 1, :], bias[:, 1, :], bias[:, 2, :], ALU.add)
            nc.vector.tensor_tensor(bias[:, 3, :], bias[:, 3, :], bias[:, 4, :], ALU.add)
            for k in range(3):
                last = nc.vector.tensor_scalar(pick[:, k:k + 1], m.iota_part[0:3, :], float(k), None, ALU.is_equal)
            link(last)
            for out, i in ((m.b0, 0), (m.b2, 1), (m.b3, 3)):
                link(nc.vector.tensor_copy(hi[:], bias[:, i, :]))
                link(nc.vector.tensor_tensor(rest[:], bias[:, i, :], hi[:], ALU.subtract))
                link(nc.vector.tensor_copy(mid[:], rest[:]))
                link(nc.vector.tensor_tensor(lo[:], rest[:], mid[:], ALU.subtract))
                link(nc.vector.tensor_scalar(one[:], hi[:], pick[:, 0:1], None, ALU.mult))
                link(nc.vector.scalar_tensor_tensor(one[:], mid[:], pick[:, 1:2], one[:], ALU.mult, ALU.add))
                link(nc.vector.scalar_tensor_tensor(one[:], lo[:], pick[:, 2:3], one[:], ALU.mult, ALU.add))
                for j in range(PER):
                    last = nc.vector.tensor_copy(out[:, j * D:(j + 1) * D], one[:])
                link(last)


def phase_edges(nc, d, m, a):
    with ExitStack() as ctx:
        take = ctx.enter_context(semaphores(nc))

        names = ["src", "dst", "edge_weight"]
        rows = [ctx.enter_context(nc.sbuf_tensor(f"rows_{n}", [P, 4, P], F32 if n == "edge_weight" else I32))
                for n in names]
        rows_f = [ctx.enter_context(nc.sbuf_tensor(f"rowsf_{n}", [P, 4, P], F32)) for n in names[:2]]
        row_f = [ctx.enter_context(nc.sbuf_tensor(f"rowf_{n}", [P, d.NC], F32)) for n in names[:2]]
        filled = take("rows_filled")
        loaded = take("rows_loaded")
        as_float = take("rows_as_float")
        turned = take("rows_turned")
        copied = take("rows_copied")
        masked = take("rows_masked")
        block = ctx.enter_context(nc.Block())
        pieces = rows_pieces(d)

        @block.sync
        def _(sp):
            sp.wait_ge(filled, 1)
            for n, tile in zip(names, rows):
                for k, p0, np_, e0, w in pieces:
                    sp.dma_start(tile[p0:p0 + np_, k, 0:w],
                                 a[n][e0:e0 + (np_ - 1) * P + w].rearrange("(p w) -> p w", w=w)).then_inc(loaded, 16)

        @block.vector
        def _(dve):
            nc.vector.memset(rows[0][:], d.KEY_PAD)
            nc.vector.memset(rows[1][:], d.KEY_PAD)
            nc.vector.memset(rows[2][:], 0.0).then_inc(filled, 1)
            dve.wait_ge(loaded, 16 * 3 * len(pieces))
            nc.vector.tensor_copy(rows_f[0][:], rows[0][:])
            nc.vector.tensor_copy(rows_f[1][:], rows[1][:]).then_inc(as_float, 1)
            dve.wait_ge(turned, 1)
            nc.vector.tensor_copy(m.key_src[:], m.bank[0][:, 0:d.NC])
            nc.vector.tensor_copy(m.key_dst[:], m.bank[1][:, 0:d.NC])
            nc.vector.tensor_copy(m.ev[:], m.bank[2][:, 0:d.NC]).then_inc(copied, 1)
            dve.wait_ge(copied, 1)
            for key, out in ((m.key_src, row_f[0]), (m.key_dst, row_f[1])):
                last = nc.vector.scalar_tensor_tensor(out[:], key[:], float(d.N), key[:], ALU.is_lt, ALU.mult)
            last.then_inc(masked, 1)
            dve.wait_ge(masked, 1)
            nc.vector.tensor_copy(m.row_src[:], row_f[0][:])
            nc.vector.tensor_copy(m.row_dst[:], row_f[1][:])

        @block.tensor
        def _(pe):
            pe.wait_ge(as_float, 1)
            for i, tile in enumerate((rows_f[0], rows_f[1], rows[2])):
                for k in range(4):
                    last = nc.tensor.transpose(m.bank[i][:, k * d.RB:(k + 1) * d.RB], tile[0:d.RB, k, :],
                                               m.ident[0:d.RB, 0:d.RB])
            last.then_inc(turned, 1)


def phase_segments(nc, d, m, a, weights_dram):
    SP, SW = d.SP, d.SW
    with ExitStack() as ctx:
        take = ctx.enter_context(semaphores(nc))

        def sb(name, shape, dt=F32):
            return ctx.enter_context(nc.sbuf_tensor(name, shape, dt))

        def sem(name):
            return take(name)

        dst_i, prev_i, next_i = (sb(n, [SP, SW], I32) for n in ("sg_dst", "sg_prev", "sg_next"))
        ev = sb("sg_ev", [SP, SW])
        same_prev, same_next, ends = sb("same_prev", [SP, SW]), sb("same_next", [SP, SW]), sb("seg_ends", [SP, SW])
        reset = sb("sg_reset", [SP, SW])
        ones = sb("sg_ones", [SP, SW])
        top, ex, work, work2 = sb("sg_top", [SP, SW]), sb("sg_ex", [SP, SW]), sb("sg_work", [SP, SW]), sb("sg_work2", [SP, SW])
        alpha, mean, rsq = sb("sg_alpha", [SP, SW]), sb("sg_mean", [SP, SW]), sb("sg_rsq", [SP, SW])
        cols = sb("sg_cols", [SP, 8])
        carry = sb("sg_carry", [SP, 8])
        whole = sb("sg_whole", [1, 3, SP])
        over = sb("sg_over", [1, 6, SP + 1])
        wrows = sb("wrows", [P, 3, 4, P])
        filled, loaded, step = sem("sg_filled"), sem("sg_loaded"), sem("sg_step")
        col_ready, row_done, row_ready, col_done = sem("sg_col_ready"), sem("sg_row_done"), sem("sg_row_ready"), sem("sg_col_done")
        shifted, expd, rooted, stored = sem("sg_shifted"), sem("sg_exp"), sem("sg_rooted"), sem("sg_stored")
        w_ready, reloaded, turned = sem("sg_w_ready"), sem("sg_reloaded"), sem("sg_turned")
        deg_ready = sem("sg_deg_ready")
        block = ctx.enter_context(nc.Block())
        pieces = rows_pieces(d)
        row_ps = m.bank[0]
        col_ps = m.bank[1]

        @block.sync
        def _(sp):
            dst, E = a["dst"], d.E
            sp.dma_start(dst_i[:], dst.rearrange("(p w) -> p w", w=SW)).then_inc(loaded, 16)
            sp.dma_start(ev[:], a["edge_weight"].rearrange("(p w) -> p w", w=SW)).then_inc(loaded, 16)
            sp.wait_ge(filled, 1)
            sp.dma_start(prev_i[0:1, 1:SW], dst[0:SW - 1].unsqueeze(0)).then_inc(loaded, 16)
            sp.dma_start(prev_i[1:SP, :], dst[SW - 1:E - 1].rearrange("(p w) -> p w", w=SW)).then_inc(loaded, 16)
            sp.dma_start(next_i[0:SP - 1, :], dst[1:E - SW + 1].rearrange("(p w) -> p w", w=SW)).then_inc(loaded, 16)
            sp.dma_start(next_i[SP - 1:SP, 0:SW - 1], dst[E - SW + 1:E].unsqueeze(0)).then_inc(loaded, 16)
            sp.wait_ge(w_ready, 1)
            for i, tile in enumerate((rsq, alpha, mean)):
                sp.dma_start(weights_dram[i, :].rearrange("(p w) -> p w", w=SW), tile[:]).then_inc(stored, 16)
            sp.wait_ge(stored, 48)
            for i in range(3):
                for k, p0, np_, e0, w in pieces:
                    sp.dma_start(wrows[p0:p0 + np_, i, k, 0:w],
                                 weights_dram[i, e0:e0 + (np_ - 1) * P + w].rearrange("(p w) -> p w", w=w)).then_inc(reloaded, 16)

        @block.vector
        def _(dve):
            link = chain(dve, step)
            nc.vector.memset(prev_i[:], -1)
            nc.vector.memset(next_i[:], -1).then_inc(filled, 1)
            nc.vector.memset(wrows[:], 0.0)
            nc.vector.memset(ones[:], 1.0)
            nc.vector.memset(over[:], 0.0)
            dve.wait_ge(loaded, 96)
            nc.vector.tensor_tensor(same_prev[:], dst_i[:], prev_i[:], ALU.is_equal)
            link(nc.vector.tensor_tensor(same_next[:], dst_i[:], next_i[:], ALU.is_equal))
            nc.vector.tensor_scalar(ends[:], same_next[:], -1.0, 1.0, ALU.mult, ALU.add)
            nc.vector.tensor_scalar(reset[:], same_prev[:], -1.0, BIG, ALU.add, ALU.mult)
            nc.vector.tensor_reduce(cols[:, 0:1], same_prev[:], AX.X, ALU.min)
            nc.vector.tensor_reduce(cols[:, 1:2], same_next[:], AX.X, ALU.min).then_inc(col_ready, 2)
            dve.wait_ge(row_done, 2)
            link(nc.vector.tensor_copy(whole[0:1, 0:2, :], row_ps[0:1, 0:2 * SP].rearrange("o (k p) -> o k p", k=2)))
            nc.vector.memset(over[0:1, 0, 0:1], -BIG)
            link(nc.vector.tensor_scalar(whole[0:1, 2, :], whole[0:1, 0, :], -1.0, BIG, ALU.add, ALU.mult))

            def scan(k, out, data0, data1, op0, op1, row0, start, backwards):
                turn = (lambda x: x[:, ::-1]) if backwards else (lambda x: x)
                link(nc.vector.tensor_tensor_scan(turn(out[:]), turn(data0[:]), turn(data1[:]), start, op0, op1))
                last = 0 if backwards else SW - 1
                nc.vector.tensor_copy(cols[:, 2 + k:3 + k], out[:, last:last + 1]).then_inc(col_ready, 1)
                dve.wait_ge(row_done, 3 + k)
                first = 0 if backwards else 1
                nc.vector.tensor_tensor_scan(turn(over[0:1, k, first:first + SP]), turn(row0),
                                             turn(row_ps[0:1, 0:SP]), start, op0, op1).then_inc(row_ready, 1)
                dve.wait_ge(col_done, 1 + k)
                link(nc.vector.tensor_copy(carry[:, k:k + 1], col_ps[0:SP, 0:1]))
                link(nc.vector.tensor_tensor_scan(turn(out[:]), turn(data0[:]), turn(data1[:]),
                                                  carry[:, k:k + 1], op0, op1))

            def total(k, out, inclusive):
                link(nc.vector.tensor_tensor(inclusive[:], inclusive[:], ends[:], ALU.mult))
                scan(k, out, same_next, inclusive, ALU.mult, ALU.add, whole[0:1, 1, :], 0.0, True)

            scan(0, work, reset, ev, ALU.add, ALU.max, whole[0:1, 2, :], -BIG, False)
            total(1, top, work)
            nc.vector.tensor_tensor(ex[:], ev[:], top[:], ALU.subtract).then_inc(shifted, 1)
            scan(2, work, same_prev, ones, ALU.mult, ALU.add, whole[0:1, 0, :], 0.0, False)
            total(3, mean, work)
            link(nc.vector.tensor_copy(work2[:], mean[:]))
            nc.vector.engine_nop().then_inc(deg_ready, 1)
            link(nc.vector.reciprocal(mean[:], work2[:]))
            dve.wait_ge(expd, 1)
            scan(4, work, same_prev, alpha, ALU.mult, ALU.add, whole[0:1, 0, :], 0.0, False)
            total(5, top, work)
            link(nc.vector.reciprocal(top[:], top[:]))
            link(nc.vector.tensor_tensor(alpha[:], alpha[:], top[:], ALU.mult))
            dve.wait_ge(rooted, 1)
            link(nc.vector.reciprocal(rsq[:], rsq[:]))
            nc.vector.engine_nop().then_inc(w_ready, 1)
            dve.wait_ge(turned, 1)
            nc.vector.tensor_copy(m.w_in[:], m.bank[2][:, 0:d.NC])
            nc.vector.tensor_scalar(m.w_alpha[:], m.bank[3][:, 0:d.NC], HALF_SCALE, None, ALU.mult)
            nc.vector.tensor_scalar(m.w_mean[:], m.bank[4][:, 0:d.NC], HALF_SCALE, None, ALU.mult)

        @block.scalar
        def _(act):
            act.wait_ge(shifted, 1)
            nc.scalar.activation(alpha[:], ex[:], ACT.Exp).then_inc(expd, 1)
            act.wait_ge(deg_ready, 1)
            nc.scalar.activation(rsq[:], work2[:], ACT.Sqrt).then_inc(rooted, 1)

        @block.tensor
        def _(pe):
            pe.wait_ge(col_ready, 2)
            nc.tensor.transpose(row_ps[0:1, 0:SP], cols[:, 0:1], m.ident[0:SP, 0:SP])
            nc.tensor.transpose(row_ps[0:1, SP:2 * SP], cols[:, 1:2], m.ident[0:SP, 0:SP]).then_inc(row_done, 2)
            for k in range(6):
                backwards = k % 2
                pe.wait_ge(col_ready, 3 + k)
                nc.tensor.transpose(row_ps[0:1, 0:SP], cols[:, 2 + k:3 + k], m.ident[0:SP, 0:SP]).then_inc(row_done, 1)
                pe.wait_ge(row_ready, 1 + k)
                nc.tensor.transpose(col_ps[0:SP, 0:1], over[0:1, k, backwards:backwards + SP],
                                    m.ident[0:1, 0:1]).then_inc(col_done, 1)
            pe.wait_ge(reloaded, 16 * 3 * len(pieces))
            for i in range(3):
                for k in range(4):
                    last = nc.tensor.transpose(m.bank[2 + i][:, k * d.RB:(k + 1) * d.RB], wrows[0:d.RB, i, k, :],
                                               m.ident[0:d.RB, 0:d.RB])
            last.then_inc(turned, 1)


def phase_histogram(nc, d, m, norm_dram, sorts):
    with ExitStack() as ctx:
        take = ctx.enter_context(semaphores(nc))

        def sb(name, shape, dt):
            return ctx.enter_context(nc.sbuf_tensor(name, shape, dt))

        def sem(name):
            return take(name)

        U = 4
        oh_group = sb("oh_group", [P, U, d.NG], BF16)
        oh_node = sb("oh_node", [P, U, GROUP], BF16)
        oh_hi = sb("oh_hi", [P, 2 * U, d.HI], BF16)
        oh_lo = sb("oh_lo", [P, 2 * U, d.LO], BF16)
        totals = sb("totals", [d.TH, d.KH], F32)
        spread_src = sb("spread_src", [d.TH, d.KH, d.TH], F32)
        dst_table = sb("dst_table", [d.HI, d.LO], F32)
        spread_dst = sb("spread_dst", [d.HI, d.HI, d.LO], F32)
        ones_f = sb("h_ones", [P, P], F32)
        deg = sb("deg", [d.TH, d.KH, GROUP], F32)
        deg_r = sb("deg_r", [d.TH, d.KH, GROUP], F32)
        incl = sb("incl", [P, 2, d.NG], F32)
        incl_i = sb("incl_i", [P, 2, d.NG], I32)
        start_f = sb("start_f", [P, d.NG], F32)
        start_i = sb("start_i", [P, 2, d.NG], I32)
        zeros = sb("h_zeros", [P, d.NG], F32)
        in_block = sb("in_block", [1, 2, d.NB], F32)
        most = sb("most", [1, 1], F32)
        built, used, step = sem("hist_built"), sem("hist_used"), sem("hist_step")
        at_least_one, rooted, table_ready, stored = sem("hist_max"), sem("hist_root"), sem("hist_table"), sem("hist_stored")
        spread, summed = sem("hist_spread"), sem("hist_summed")
        hist = m.bank[0:-(-d.KH // 2)]
        block = ctx.enter_context(nc.Block())

        def hist_ap(k):
            return hist[k // 2][0:d.TH, (k % 2) * GROUP:(k % 2 + 1) * GROUP]

        @block.vector
        def _(dve):
            link = chain(dve, step)
            nc.vector.memset(ones_f[:], 1.0)
            with dve.Fori(0, d.NC // RING) as i:
                for v in range(RING):
                    c, u = i * RING + v, v % U
                    col = bass.ds(c, 1)
                    if u == 0:
                        dve.wait_ge(used, i * RING + v)
                        for hot, digit, n in ((oh_hi, sorts.dst_hi, d.HI), (oh_lo, sorts.dst_lo, d.LO)):
                            nc.vector.tensor_tensor(hot[:, v:v + U, :], m.iota_free[:, 0:n].unsqueeze(1).broadcast_to([P, U, n]),
                                                    digit[:, bass.ds(c, U)].unsqueeze(2).broadcast_to([P, U, n]), ALU.is_equal)
                    dve.wait_ge(used, c + 1)
                    nc.vector.tensor_scalar(oh_group[:, u, :], m.iota_half[:, 0:d.NG], sorts.src_group[:, col], None, ALU.is_equal)
                    nc.vector.tensor_scalar(oh_node[:, u, :], m.iota_half[:, 0:GROUP], sorts.src_node[:, col], None, ALU.is_equal).then_inc(built, 1)
            dve.wait_ge(used, d.NC + U)
            for k in range(d.KH):
                nc.vector.tensor_scalar(deg[:, k, :], hist_ap(k), 1.0, None, ALU.max)
                last = nc.vector.tensor_reduce(totals[:, k:k + 1], hist_ap(k), AX.X, ALU.add)
            last.then_inc(at_least_one, 1)
            dve.wait_ge(at_least_one, 1)
            link(nc.vector.tensor_copy(dst_table[:], m.bank[4][0:d.HI, 0:d.LO]))
            for k in range(d.KH):
                nc.vector.tensor_scalar(spread_src[:, k, :], m.ident[0:d.TH, 0:d.TH], totals[:, k:k + 1], None, ALU.mult)
            for hi in range(d.HI):
                last = nc.vector.tensor_scalar(spread_dst[:, hi, :], dst_table[:], m.ident[0:d.HI, hi:hi + 1], None, ALU.mult)
            last.then_inc(spread, 1)
            link(nc.vector.memset(zeros[:], 0.0))
            dve.wait_ge(summed, 1)
            for k in range(2):
                last = nc.vector.tensor_tensor_scan(incl[:, k, :], m.bank[2 + k][:, 0:d.NG], zeros[:], 0.0, ALU.add, ALU.add)
            link(last)
            nc.vector.tensor_copy(incl_i[:], incl[:])
            for k in range(2):
                last = nc.vector.tensor_tensor(m.start[0:1, k, :], incl[0:1, k, 0:d.NG:2], m.bank[2 + k][0:1, 0:d.NG:2], ALU.subtract)
            link(last)
            link(nc.vector.tensor_tensor(in_block[:], incl[0:1, :, 1:d.NG:2], m.start[:], ALU.subtract))
            link(nc.vector.tensor_reduce(most[:], in_block[:], AX.XY, ALU.max))
            nc.vector.tensor_scalar(m.regular[:], most[:], float(SPAN * P), None, ALU.is_le)
            link(nc.vector.tensor_tensor(start_f[:], incl[:, 0, :], m.bank[2][:, 0:d.NG], ALU.subtract))
            link(nc.vector.tensor_copy(start_i[:, 0, :], start_f[:]))
            link(nc.vector.tensor_copy(start_i[:, 1, :], start_f[:]))
            nc.vector.tensor_scalar(incl_i[:], incl_i[:], 7, None, ALU.arith_shift_right)
            nc.vector.tensor_scalar(start_i[:, 0, :], start_i[:, 0, :], 7, None, ALU.arith_shift_right)
            link(nc.vector.tensor_scalar(start_i[:, 1, :], start_i[:, 1, :], 127, None, ALU.bitwise_and))
            link(nc.vector.tensor_scalar(start_f[:], start_i[:, 1, :], m.iota_part[:], None, ALU.is_gt))
            nc.vector.tensor_tensor(sorts.earlier[:, 0, :], start_f[:], start_i[:, 0, :], ALU.add)
            nc.vector.tensor_scalar(m.end_src[:], incl_i[0:1, 0, :], float(d.NC - 1), None, ALU.min)
            nc.vector.tensor_scalar(m.end_dst[:], incl_i[0:1, 1, :], float(d.NC - 1), None, ALU.min)
            dve.wait_ge(rooted, 1)
            nc.vector.reciprocal(deg_r[:], deg_r[:]).then_inc(table_ready, 1)

        @block.scalar
        def _(act):
            act.wait_ge(at_least_one, 1)
            nc.scalar.activation(deg_r[:], deg[:], ACT.Sqrt).then_inc(rooted, 1)

        @block.tensor
        def _(pe):
            pe.sem_inc(used, U)

            for i, bank in enumerate(hist):
                width = min(d.KH - i * 2, 2) * GROUP
                nc.tensor.matmul(bank[0:d.TH, 0:width], m.zeros[:, 0:d.TH], m.zeros[:, 0:width], start=True, stop=False)

            def chunk(c, v, first, last_one):
                u = v % U
                pe.wait_ge(built, c + 1)
                for k in range(d.KH):
                    ends_bank = k % 2 == 1 or k == d.KH - 1
                    nc.tensor.matmul(hist_ap(k), oh_group[:, u, k * d.TH:(k + 1) * d.TH], oh_node[:, u, :], start=False,
                                     stop=last_one and ends_bank)
                nc.tensor.matmul(m.bank[4][0:d.HI, 0:d.LO], oh_hi[:, v, :], oh_lo[:, v, :], start=first, stop=last_one).then_inc(used, 1)

            for v in range(RING):
                chunk(v, v, v == 0, False)
            with pe.Fori(1, d.NC // RING - 1) as i:
                for v in range(RING):
                    chunk(i * RING + v, v, False, False)
            for v in range(RING):
                chunk(d.NC - RING + v, v, False, v == RING - 1)
            pe.wait_ge(spread, 1)
            nc.tensor.matmul(m.bank[2][:, 0:d.NG], ones_f[0:d.TH, :], spread_src[:].rearrange("r k g -> r (k g)"), start=True, stop=True)
            nc.tensor.matmul(m.bank[3][:, 0:d.NG], ones_f[0:d.HI, :], spread_dst[:].rearrange("r h l -> r (h l)")[:, 0:d.NG],
                             start=True, stop=True).then_inc(summed, 1)

        @block.sync
        def _(sp):
            sp.wait_ge(table_ready, 1)
            sp.dma_start(norm_dram.rearrange("(k r l) o -> r k (l o)", k=d.KH, l=GROUP), deg_r[:]).then_inc(stored, 16)
            sp.wait_ge(stored, 16)


class Sorts:

    def __init__(self, nc, ctx, d):
        def sb(name, shape, dt=F32):
            return ctx.enter_context(nc.sbuf_tensor(name, shape, dt))

        self.src_group, self.src_node = sb("src_group", [P, d.NC]), sb("src_node", [P, d.NC])
        self.dst_hi, self.dst_lo = sb("dst_hi", [P, d.NC]), sb("dst_lo", [P, d.NC])
        self.earlier = sb("earlier", [P, 4, d.NG], F16)
        self.place = sb("place", [P, d.NC])
        self.place_i = sb("place_i", [P, 2, d.NC], I32)
        self.target = sb("target", [P, d.NC], I32)
        self.cut = sb("cut_i", [P, 4, d.NC], I32)


def phase_digits(nc, d, m, s):
    with ExitStack() as ctx:
        take = ctx.enter_context(semaphores(nc))

        step = take("digits_step")
        block = ctx.enter_context(nc.Block())

        @block.vector
        def _(dve):
            link = chain(dve, step)
            for k, key in enumerate((m.key_src, m.key_src, m.key_dst, m.key_dst)):
                last = nc.vector.tensor_copy(s.cut[:, k, :], key[:])
            link(last)
            group_bits, digit_bits = GROUP.bit_length() - 1, d.LO.bit_length() - 1
            nc.vector.tensor_scalar(s.cut[:, 0, :], s.cut[:, 0, :], group_bits, None, ALU.arith_shift_right)
            nc.vector.tensor_scalar(s.cut[:, 1, :], s.cut[:, 1, :], GROUP - 1, None, ALU.bitwise_and)
            nc.vector.tensor_scalar(s.cut[:, 2, :], s.cut[:, 2, :], group_bits + digit_bits, None, ALU.arith_shift_right)
            link(nc.vector.tensor_scalar(s.cut[:, 3, :], s.cut[:, 3, :], group_bits, None, ALU.arith_shift_right))
            link(nc.vector.tensor_scalar(s.cut[:, 3, :], s.cut[:, 3, :], d.LO - 1, None, ALU.bitwise_and))
            for k, out in enumerate((s.src_group, s.src_node, s.dst_hi, s.dst_lo)):
                nc.vector.tensor_copy(out[:], s.cut[:, k, :])
            nc.vector.tensor_copy(m.records[:, :, 0], m.row_dst[:])
            nc.vector.tensor_copy(m.records[:, :, 1], m.key_src[:])
            nc.vector.tensor_copy(m.records[:, :, 2], m.ev[:])
            nc.vector.tensor_copy(m.records[:, :, 3], m.ev[:])


def phase_rank(nc, d, m, s, norm_dram):
    with ExitStack() as ctx:
        take = ctx.enter_context(semaphores(nc))

        def sb(name, shape, dt):
            return ctx.enter_context(nc.sbuf_tensor(name, shape, dt))

        def sem(name):
            return take(name)

        one_hot = sb("rank_hot", [P, 4, d.NG], F16)
        unused = sb("rank_unused", [P, 4, d.NG], BF16)
        index = sb("norm_index", [P, 2, RING], I32)
        norms = sb("norm_rows", [P, 2, RING], F32)
        norm_out = sb("norm_out", [P, d.NC], F32)
        hot_built, ranked, read = sem("rank_built"), sem("rank_ready"), sem("rank_read")
        rounds = d.NC // RING
        index_staged = sem("norm_index_staged")
        past_wait = sem("norm_past_wait")
        gathered = [[sem(f"norm_gathered{h}_{u}") for u in range(RING)] for h in range(2)]
        counted, copied, step = sem("rank_counted"), sem("norm_copied"), sem("rank_step")
        block = ctx.enter_context(nc.Block())

        @block.vector
        def _(dve):
            link = chain(dve, step)

            def build(c, slot):
                wait_from(dve, read, c - 3)
                nc.vector.tensor_scalar(one_hot[:, slot, :], m.iota_half[:, 0:d.NG], s.src_group[:, bass.ds(c, 1)], None,
                                        ALU.is_equal).then_inc(hot_built, 1)

            def count(c, slot):
                dve.wait_ge(hot_built, c + 1)
                wait_from(dve, counted, c)
                wait_from(dve, ranked, c - 2)
                nc.vector.tensor_tensor(s.earlier[:, (slot + 1) % 4, :], s.earlier[:, slot, :], one_hot[:, slot, :],
                                        ALU.add).then_inc(counted, 1)

            def extract(c, slot):
                dve.wait_ge(ranked, c + 1)
                wait_from(dve, read, c - 3)
                nc.vector.scalar_tensor_tensor(unused[:, slot, :], m.bank[slot][:, 0:d.NG], 1.0, one_hot[:, slot, :], ALU.mult, ALU.mult,
                                               accum_out=s.place[:, bass.ds(c, 1)]).then_inc(read, 1)

            build(0, 0)
            build(1, 1)
            count(0, 0)
            build(2, 2)
            count(1, 1)
            extract(0, 0)
            for c in (1, 2, 3):
                build(c + 2, (c + 2) % 4)
                count(c + 1, (c + 1) % 4)
                extract(c, c % 4)
            for c in range(4, RING):
                build(c + 2, (c + 2) % 4)
                count(c + 1, (c + 1) % 4)
                extract(c, c % 4)
            with dve.Fori(1, d.NC // RING - 1) as i:
                for u in range(RING):
                    build(i * RING + u + 2, (u + 2) % 4)
                    count(i * RING + u + 1, (u + 1) % 4)
                    extract(i * RING + u, u % 4)
            for c in range(d.NC - RING, d.NC):
                if c + 2 < d.NC:
                    build(c + 2, (c + 2) % 4)
                    count(c + 1, (c + 1) % 4)
                extract(c, c % 4)
            dve.wait_ge(read, d.NC)
            nc.vector.tensor_copy(s.place_i[:, 0, :], s.place[:])
            link(nc.vector.tensor_copy(s.place_i[:, 1, :], s.place[:]))
            nc.vector.tensor_scalar(s.place_i[:, 0, :], s.place_i[:, 0, :], 7, None, ALU.arith_shift_right)
            link(nc.vector.tensor_scalar(s.place_i[:, 1, :], s.place_i[:, 1, :], 127, None, ALU.bitwise_and))
            link(nc.vector.scalar_tensor_tensor(s.target[:], s.place_i[:, 1, :], float(d.NC), s.place_i[:, 0, :], ALU.mult, ALU.add))
            dve.wait_ge(copied, rounds)
            nc.vector.tensor_tensor(m.w_gcn[:], norm_out[:], m.w_in[:], ALU.mult)

        @block.tensor
        def _(pe):
            def chunk(c, slot):
                pe.wait_ge(hot_built, c + 1)
                wait_from(pe, counted, c)
                wait_from(pe, read, c - 3)
                nc.tensor.matmul(m.bank[slot][:, 0:d.NG], m.before[:], one_hot[:, slot, :], start=True, stop=False)
                nc.tensor.matmul(m.bank[slot][:, 0:d.NG], m.ones_half[:], s.earlier[:, slot, :], start=False,
                                 stop=True).then_inc(ranked, 1)

            for c in range(4):
                chunk(c, c)
            with pe.Fori(1, d.NC // 4) as i:
                for u in range(4):
                    chunk(i * 4 + u, u)

        @block.gpsimd
        def _(pool):
            def gather(i, h):
                wait_from(pool, copied, i - 1)
                nc.gpsimd.tensor_copy(index[:, h, :], m.row_src[:, bass.ds(i * RING, RING)]).then_inc(index_staged, 1)
                pool.wait_ge(index_staged, i + 1)
                pool.sem_inc(past_wait, 1)
                for u in range(RING):
                    nc.gpsimd.indirect_dma_start(
                        out=norms[:, h, u:u + 1], out_offset=None, in_=norm_dram,
                        in_offset=bass.IndirectOffsetOnAxis(ap=index[:, h, u:u + 1], axis=0)).then_inc(gathered[h][u], 16)

            gather(0, 0)
            gather(1, 1)
            with pool.Fori(1, rounds // 2) as k:
                gather(k * 2, 0)
                gather(k * 2 + 1, 1)
            if rounds % 2:
                gather(rounds - 1, 0)

        @block.scalar
        def _(act):
            def take_out(i, h, k):
                for u in range(RING):
                    act.wait_ge(gathered[h][u], k * 16)
                nc.scalar.copy(norm_out[:, bass.ds(i * RING, RING)], norms[:, h, :]).then_inc(copied, 1)

            with act.Fori(0, rounds // 2) as k:
                take_out(k * 2, 0, k + 1)
                take_out(k * 2 + 1, 1, k + 1)
            if rounds % 2:
                take_out(rounds - 1, 0, rounds // 2 + 1)


def phase_scatter(nc, d, m, s, sorted_dram):
    with ExitStack() as ctx:
        take = ctx.enter_context(semaphores(nc))

        def sb(name, shape, dt):
            return ctx.enter_context(nc.sbuf_tensor(name, shape, dt))

        def sem(name):
            return take(name)

        index = sb("place_index", [P, 2, RING], I32)
        sent = sb("records_sent", [P, 2, RING, 4], F32)
        back = sb("records_back", [P, d.NC, 4], F32)
        rest = sb("ev_rest", [P, d.NC], F32)
        staged, past_wait, past_dve_wait = sem("record_staged"), sem("record_past_wait"), sem("record_past_dve_wait")
        scattered = [[sem(f"scattered{h}_{u}") for u in range(RING)] for h in range(2)]
        all_done, loaded, step = sem("scatter_done"), sem("sorted_loaded"), sem("sorted_step")
        block = ctx.enter_context(nc.Block())
        rounds = d.NC // RING

        @block.gpsimd
        def _(pool):
            def send(i, h):
                pool.wait_ge(staged, i + 1)
                pool.sem_inc(past_wait, 1)
                for u in range(RING):
                    nc.gpsimd.indirect_dma_start(
                        out=sorted_dram, out_offset=bass.IndirectOffsetOnAxis(ap=index[:, h, u:u + 1], axis=0),
                        in_=sent[:, h, u, :], in_offset=None).then_inc(scattered[h][u], 16)

            def landed(h, k):
                for u in range(RING):
                    pool.wait_ge(scattered[h][u], 16 * k)
                pool.sem_inc(past_wait, 1)

            with pool.Fori(0, rounds // 2) as k:
                send(k * 2, 0)
                send(k * 2 + 1, 1)
            if rounds % 2:
                send(rounds - 1, 0)
            landed(0, (rounds + 1) // 2)
            landed(1, rounds // 2)
            pool.sem_inc(all_done, 1)

        @block.sync
        def _(sp):
            sp.wait_ge(all_done, 1)
            sp.dma_start(back[:], sorted_dram.rearrange("(p c) f -> p c f", c=d.NC)).then_inc(loaded, 16)

        @block.vector
        def _(dve):
            link = chain(dve, step)

            def stage(i, h):
                nc.vector.tensor_copy(index[:, h, :], s.target[:, bass.ds(i * RING, RING)])
                nc.vector.tensor_copy(sent[:, h, :, :], m.records[:, bass.ds(i * RING, RING), :]).then_inc(staged, 1)

            def stage_again(i, h, k):
                for u in range(RING):
                    dve.wait_ge(scattered[h][u], 16 * k)
                dve.sem_inc(past_dve_wait, 1)
                stage(i, h)

            stage(0, 0)
            stage(1, 1)
            with dve.Fori(1, rounds // 2) as k:
                stage_again(k * 2, 0, k)
                stage_again(k * 2 + 1, 1, k)
            if rounds % 2:
                stage_again(rounds - 1, 0, rounds // 2)
            dve.wait_ge(loaded, 16)
            nc.vector.tensor_copy(m.s_row[:], back[:, :, 0])
            nc.vector.tensor_copy(m.s_key[:], back[:, :, 1])
            link(nc.vector.tensor_copy(m.s_ev[:], back[:, :, 2]))
            link(nc.vector.tensor_copy(m.s_ev_parts[:, :, 0], m.s_ev[:]))
            link(nc.vector.tensor_tensor(rest[:], m.s_ev[:], m.s_ev_parts[:, :, 0], ALU.subtract))
            link(nc.vector.tensor_copy(m.s_ev_parts[:, :, 1], rest[:]))
            link(nc.vector.tensor_tensor(m.s_ev_parts[:, :, 2], rest[:], m.s_ev_parts[:, :, 1], ALU.subtract))


def phase_blocks(nc, d, m, starts_dram, flat_dst, flat_src):
    with ExitStack() as ctx:
        take = ctx.enter_context(semaphores(nc))

        def sb(name, shape, dt=F32):
            return ctx.enter_context(nc.sbuf_tensor(name, shape, dt))

        def sem(name):
            return take(name)

        rows_f = sb("rows_float", [P, 2, d.NC])
        rest = sb("bl_rest", [P, d.NQ])
        orders = [(1, flat_dst, [m.key_dst[:], rows_f[:, 0, :], m.w_gcn[:], m.w_alpha[:], m.w_mean[:]],
                   [m.b_key, m.b_row, m.b_gcn, m.b_alpha, m.b_mean]),
                  (0, flat_src, [m.s_key[:], rows_f[:, 1, :], m.s_ev[:]], [m.bs_key, m.bs_row, m.bs_ev])]
        width = SPAN * P
        recs = [sb(f"recs{o}", [d.RB, 4, P, len(f)]) for o, _, f, _ in orders]
        wins = [sb(f"wins{o}", [d.WP, d.WT, width, len(f)]) for o, _, f, _ in orders]
        tails = [sb(f"tails{o}", [1, width, len(f)]) for o, _, f, _ in orders]
        first_f = sb("first_f", [d.WP, 2, d.WT])
        at_f = sb("at_f", [d.WP, 2, d.WT])
        at_i = sb("at_i", [d.WP, 2, d.WT], I32)
        as_float, turned, copied, step = sem("bl_as_float"), sem("bl_turned"), sem("bl_copied"), sem("bl_step")
        starts_out, starts_in, tails_ready, flat_out = sem("bl_starts_out"), sem("bl_starts_in"), sem("bl_tails"), sem("bl_flat_out")
        at_ready, cut, cut_turned, placed = sem("bl_at_ready"), [sem(f"bl_cut{i}") for i in range(2)], sem("bl_cut_turned"), sem("bl_placed")
        block = ctx.enter_context(nc.Block())
        fields = [(o, i, k) for i, (o, _, f, _) in enumerate(orders) for k in range(len(f))]
        cuts = [(o, i, k, j) for o, i, k in fields for j in range(SPAN)]

        @block.sync
        def _(sp):
            sp.dma_start(starts_dram, m.start[0:1, :, :]).then_inc(starts_out, 16)
            sp.wait_ge(starts_out, 16)
            for o in range(2):
                for t in range(d.WT):
                    sp.dma_start(first_f[:, o, t:t + 1],
                                 starts_dram[0, o, t * d.WP:(t + 1) * d.WP].unsqueeze(1)).then_inc(starts_in, 16)
            sp.wait_ge(tails_ready, 1)
            for i, (o, flat, f, _) in enumerate(orders):
                n = len(f)
                sp.dma_start(flat[d.EP * n:(d.EP + width) * n].unsqueeze(0), tails[i][:].rearrange("o e f -> o (e f)")).then_inc(flat_out, 16)
            for i, (o, flat, f, _) in enumerate(orders):
                sp.wait_ge(copied, len(fields) if i else len(orders[0][2]))
                n = len(f)
                sp.dma_start(flat[0:d.EP * n].rearrange("(k r w) -> r k w", k=4, r=d.RB),
                             recs[i][:].rearrange("r k e f -> r k (e f)")).then_inc(flat_out, 16)

        @block.vector
        def _(dve):
            link = chain(dve, step)
            nc.vector.tensor_copy(rows_f[:, 0, :], m.row_src[:])
            nc.vector.tensor_copy(rows_f[:, 1, :], m.s_row[:]).then_inc(as_float, 1)
            for i, (o, _, f, _) in enumerate(orders):
                link(nc.vector.memset(tails[i][:], 0.0))
                link(nc.vector.memset(tails[i][:, :, 0], -1.0))
            nc.vector.engine_nop().then_inc(tails_ready, 1)
            dve.wait_ge(starts_in, 32 * d.WT)
            for i, (o, _, f, _) in enumerate(orders):
                last = nc.vector.tensor_scalar(at_f[:, o, :], first_f[:, o, :], float(len(f)), None, ALU.mult)
            link(last)
            nc.vector.tensor_copy(at_i[:], at_f[:]).then_inc(at_ready, 1)
            for x, (o, i, k) in enumerate(fields):
                dve.wait_ge(turned, x + 1)
                nc.vector.tensor_copy(recs[i][:, :, :, k], m.bank[x % 4][0:d.RB, :].rearrange("r (k e) -> r k e", k=4)).then_inc(copied, 1)
            for x, (o, i, k, j) in enumerate(cuts):
                out = orders[i][3][k][:, j:d.NQ:SPAN]
                dve.wait_ge(cut_turned, x + 1)
                if k == 0:
                    last = nc.vector.tensor_tensor(out, m.bank[4 + x % 4][:, 0:d.NB], m.group_base[:, 0:d.NG:2], ALU.subtract)
                else:
                    last = nc.vector.tensor_copy(out, m.bank[4 + x % 4][:, 0:d.NB])
                last.then_inc(placed, 1)
            dve.wait_ge(placed, len(cuts))
            link(nc.vector.tensor_copy(m.bs_ev_parts[:, :, 0], m.bs_ev[:]))
            link(nc.vector.tensor_tensor(rest[:], m.bs_ev[:], m.bs_ev_parts[:, :, 0], ALU.subtract))
            link(nc.vector.tensor_copy(m.bs_ev_parts[:, :, 1], rest[:]))
            link(nc.vector.tensor_tensor(m.bs_ev_parts[:, :, 2], rest[:], m.bs_ev_parts[:, :, 1], ALU.subtract))

        @block.tensor
        def _(pe):
            pe.wait_ge(as_float, 1)
            for x, (o, i, k) in enumerate(fields):
                wait_from(pe, copied, x - 3)
                for q in range(4):
                    last = nc.tensor.transpose(m.bank[x % 4][0:d.RB, q * P:(q + 1) * P],
                                               orders[i][2][k][:, q * d.RB:(q + 1) * d.RB], m.ident[:])
                last.then_inc(turned, 1)
            for x, (o, i, k, j) in enumerate(cuts):
                pe.wait_ge(cut[i], 16 * d.WT)
                wait_from(pe, placed, x - 3)
                for t in range(d.WT):
                    last = nc.tensor.transpose(m.bank[4 + x % 4][:, t * d.WP:(t + 1) * d.WP],
                                               wins[i][:, t, j * P:(j + 1) * P, k], m.ident[0:d.WP, 0:d.WP])
                last.then_inc(cut_turned, 1)

        @block.gpsimd
        def _(pool):
            pool.wait_ge(at_ready, 1)
            pool.wait_ge(flat_out, 64)
            for i, (o, flat, f, _) in enumerate(orders):
                for t in range(d.WT):
                    nc.gpsimd.indirect_dma_start(
                        out=wins[i][:, t, :, :].rearrange("p e f -> p (e f)"), out_offset=None, in_=flat.unsqueeze(1),
                        in_offset=bass.IndirectOffsetOnAxis(ap=at_i[:, o, t:t + 1], axis=0)).then_inc(cut[i], 16)


GCN, REL, ATT, SAGE = "gcn", "rel", "att", "sage"


class At:

    def __init__(self, k, u, lag=0):
        self.k = k + (u - lag) // SLOTS
        self.u = (u - lag) % SLOTS
        self.b = self.k * SLOTS + self.u
        self.pair = self.u % 2


def over_blocks(engine, d, lags, body):
    first = -(-lags // SLOTS) + 1
    def known(step):
        def at(lag):
            here = At(step // SLOTS, step % SLOTS, lag)
            return here if 0 <= here.b < d.NB else None
        body(at)

    for step in range(first * SLOTS):
        known(step)
    with engine.Fori(first, d.NB // SLOTS - 1) as k:
        for u in range(SLOTS):
            body(lambda lag: At(k, u, lag))
    for step in range(d.NB - SLOTS, d.NB + lags):
        known(step)


def wait_from(engine, semaphore, value):
    if not isinstance(value, int) or value > 0:
        engine.wait_ge(semaphore, value)


def phase_layer(nc, d, m, kind, x_in, x_out, rows_out, row, key, weight, ends, b_row, b_key, b_weight):
    att, transposed = kind == ATT, kind in (ATT, SAGE)
    n_sums = 2 if kind in (ATT, SAGE) else 3
    part_type = F16 if n_sums == 2 else BF16
    unscale = 1.0 / HALF_SCALE if n_sums == 2 else 1.0
    n_parts = 4 if kind == REL else n_sums
    node_lag = 3
    length_lag, variance_lag, factor_lag = 4, 5, 6
    stats_lag = 8 if att else 3
    beta_lag, gamma_lag = 4, 10
    root_lag = stats_lag + 1
    scale_lag = root_lag + 1
    norm_lag = scale_lag + 1
    out_lag = norm_lag + 1
    with ExitStack() as ctx:
        take = ctx.enter_context(semaphores(nc))

        def sb(name, shape, dt=F32):
            return ctx.enter_context(nc.sbuf_tensor(f"{kind}_{name}", shape, dt))

        def sem(name):
            return take(f"{kind}_{name}")

        index = sb("index", [P, RING], I32)
        raw = sb("raw", [P, RING, D])
        parts = sb("parts", [P, RING * n_parts, D], part_type)
        resid = sb("resid", [P, RING, D]) if n_sums == 3 else None
        hot = sb("hot", [P, RING, GROUP], part_type)
        b_index = sb("b_index", [P, SLOTS * SPAN], I32)
        b_raw = sb("b_raw", [P, SLOTS * SPAN, D])
        b_cut = kind == SAGE
        b_hot = sb("b_hot", [P, 2 * SPAN, BLOCK], F16 if b_cut else F32)
        b_parts = sb("b_parts", [P, SLOTS * SPAN, 2, D], F16) if b_cut else None
        b_ones = sb("b_ones", [P, 2 * SPAN, BLOCK], BF16) if kind == REL else None
        x = sb("x", [P, SLOTS, PER, D])
        agg = sb("agg", [P, 2, BLOCK])
        xt = sb("xt", [P, 2, BLOCK])
        y = sb("y", [P, SLOTS, PER, D])
        out = sb("out", [P, SLOTS, PER, D])
        stats = sb("stats", [P, SLOTS, PER, 6])
        moments = sb("moments", [P, SLOTS, PER, 2])
        root = sb("root", [P, SLOTS, PER])
        scale = sb("scale", [P, SLOTS, PER])
        shift = sb("shift", [P, SLOTS, PER])
        ev_sum = sb("ev_sum", [3, 2, BLOCK]) if kind == REL else None
        if att:
            square = sb("square", [P, 2, BLOCK])
            own = sb("own", [P, SLOTS, PER, D])
            u_ = sb("u", [P, SLOTS, PER, D])
            t_ = sb("t", [P, SLOTS, PER, D])
            xb = sb("xb", [P, 2 * SLOTS, PER * D])
            agg_norm = sb("agg_norm", [P, SLOTS, PER])
            inv = sb("inv", [P, SLOTS, PER])
            moments_u = sb("moments_u", [P, SLOTS, PER, 2])
            mean_sq = sb("mean_sq", [P, SLOTS, PER])
            u_norm = sb("u_norm", [P, SLOTS, PER])
            floor = sb("floor", [P, SLOTS, PER])
            floored_var = sb("floored_var", [P, SLOTS, PER])
            root_var = sb("root_var", [P, SLOTS, PER])
            k_ = sb("k", [P, SLOTS, PER])
            shift_u = sb("shift_u", [P, SLOTS, PER])
            stats_u = sb("stats_u", [P, SLOTS, PER, 6])

        past_wait, past_dve_wait = sem("past_wait"), sem("past_dve_wait")
        index_staged = sem("index_staged")
        gathered = [sem(f"gathered{u}") for u in range(RING)]
        b_gathered = [sem(f"b_gathered{u}") for u in range(SLOTS * SPAN)]
        b_hi_done, b_low_done = sem("b_hi_done"), sem("b_low_done")
        b_index_staged, b_hot_built = sem("b_index_staged"), sem("b_hot_built")
        raw_ready, raw_free = sem("raw_ready"), sem("raw_free")
        hi_done, mid_done = sem("hi_done"), sem("mid_done")
        low_done = sem("low_done") if n_sums == 3 else None
        hot_built, pairs_done = sem("hot_built"), sem("pairs_done")
        x_loaded = [sem(f"x_loaded{u}") for u in range(SLOTS)]
        stored = [sem(f"stored{u}") for u in range(SLOTS)]
        agg_summed, agg_copied = sem("agg_summed"), sem("agg_copied")
        x_turned, xt_copied = sem("x_turned"), sem("xt_copied")
        y_ready, summed = sem("y_ready"), sem("summed")
        x_used = sem("x_used") if att else summed
        stats_done, moments_done, rooted, inverted, scaled, normed = (sem(n) for n in (
            "stats_done", "moments_done", "rooted", "inverted", "scaled", "normed"))
        zeroed, step = sem("zeroed"), sem("step")
        if att:
            own_copied = sem("own_copied")
            agg_rooted, mean_ready, u_rooted, floor_ready = sem("agg_rooted"), sem("mean_ready"), sem("u_rooted"), sem("floor_ready")
            k_inverted, var_ready, var_rooted, k_ready, t_ready, t_scaled, y_made = (sem(n) for n in (
                "k_inverted", "var_ready", "var_rooted", "k_ready", "t_ready", "t_scaled", "y_made"))
        agg_ps = m.bank[0:2]
        y_ps = m.bank[2:4]
        xt_ps = m.bank[4]
        own_ps = m.bank[5:7]
        ev_ps = m.bank[6:8]
        norm_ps = m.bank[7]
        block = ctx.enter_context(nc.Block())

        def slot(c):
            return bass.ds(c % RING, 1)

        def part(c, k):
            return parts[:, bass.ds(c % RING * n_parts + k, 1), :].rearrange("p s f -> p (s f)")

        def flat(ap):
            return ap.rearrange("p j f -> p (j f)")

        def xb_slot(here):
            return xb[:, bass.ds(here.b % (2 * SLOTS), 1), :].rearrange("p s f -> p (s f)")

        def add_beta(engine, maker, here):
            engine.wait_ge(x_loaded[here.u], (here.k + 1) * 16)
            wait_from(engine, y_made, here.b - 2 * SLOTS + 1)
            maker.tensor_tensor(xb_slot(here), flat(x[:, here.u, :, :]), flat(m.beta[:]), ALU.add).then_inc(x_used, 1)

        def scale_gamma(engine, maker, here):
            engine.wait_ge(t_ready, here.b + 1)
            maker.tensor_tensor(flat(t_[:, here.u, :, :]), flat(t_[:, here.u, :, :]), flat(m.gamma[:]), ALU.mult).then_inc(t_scaled, 1)

        @block.gpsimd
        def _(pool):
            half_b = SLOTS // 2

            def gather_blocks(k, h):
                wait_from(pool, agg_summed, (k - 1) * SLOTS + (h + 1) * half_b)
                window = slice(h * half_b * SPAN, (h + 1) * half_b * SPAN)
                nc.gpsimd.tensor_copy(b_index[:, window], b_row[:, bass.ds((k * SLOTS + h * half_b) * SPAN, half_b * SPAN)]).then_inc(
                    b_index_staged, 1)
                pool.wait_ge(b_index_staged, k * 2 + h + 1)
                pool.sem_inc(past_wait, 1)
                for u in range(window.start, window.stop):
                    nc.gpsimd.indirect_dma_start(
                        out=b_raw[:, u, :], out_offset=None, in_=x_in,
                        in_offset=bass.IndirectOffsetOnAxis(ap=b_index[:, u:u + 1], axis=0)).then_inc(b_gathered[u], 16)

            def body(at):
                here = at(gamma_lag)
                if here:
                    scale_gamma(pool, nc.gpsimd, here)
                here = at(0)
                if here:
                    wait_from(pool, agg_summed, here.b - SLOTS + 1)
                    window = slice(here.u * SPAN, (here.u + 1) * SPAN)
                    nc.gpsimd.tensor_copy(b_index[:, window], b_row[:, bass.ds(here.b * SPAN, SPAN)]).then_inc(b_index_staged, 1)
                    pool.wait_ge(b_index_staged, here.b + 1)
                    pool.sem_inc(past_wait, 1)
                    for u in range(window.start, window.stop):
                        nc.gpsimd.indirect_dma_start(
                            out=b_raw[:, u, :], out_offset=None, in_=x_in,
                            in_offset=bass.IndirectOffsetOnAxis(ap=b_index[:, u:u + 1], axis=0)).then_inc(b_gathered[u], 16)
                here = at(beta_lag)
                if here:
                    add_beta(pool, nc.gpsimd, here)

            regular = pool.alloc_register(f"{kind}_pool_regular")
            pool.reg_load(regular, m.regular[0:1, 0:1])
            with pool.If(pool.snap(regular) > 0):
                if att:
                    over_blocks(pool, d, gamma_lag, body)
                else:
                    gather_blocks(0, 0)
                    gather_blocks(0, 1)
                    with pool.Fori(1, d.NB // SLOTS) as k:
                        gather_blocks(k, 0)
                        gather_blocks(k, 1)
            with pool.Else():
                pool.sem_inc(raw_free, RING)
                half = RING // 2

                def gather(i, h):
                    nc.gpsimd.tensor_copy(index[:, h * half:(h + 1) * half],
                                          row[:, bass.ds(i * RING + h * half, half)]).then_inc(index_staged, 1)
                    pool.wait_ge(index_staged, i * 2 + h + 1)
                    for u in range(h * half, (h + 1) * half):
                        pool.wait_ge(raw_free, i * RING + u + 1)
                        pool.sem_inc(past_wait, 1)
                        nc.gpsimd.indirect_dma_start(
                            out=raw[:, u, :], out_offset=None, in_=x_in,
                            in_offset=bass.IndirectOffsetOnAxis(ap=index[:, u:u + 1], axis=0)).then_inc(gathered[u], 16)

                def pass_on(i, h):
                    for u in range(h * half, (h + 1) * half):
                        pool.wait_ge(gathered[u], (i + 1) * 16)
                        pool.sem_inc(raw_ready, 1)

                gather(0, 0)
                gather(0, 1)
                pass_on(0, 0)
                with pool.Fori(1, d.NC // RING) as i:
                    gather(i, 0)
                    pass_on(i - 1, 1)
                    gather(i, 1)
                    pass_on(i, 0)
                pass_on(d.NC // RING - 1, 1)

        @block.sync
        def _(sp):
            def body(at):
                here = at(0)
                if here:
                    wait_from(sp, x_used, here.b - SLOTS + 1)
                    if att:
                        wait_from(sp, x_turned, here.b - SLOTS + 1)
                    rows = x_in.shape[0]
                    if isinstance(here.b, int) and (here.b + 1) * BLOCK > rows:
                        p = (rows - here.b * BLOCK) // PER
                        sp.dma_start(flat(x[0:p, here.u, :, :]), x_in[here.b * BLOCK:rows, :].rearrange(
                            "(p j) f -> p (j f)", j=PER)).then_inc(x_loaded[here.u], 16)
                    else:
                        sp.dma_start(flat(x[:, here.u, :, :]), x_in[bass.ds(here.b * BLOCK, BLOCK), :].rearrange(
                            "(p j) f -> p (j f)", j=PER)).then_inc(x_loaded[here.u], 16)
                here = at(out_lag)
                if here:
                    sp.wait_ge(normed, here.b + 1)
                    if isinstance(here.b, int) and (here.b + 1) * BLOCK > rows_out:
                        p = (rows_out - here.b * BLOCK) // PER
                        sp.dma_start(x_out[here.b * BLOCK:rows_out, :].rearrange("(p j) f -> p (j f)", j=PER),
                                     flat(out[0:p, here.u, :, :])).then_inc(stored[here.u], 16)
                    else:
                        sp.dma_start(x_out[bass.ds(here.b * BLOCK, BLOCK), :].rearrange("(p j) f -> p (j f)", j=PER),
                                     flat(out[:, here.u, :, :])).then_inc(stored[here.u], 16)

            over_blocks(sp, d, out_lag, body)
            for u in range(SLOTS):
                sp.wait_ge(stored[u], 16 * (d.NB // SLOTS))

        @block.scalar
        def _(act):
            chunk = act.alloc_register(f"{kind}_act_chunk")
            end = [act.alloc_register(f"{kind}_act_end{i}") for i in range(2 * SLOTS)]
            act.reg_mov(chunk, 0)

            def high(c, g):
                act.wait_ge(raw_ready, c + 1)
                act.wait_ge(pairs_done, c + g + 1)
                nc.scalar.activation(part(c, 0), raw[:, slot(c), :].rearrange("p s f -> p (s f)"), ACT.Copy,
                                     scale=weight[:, bass.ds(c, 1)]).then_inc(hi_done, 1)

            def high_block(here):
                for j in range(SPAN):
                    u = here.u * SPAN + j
                    act.wait_ge(b_gathered[u], (here.k + 1) * 16)
                    nc.scalar.activation(b_parts[:, u, 0, :], b_raw[:, u, :], ACT.Copy,
                                         scale=b_weight[:, bass.ds(here.b * SPAN + j, 1)]).then_inc(b_hi_done, 1)

            def body(at, by_block):
                here = at(-1)
                if here and by_block and b_cut:
                    high_block(here)
                here = at(0)
                if here and not by_block:
                    if here.u == 0:
                        act.reg_load(end, ends[0:1, bass.ds(here.b * 2, 2 * SLOTS)])
                    for h in range(2):
                        with act.While(lambda: act.snap(chunk) < act.snap(end[here.u * 2 + h])):
                            act.reg_add(chunk, chunk, 1)
                            high(act.snap(chunk), here.b * 2 + h)
                here = at(1)
                if here:
                    q = here.pair
                    if transposed:
                        act.wait_ge(x_turned, here.b + 1)
                        wait_from(act, y_ready, here.b - 1)
                        nc.scalar.copy(xt[:, q, :], xt_ps[:]).then_inc(xt_copied, 1)
                    act.wait_ge(agg_summed, here.b + 1)
                    wait_from(act, y_ready, here.b - 1)
                    if kind == REL:
                        nc.scalar.copy(ev_sum[:, q, :], ev_ps[q][0:3, :])
                    if att:
                        nc.scalar.activation(square[:, q, :], agg_ps[q][:], ACT.Square, scale=unscale)
                    nc.scalar.activation(agg[:, q, :], agg_ps[q][:], ACT.Copy, scale=unscale).then_inc(agg_copied, 1)
                here = at(variance_lag)
                if here and att:
                    act.wait_ge(var_ready, here.b + 1)
                    nc.scalar.activation(root_var[:, here.u, :], floored_var[:, here.u, :], ACT.Sqrt).then_inc(var_rooted, 1)
                here = at(length_lag)
                if here and att:
                    act.wait_ge(mean_ready, here.b + 1)
                    nc.scalar.activation(u_norm[:, here.u, :], mean_sq[:, here.u, :], ACT.Sqrt, scale=float(D)).then_inc(u_rooted, 1)
                    act.wait_ge(u_rooted, here.b + 1)
                    nc.scalar.activation(floor[:, here.u, :], u_norm[:, here.u, :], ACT.Square, bias=m.eps_length[:],
                                         scale=LN_EPS ** 0.5).then_inc(floor_ready, 1)
                here = at(norm_lag)
                if here:
                    act.wait_ge(scaled, here.b + 1)
                    wait_from(act, stored[here.u], here.k * 16)
                    for j in range(PER):
                        last = nc.scalar.activation(out[:, here.u, j, :], y[:, here.u, j, :], ACT.Identity,
                                                    bias=shift[:, here.u, j:j + 1], scale=scale[:, here.u, j:j + 1])
                    last.then_inc(normed, 1)
                here = at(2)
                if here and att:
                    act.wait_ge(y_ready, here.b + 1)
                    wait_from(act, summed, here.b - SLOTS + 1)
                    nc.scalar.activation(agg_norm[:, here.u, :], norm_ps[:, 0:PER], ACT.Sqrt).then_inc(agg_rooted, 1)
                    nc.scalar.copy(flat(own[:, here.u, :, :]), own_ps[here.pair][:]).then_inc(own_copied, 1)
                here = at(root_lag)
                if here:
                    act.wait_ge(moments_done, here.b + 1)
                    nc.scalar.activation(root[:, here.u, :], moments[:, here.u, :, 1], ACT.Sqrt, bias=m.eps_col[:]).then_inc(rooted, 1)
                here = at(factor_lag)
                if here and att:
                    act.wait_ge(k_ready, here.b + 1)
                    for j in range(PER):
                        last = nc.scalar.activation(t_[:, here.u, j, :], u_[:, here.u, j, :], ACT.Identity,
                                                    bias=shift_u[:, here.u, j:j + 1], scale=k_[:, here.u, j:j + 1])
                    last.then_inc(t_ready, 1)

            regular = act.alloc_register(f"{kind}_act_regular")
            act.reg_load(regular, m.regular[0:1, 0:1])
            with act.If(act.snap(regular) > 0):
                if b_cut:
                    high_block(At(0, 0))
                over_blocks(act, d, norm_lag, lambda at: body(at, True))
            with act.Else():
                high(0, 0)
                over_blocks(act, d, norm_lag, lambda at: body(at, False))

        @block.vector
        def _(dve):
            chunk = dve.alloc_register(f"{kind}_dve_chunk")
            end = [dve.alloc_register(f"{kind}_dve_end{i}") for i in range(2 * SLOTS)]
            dve.reg_mov(chunk, 0)
            if kind == REL:
                nc.vector.memset(parts[:, 3:RING * n_parts:n_parts, :], 0.0).then_inc(zeroed, 1)
                dve.wait_ge(zeroed, 1)

            def low(c, between=lambda half: None):
                rows = raw[:, slot(c), :].rearrange("p s f -> p (s f)")
                dve.wait_ge(hi_done, c + 1)
                if n_sums == 2:
                    nc.vector.scalar_tensor_tensor(part(c, 1), rows, weight[:, bass.ds(c, 1)], part(c, 0), ALU.mult,
                                                   ALU.subtract).then_inc(raw_free, 1)
                    between(0)
                    between(1)
                    return
                left = resid[:, slot(c), :].rearrange("p s f -> p (s f)")
                nc.vector.scalar_tensor_tensor(left, rows, weight[:, bass.ds(c, 1)], part(c, 0), ALU.mult,
                                               ALU.subtract).then_inc(raw_free, 1)
                if kind == REL:
                    nc.vector.tensor_copy(part(c, 3)[:, 0:3], m.s_ev_parts[:, bass.ds(c, 1), :].rearrange("p c k -> p (c k)"))
                between(0)
                dve.wait_ge(raw_free, c + 1 + RING)
                nc.vector.tensor_copy(part(c, 1), left).then_inc(mid_done, 1)
                between(1)
                dve.wait_ge(mid_done, c + 1)
                nc.vector.tensor_tensor(part(c, 2), left, part(c, 1), ALU.subtract).then_inc(low_done, 1)

            def one_hot(c, g, half):
                to = slice(half * (GROUP // 2), (half + 1) * (GROUP // 2))
                dve.wait_ge(pairs_done, c + g + 1)
                return nc.vector.tensor_scalar(hot[:, slot(c + g), to].rearrange("p s n -> p (s n)"), m.iota_half[:, to],
                                               m.group_base[:, bass.ds(g, 1)], key[:, bass.ds(c, 1)], ALU.add, ALU.is_equal)

            def one_hots(c, g):
                one_hot(c, g, 0)
                one_hot(c, g, 1).then_inc(hot_built, 1)

            def body(at, by_block):
                here, kth, yth = (at(lag) if att else None for lag in (variance_lag, factor_lag, stats_lag))
                if kth:
                    dve.wait_ge(var_rooted, kth.b + 1)
                    nc.vector.reciprocal(k_[:, kth.u, :], root_var[:, kth.u, :]).then_inc(k_inverted, 1)
                if here:
                    dve.wait_ge(floor_ready, here.b + 1)
                    nc.vector.tensor_tensor(floored_var[:, here.u, :], floor[:, here.u, :], moments_u[:, here.u, :, 1],
                                            ALU.add).then_inc(var_ready, 1)
                if kth:
                    dve.wait_ge(k_inverted, kth.b + 1)
                    nc.vector.scalar_tensor_tensor(shift_u[:, kth.u, :], moments_u[:, kth.u, :, 0], -1.0, k_[:, kth.u, :], ALU.mult,
                                                   ALU.mult).then_inc(k_ready, 1)
                if yth:
                    if not by_block:
                        scale_gamma(dve, nc.vector, yth)
                    dve.wait_ge(t_scaled, yth.b + 1)
                    dve.wait_ge(x_used, yth.b + 1)
                    wait_from(dve, normed, yth.b - SLOTS + 1)
                    nc.vector.tensor_tensor(flat(y[:, yth.u, :, :]), flat(t_[:, yth.u, :, :]), xb_slot(yth), ALU.add).then_inc(y_made, 1)
                here = at(node_lag)
                if here:
                    dve.wait_ge(y_ready, here.b + 1)
                    dve.wait_ge(x_loaded[here.u], (here.k + 1) * 16)
                if here and att:
                    dve.wait_ge(agg_rooted, here.b + 1)
                    dve.wait_ge(own_copied, here.b + 1)
                    wait_from(dve, t_ready, here.b - SLOTS + 1)
                    nc.vector.tensor_scalar(inv[:, here.u, :], agg_norm[:, here.u, :], NORM_EPS, None, ALU.add).then_inc(step, 1)
                    if not by_block:
                        add_beta(dve, nc.vector, here)
                    dve.wait_ge(step, here.b * 5 + 1)
                    nc.vector.reciprocal(inv[:, here.u, :], inv[:, here.u, :]).then_inc(step, 1)
                    dve.wait_ge(step, here.b * 5 + 2)
                    for j in range(PER):
                        last = nc.vector.scalar_tensor_tensor(u_[:, here.u, j, :], y_ps[here.pair][:, j * D:(j + 1) * D],
                                                              inv[:, here.u, j:j + 1], own[:, here.u, j, :],
                                                              ALU.mult, ALU.add)
                    last.then_inc(summed, 1)
                    dve.wait_ge(summed, here.b + 1)
                    for j in range(PER):
                        last = nc.vector.bn_stats(stats_u[:, here.u, j, :], u_[:, here.u, j, :])
                    last.then_inc(step, 1)
                elif here:
                    wait_from(dve, normed, here.b - SLOTS + 1)
                    if kind == SAGE:
                        nc.vector.tensor_tensor(flat(y[:, here.u, :, :]), y_ps[here.pair][:], flat(x[:, here.u, :, :]),
                                                ALU.add).then_inc(summed, 1)
                    else:
                        nc.vector.scalar_tensor_tensor(flat(y[:, here.u, :, :]), y_ps[here.pair][:], 0.0,
                                                       flat(x[:, here.u, :, :]), ALU.max, ALU.add).then_inc(summed, 1)
                first = at(0)
                if first and by_block:
                    wait_from(dve, agg_summed, first.b - 1)
                    for j in range(SPAN):
                        q = bass.ds(first.b * SPAN + j, 1)
                        if kind == REL:
                            nc.vector.tensor_scalar(b_ones[:, first.pair * SPAN + j, :], m.iota_half[:, 0:BLOCK], b_key[:, q], None,
                                                    ALU.is_equal)
                        if b_cut:
                            u = first.u * SPAN + j
                            nc.vector.tensor_scalar(b_hot[:, first.pair * SPAN + j, :], m.iota_half[:, 0:BLOCK], b_key[:, q], None,
                                                    ALU.is_equal).then_inc(b_hot_built, 1)
                            dve.wait_ge(b_hi_done, first.b * SPAN + j + 1)
                            nc.vector.scalar_tensor_tensor(b_parts[:, u, 1, :], b_raw[:, u, :], b_weight[:, q], b_parts[:, u, 0, :],
                                                           ALU.mult, ALU.subtract).then_inc(b_low_done, 1)
                        else:
                            nc.vector.tensor_scalar(b_hot[:, first.pair * SPAN + j, :], m.iota_half[:, 0:BLOCK], b_key[:, q], b_weight[:, q],
                                                    ALU.is_equal, ALU.mult).then_inc(b_hot_built, 1)
                elif first:
                    if first.u == 0:
                        dve.reg_load(end, ends[0:1, bass.ds(first.b * 2, 2 * SLOTS)])
                    for h in range(2):
                        g = first.b * 2 + h
                        one_hots(dve.snap(chunk), g)
                        with dve.While(lambda: dve.snap(chunk) < dve.snap(end[first.u * 2 + h])):
                            dve.reg_add(chunk, chunk, 1)
                            c = dve.snap(chunk)

                            def between(half):
                                made = one_hot(c, g, half)
                                if half:
                                    made.then_inc(hot_built, 1)

                            low(c, between)
                here = at(node_lag)
                if here and att:
                    dve.wait_ge(step, here.b * 5 + 3)
                    dve.sem_inc(past_dve_wait, 1)
                    for j in range(PER):
                        last = nc.vector.bn_aggr(moments_u[:, here.u, j, :], stats_u[:, here.u, j, :])
                    last.then_inc(step, 1)
                last_one = at(scale_lag)
                if last_one:
                    dve.wait_ge(rooted, last_one.b + 1)
                    nc.vector.reciprocal(scale[:, last_one.u, :], root[:, last_one.u, :]).then_inc(inverted, 1)
                if here and att:
                    dve.wait_ge(step, here.b * 5 + 4)
                    mean, var = moments_u[:, here.u, :, 0], moments_u[:, here.u, :, 1]
                    nc.vector.tensor_tensor(mean_sq[:, here.u, :], mean, mean, ALU.mult).then_inc(step, 1)
                if last_one:
                    dve.wait_ge(inverted, last_one.b + 1)
                    nc.vector.scalar_tensor_tensor(shift[:, last_one.u, :], moments[:, last_one.u, :, 0], -1.0,
                                                   scale[:, last_one.u, :], ALU.mult, ALU.mult).then_inc(scaled, 1)
                if here and att:
                    dve.wait_ge(step, here.b * 5 + 5)
                    nc.vector.tensor_tensor(mean_sq[:, here.u, :], mean_sq[:, here.u, :], var, ALU.add).then_inc(mean_ready, 1)
                here = at(stats_lag)
                if here:
                    if att:
                        dve.wait_ge(y_made, here.b + 1)
                    else:
                        dve.wait_ge(summed, here.b + 1)
                    for j in range(PER):
                        last = nc.vector.bn_stats(stats[:, here.u, j, :], y[:, here.u, j, :])
                    last.then_inc(stats_done, 1)
                    dve.wait_ge(stats_done, here.b + 1)
                    dve.sem_inc(past_dve_wait, 1)
                    for j in range(PER):
                        last = nc.vector.bn_aggr(moments[:, here.u, j, :], stats[:, here.u, j, :])
                    last.then_inc(moments_done, 1)

            regular = dve.alloc_register(f"{kind}_dve_regular")
            dve.reg_load(regular, m.regular[0:1, 0:1])
            with dve.If(dve.snap(regular) > 0):
                over_blocks(dve, d, scale_lag, lambda at: body(at, True))
            with dve.Else():
                low(0)
                over_blocks(dve, d, scale_lag, lambda at: body(at, False))

        @block.tensor
        def _(pe):
            chunk = pe.alloc_register(f"{kind}_pe_chunk")
            end = [pe.alloc_register(f"{kind}_pe_end{i}") for i in range(2 * SLOTS)]
            pe.reg_mov(chunk, 0)
            pe.sem_inc(pairs_done, RING)

            def pair(c, g, h, here, stop):
                window = slice(h * GROUP, (h + 1) * GROUP)
                one_hot = hot[:, slot(c + g), :].rearrange("p s n -> p (s n)")
                pe.wait_ge(hot_built, c + g + 1)
                if n_sums == 3:
                    pe.wait_ge(low_done, c + 1)
                else:
                    pe.wait_ge(raw_free, c + 1 + RING)
                if kind == REL:
                    nc.tensor.matmul(ev_ps[here.pair][:, window], part(c, 3), one_hot, start=False, stop=stop)
                for k in range(n_sums):
                    last = nc.tensor.matmul(agg_ps[here.pair][:, window], part(c, k), one_hot, start=False,
                                            stop=stop and k == n_sums - 1)
                last.then_inc(pairs_done, 1)

            def body(at, by_block):
                here = at(0)
                if here and by_block:
                    wait_from(pe, agg_copied, here.b - 1)
                    for j in range(SPAN):
                        u = here.u * SPAN + j
                        one_hot = b_hot[:, here.pair * SPAN + j, :]
                        pe.wait_ge(b_hot_built, here.b * SPAN + j + 1)
                        pe.wait_ge(b_gathered[u], (here.k + 1) * 16)
                        if kind == REL:
                            nc.tensor.matmul(ev_ps[here.pair][0:3, :], m.bs_ev_parts[:, bass.ds(here.b * SPAN + j, 1), :].rearrange("p q k -> p (q k)"),
                                             b_ones[:, here.pair * SPAN + j, :], start=j == 0, stop=j == SPAN - 1)
                        if b_cut:
                            pe.wait_ge(b_low_done, here.b * SPAN + j + 1)
                        for k, rows in enumerate([b_parts[:, u, 0, :], b_parts[:, u, 1, :]] if b_cut else [b_raw[:, u, :]]):
                            last = nc.tensor.matmul(agg_ps[here.pair][:], rows, one_hot, start=j == 0 and k == 0,
                                                    stop=j == SPAN - 1 and (k == 1 or not b_cut))
                    last.then_inc(agg_summed, 1)
                elif here:
                    if here.u == 0:
                        pe.reg_load(end, ends[0:1, bass.ds(here.b * 2, 2 * SLOTS)])
                    wait_from(pe, agg_copied, here.b - 1)
                    for h in range(2):
                        g = here.b * 2 + h
                        for sums in (agg_ps, ev_ps)[:1 + (kind == REL)]:
                            nc.tensor.matmul(sums[here.pair][:, h * GROUP:(h + 1) * GROUP], m.zeros[:, 0:P], m.zeros[:, 0:GROUP],
                                             start=True, stop=False)
                        with pe.While(lambda: pe.snap(chunk) < pe.snap(end[here.u * 2 + h])):
                            pair(pe.snap(chunk), g, h, here, False)
                            pe.reg_add(chunk, chunk, 1)
                        pair(pe.snap(chunk), g, h, here, True)
                    pe.wait_ge(pairs_done, pe.snap(chunk) + (here.b * 2 + 2 + RING))
                    pe.sem_inc(agg_summed, 1)
                if here:
                    if transposed:
                        pe.wait_ge(x_loaded[here.u], (here.k + 1) * 16)
                        wait_from(pe, xt_copied, here.b)
                        for j in range(PER):
                            last = nc.tensor.transpose(xt_ps[:, j * P:(j + 1) * P], x[:, here.u, j, :], m.ident[:])
                        last.then_inc(x_turned, 1)
                here = at(1)
                if here:
                    q = here.pair
                    sums = y_ps[q]
                    pe.wait_ge(agg_copied, here.b + 1)
                    wait_from(pe, summed, here.b - 1)
                    aggT = [agg[:, q, j:BLOCK:PER] for j in range(PER)]
                    xT = [xt[:, q, j * P:(j + 1) * P] for j in range(PER)]
                    if kind == GCN or kind == SAGE:
                        nc.tensor.matmul(sums[:], m.ones[0:3, :], (m.b0 if kind == GCN else m.b3)[:], start=True, stop=False)
                    if att:
                        nc.tensor.matmul(own_ps[q][:], m.ones[0:3, :], m.b2[:], start=True, stop=False)
                    for j in range(PER):
                        window = slice(j * D, (j + 1) * D)
                        if kind == GCN:
                            last = nc.tensor.matmul(sums[:, window], aggT[j], m.w0[:], start=False, stop=j == PER - 1)
                        elif kind == REL:
                            nc.tensor.matmul(sums[:, window], ev_sum[:, q, j:BLOCK:PER], m.b1[:], start=True, stop=False)
                            last = nc.tensor.matmul(sums[:, window], aggT[j], m.w1[:], start=False, stop=True)
                        elif kind == SAGE:
                            nc.tensor.matmul(sums[:, window], xT[j], m.w3s[:], start=False, stop=False)
                            last = nc.tensor.matmul(sums[:, window], aggT[j], m.w3n[:], start=False, stop=j == PER - 1)
                        else:
                            nc.tensor.matmul(own_ps[q][:, window], xT[j], m.w2s[:], start=False, stop=j == PER - 1)
                            last = nc.tensor.matmul(sums[:, window], aggT[j], m.w2n[:], start=True, stop=True)
                    if att:
                        wait_from(pe, agg_rooted, here.b)
                        for j in range(PER):
                            last = nc.tensor.matmul(norm_ps[:, j:j + 1], square[:, q, j:BLOCK:PER], m.ones_col[:], start=True, stop=True)
                    last.then_inc(y_ready, 1)

            regular = pe.alloc_register(f"{kind}_pe_regular")
            pe.reg_load(regular, m.regular[0:1, 0:1])
            with pe.If(pe.snap(regular) > 0):
                over_blocks(pe, d, 1, lambda at: body(at, True))
            with pe.Else():
                over_blocks(pe, d, 1, lambda at: body(at, False))


NAMES = ["x", "src", "dst", "edge_weight", "L0_gnn_weight", "L0_gnn_bias", "L1_gnn_W", "L1_gnn_b", "L2_gnn_W_self",
         "L2_gnn_b_self", "L2_gnn_W_nb", "L2_gnn_b_nb", "L2_gnn_gamma", "L2_gnn_beta", "L3_gnn_W_self",
         "L3_gnn_b_self", "L3_gnn_W_neigh", "L3_gnn_b_neigh"]


def program(nc, *args):
    a = dict(zip(NAMES, args))
    result = args[len(NAMES)]
    d = Dims(a["x"].shape[0], a["src"].shape[0])
    weights_dram = nc.dram_tensor("weights_scratch", [3, d.E], F32).ap()
    norm_dram = nc.dram_tensor("norm_scratch", [d.NP, 1], F32).ap()
    sorted_dram = nc.dram_tensor("sorted_scratch", [d.EP, 4], F32).ap()
    starts_dram = nc.dram_tensor("starts_scratch", [1, 2, d.NB], F32).ap()
    flat_dst = nc.dram_tensor("flat_dst_scratch", [(d.EP + SPAN * P) * 5], F32).ap()
    flat_src = nc.dram_tensor("flat_src_scratch", [(d.EP + SPAN * P) * 3], F32).ap()
    x1 = nc.dram_tensor("x1_scratch", [d.NP, D], F32).ap()
    x2 = nc.dram_tensor("x2_scratch", [d.NP, D], F32).ap()
    with ExitStack() as ctx:
        m = Memory(nc, ctx, d)
        with ExitStack() as prep:
            s = Sorts(nc, prep, d)
            phase_constants(nc, d, m)
            phase_weights(nc, d, m, a)
            phase_edges(nc, d, m, a)
            phase_segments(nc, d, m, a, weights_dram)
            phase_digits(nc, d, m, s)
            phase_histogram(nc, d, m, norm_dram, s)
            phase_rank(nc, d, m, s, norm_dram)
            phase_scatter(nc, d, m, s, sorted_dram)
        phase_blocks(nc, d, m, starts_dram, flat_dst, flat_src)
        by_dst = (m.row_src, m.key_dst)
        phase_layer(nc, d, m, GCN, a["x"], x1, d.NP, *by_dst, m.w_gcn, m.end_dst, m.b_row, m.b_key, m.b_gcn)
        phase_layer(nc, d, m, REL, x1, x2, d.NP, m.s_row, m.s_key, m.s_ev, m.end_src, m.bs_row, m.bs_key, m.bs_ev)
        phase_layer(nc, d, m, ATT, x2, x1, d.NP, *by_dst, m.w_alpha, m.end_dst, m.b_row, m.b_key, m.b_alpha)
        phase_layer(nc, d, m, SAGE, x1, result, d.N, *by_dst, m.w_mean, m.end_dst, m.b_row, m.b_key, m.b_mean)


def kernel(**inputs):
    import numpy as np
    import concourse.bacc as bacc
    from concourse.bass_utils import run_bass_kernel_spmd

    nc = bacc.Bacc("TRN2", target_bir_lowering=False, num_devices=1)
    arrays, args = {}, []
    for name in NAMES:
        value = np.ascontiguousarray(inputs[name])
        arrays[f"in_{name}"] = value
        args.append(nc.dram_tensor(f"in_{name}", value.shape, mybir.dt.from_np(value.dtype), kind="ExternalInput").ap())
    args.append(nc.dram_tensor("out_0", arrays["in_x"].shape, F32, kind="ExternalOutput").ap())
    program(nc, *args)
    results = run_bass_kernel_spmd(nc, [arrays], core_ids=[0])
    return results.results[0]["out_0"]
```
